# Optimizing a Trainium2 kernel written in Bass

```python
import numpy as np
import jax
import jax.numpy as jnp

def _softmax(x, axis=-1):
    return jax.nn.softmax(x, axis=axis)

def _gelu(x):
    return jax.nn.gelu(x, approximate=True)

def _silu(x):
    return jax.nn.silu(x)

def _sigmoid(x):
    return jax.nn.sigmoid(x)

def _layernorm(x, axis=-1, eps=1e-05):
    m = jnp.mean(x, axis=axis, keepdims=True)
    v = jnp.var(x, axis=axis, keepdims=True)
    return (x - m) / jnp.sqrt(v + eps)

def _scatter_add(tgt, idx, src, axis=0):
    return tgt.at[idx].add(src)

def _segment_sum(src, seg, n):
    return jax.ops.segment_sum(src, seg, n)
kernel_name = 'mk_gnn_ffn_d1_gnn_r8_9b7e7c'

def setup_inputs(seed: int=0):
    np.random.seed(seed)
    _w = jnp.asarray

    def _rec_inputs():
        import jax
        import jax.numpy as jnp
        _gk = jax.random.key(seed)
        x = -0.0001126 + 1 * jax.random.normal(jax.random.fold_in(_gk, 1), (1250, 768), jnp.float32)
        _s = jax.random.randint(jax.random.fold_in(_gk, 2), (10000,), 0, 1250, jnp.int32)
        _d = jax.random.randint(jax.random.fold_in(_gk, 3), (10000,), 0, 1250, jnp.int32)
        _loop = jnp.arange(1250, dtype=jnp.int32)
        src = jnp.concatenate([_s, _d, _loop])
        dst = jnp.concatenate([_d, _s, _loop])
        _o = jnp.argsort(dst, stable=True)
        src = src[_o]
        dst = dst[_o]
        return (x, src, dst)
    x, src, dst = _rec_inputs()

    def _L0_gnn_setup():
        import jax, jax.numpy as jnp
        import numpy as np
        N_NODES = 1250
        NEG_SLOPE = 0.2
        EPS = 1e-16

        def gat_layer(x, W, att_src, att_dst, bias, src, dst, heads, out_ch, concat):
            n = x.shape[0]
            h = (x @ W.T).reshape(n, heads, out_ch)
            a_src = jnp.einsum('nhc,hc->nh', h, att_src)
            a_dst = jnp.einsum('nhc,hc->nh', h, att_dst)
            e = a_src[src] + a_dst[dst]
            e = jax.nn.leaky_relu(e, NEG_SLOPE)
            m = jax.ops.segment_max(e, dst, num_segments=n)
            ex = jnp.exp(e - m[dst])
            denom = jax.ops.segment_sum(ex, dst, num_segments=n)
            alpha = ex / (denom[dst] + EPS)
            msg = alpha[:, :, None] * h[src]
            out = jax.ops.segment_sum(msg, dst, num_segments=n)
            if concat:
                out = out.reshape(n, heads * out_ch)
            else:
                out = out.mean(axis=1)
            return out + bias
        key = jax.random.key(seed)
        ks = jax.random.split(key, 12)
        x = jax.random.normal(ks[0], (N_NODES, 768), dtype=jnp.float32)
        edge_index = jax.random.randint(ks[1], (2, 20000), 0, N_NODES, dtype=jnp.int64)
        s1 = 1.0 / np.sqrt(768.0)
        W1 = jax.random.normal(ks[2], (8 * 128, 768), dtype=jnp.float32) * s1
        att_src1 = jax.random.normal(ks[3], (8, 128), dtype=jnp.float32) * (1.0 / np.sqrt(128.0))
        att_dst1 = jax.random.normal(ks[4], (8, 128), dtype=jnp.float32) * (1.0 / np.sqrt(128.0))
        b1 = jnp.zeros((8 * 128,), dtype=jnp.float32)
        s2 = 1.0 / np.sqrt(1024.0)
        W2 = jax.random.normal(ks[5], (1 * 768, 1024), dtype=jnp.float32) * s2
        att_src2 = jax.random.normal(ks[6], (1, 768), dtype=jnp.float32) * (1.0 / np.sqrt(768.0))
        att_dst2 = jax.random.normal(ks[7], (1, 768), dtype=jnp.float32) * (1.0 / np.sqrt(768.0))
        b2 = jnp.zeros((768,), dtype=jnp.float32)
        return {'x': x, 'edge_index': edge_index, 'W1': W1, 'att_src1': att_src1, 'att_dst1': att_dst1, 'b1': b1, 'W2': W2, 'att_src2': att_src2, 'att_dst2': att_dst2, 'b2': b2}
    _L0_gnn_all = _L0_gnn_setup()
    _L0_gnn_in = {k: v for k, v in _L0_gnn_all.items() if k in ('W1', 'att_src1', 'att_dst1', 'b1', 'W2', 'att_src2', 'att_dst2', 'b2')}
    del _L0_gnn_all

    def _L0_ffn_setup():
        import jax, jax.numpy as jnp
        import numpy as np
        ATOM = {'vm': 0, 'im': 1, 'cm': 2, 'sc': 3, 'cc': 4}
        TASK_PAIRS = [('vm', 'sc'), ('vm', 'cc'), ('im', 'sc'), ('im', 'cc'), ('cm', 'sc'), ('cm', 'cc')]
        SRC_IDX = np.array([[ATOM[l], ATOM[r]] for l, r in TASK_PAIRS], dtype=np.int32)
        DST_IDX = np.array([[ATOM[r], ATOM[l]] for l, r in TASK_PAIRS], dtype=np.int32)
        NCLS = 6
        NATOMS = 5

        def _l2norm(x, eps=1e-12):
            return x / jnp.clip(jnp.linalg.norm(x, axis=-1, keepdims=True), eps)
        key = jax.random.key(seed)
        ks = jax.random.split(key, 12)
        B, NPATCH, D, H = (64, 197, 768, 384)
        std = 0.02
        x = jax.random.normal(ks[0], (B, NCLS + NPATCH, D), dtype=jnp.float32)
        fc1_w = jax.random.normal(ks[1], (H, D), dtype=jnp.float32) * std
        fc1_b = jnp.zeros((H,), jnp.float32)
        fc2_w = jax.random.normal(ks[2], (D, H), dtype=jnp.float32) * std
        fc2_b = jnp.zeros((D,), jnp.float32)
        gate_pair = jax.random.normal(ks[3], (NCLS, 2, D), dtype=jnp.float32) * std
        atom_in_w = jax.random.normal(ks[4], (NATOMS, H, D), dtype=jnp.float32) * std
        atom_in_b = jax.random.normal(ks[5], (NATOMS, H), dtype=jnp.float32) * std
        atom_out_w = jax.random.normal(ks[6], (NATOMS, D, H), dtype=jnp.float32) * std
        atom_out_b = jax.random.normal(ks[7], (NATOMS, D), dtype=jnp.float32) * std
        balance_bias = jnp.zeros((NCLS, 2), jnp.float32)
        return {'x': x, 'fc1_w': fc1_w, 'fc1_b': fc1_b, 'fc2_w': fc2_w, 'fc2_b': fc2_b, 'gate_pair': gate_pair, 'atom_in_w': atom_in_w, 'atom_in_b': atom_in_b, 'atom_out_w': atom_out_w, 'atom_out_b': atom_out_b, 'balance_bias': balance_bias}
    _L0_ffn_all = _L0_ffn_setup()
    _L0_ffn_in = {k: v for k, v in _L0_ffn_all.items() if k in ('fc1_w', 'fc1_b', 'fc2_w', 'fc2_b', 'gate_pair', 'atom_in_w', 'atom_in_b', 'atom_out_w', 'atom_out_b', 'balance_bias')}
    del _L0_ffn_all
    return {'x': x, 'src': src, 'dst': dst, 'L0_gnn_W1': _L0_gnn_in['W1'], 'L0_gnn_att_src1': _L0_gnn_in['att_src1'], 'L0_gnn_att_dst1': _L0_gnn_in['att_dst1'], 'L0_gnn_b1': _L0_gnn_in['b1'], 'L0_gnn_W2': _L0_gnn_in['W2'], 'L0_gnn_att_src2': _L0_gnn_in['att_src2'], 'L0_gnn_att_dst2': _L0_gnn_in['att_dst2'], 'L0_gnn_b2': _L0_gnn_in['b2'], 'L0_ffn_fc1_w': _L0_ffn_in['fc1_w'], 'L0_ffn_fc1_b': _L0_ffn_in['fc1_b'], 'L0_ffn_fc2_w': _L0_ffn_in['fc2_w'], 'L0_ffn_fc2_b': _L0_ffn_in['fc2_b'], 'L0_ffn_gate_pair': _L0_ffn_in['gate_pair'], 'L0_ffn_atom_in_w': _L0_ffn_in['atom_in_w'], 'L0_ffn_atom_in_b': _L0_ffn_in['atom_in_b'], 'L0_ffn_atom_out_w': _L0_ffn_in['atom_out_w'], 'L0_ffn_atom_out_b': _L0_ffn_in['atom_out_b'], 'L0_ffn_balance_bias': _L0_ffn_in['balance_bias']}

def reference(x, src, dst, L0_gnn_W1, L0_gnn_att_src1, L0_gnn_att_dst1, L0_gnn_b1, L0_gnn_W2, L0_gnn_att_src2, L0_gnn_att_dst2, L0_gnn_b2, L0_ffn_fc1_w, L0_ffn_fc1_b, L0_ffn_fc2_w, L0_ffn_fc2_b, L0_ffn_gate_pair, L0_ffn_atom_in_w, L0_ffn_atom_in_b, L0_ffn_atom_out_w, L0_ffn_atom_out_b, L0_ffn_balance_bias):
    import jax
    import jax.numpy as jnp

    def _L0_gnn_ref(x, edge_index, W1, att_src1, att_dst1, b1, W2, att_src2, att_dst2, b2):
        import jax, jax.numpy as jnp
        import numpy as np
        N_NODES = 1250
        NEG_SLOPE = 0.2
        EPS = 1e-16

        def gat_layer(x, W, att_src, att_dst, bias, src, dst, heads, out_ch, concat):
            n = x.shape[0]
            h = (x @ W.T).reshape(n, heads, out_ch)
            a_src = jnp.einsum('nhc,hc->nh', h, att_src)
            a_dst = jnp.einsum('nhc,hc->nh', h, att_dst)
            e = a_src[src] + a_dst[dst]
            e = jax.nn.leaky_relu(e, NEG_SLOPE)
            m = jax.ops.segment_max(e, dst, num_segments=n)
            ex = jnp.exp(e - m[dst])
            denom = jax.ops.segment_sum(ex, dst, num_segments=n)
            alpha = ex / (denom[dst] + EPS)
            msg = alpha[:, :, None] * h[src]
            out = jax.ops.segment_sum(msg, dst, num_segments=n)
            if concat:
                out = out.reshape(n, heads * out_ch)
            else:
                out = out.mean(axis=1)
            return out + bias
        src, dst = (edge_index[0], edge_index[1])
        h = gat_layer(x, W1, att_src1, att_dst1, b1, src, dst, heads=8, out_ch=128, concat=True)
        h = jax.nn.relu(h)
        out = gat_layer(h, W2, att_src2, att_dst2, b2, src, dst, heads=1, out_ch=768, concat=True)
        return out

    def _L0_ffn_ref(x, fc1_w, fc1_b, fc2_w, fc2_b, gate_pair, atom_in_w, atom_in_b, atom_out_w, atom_out_b, balance_bias):
        import jax, jax.numpy as jnp
        import numpy as np
        ATOM = {'vm': 0, 'im': 1, 'cm': 2, 'sc': 3, 'cc': 4}
        TASK_PAIRS = [('vm', 'sc'), ('vm', 'cc'), ('im', 'sc'), ('im', 'cc'), ('cm', 'sc'), ('cm', 'cc')]
        SRC_IDX = np.array([[ATOM[l], ATOM[r]] for l, r in TASK_PAIRS], dtype=np.int32)
        DST_IDX = np.array([[ATOM[r], ATOM[l]] for l, r in TASK_PAIRS], dtype=np.int32)
        NCLS = 6
        NATOMS = 5

        def _l2norm(x, eps=1e-12):
            return x / jnp.clip(jnp.linalg.norm(x, axis=-1, keepdims=True), eps)
        src = jnp.asarray(SRC_IDX)
        dst = jnp.asarray(DST_IDX)
        D = x.shape[-1]
        H = atom_in_w.shape[1]
        cls_tokens = x[:, :NCLS]
        patch_tokens = x[:, NCLS:]
        patch_out = jax.nn.gelu(patch_tokens @ fc1_w.T + fc1_b, approximate=False) @ fc2_w.T + fc2_b
        gate_in = _l2norm(cls_tokens.astype(jnp.float32))
        gate_w = _l2norm(gate_pair.astype(jnp.float32))
        gate_logits = jnp.einsum('bnd,nrd->bnr', gate_in, gate_w) + balance_bias[None]
        route_probs = jax.nn.softmax(gate_logits, axis=-1)
        chosen_route = jnp.argmax(route_probs, axis=-1)
        hid_all = jax.nn.gelu(jnp.einsum('bnd,ahd->bnah', cls_tokens, atom_in_w) + atom_in_b[None, None], approximate=False)
        sh_pair = hid_all[:, jnp.arange(NCLS)[:, None], src, :]
        route_out_w = atom_out_w[dst.reshape(-1)].reshape(NCLS, 2, D, H)
        route_candidates = jnp.einsum('bnrh,nrdh->bnrd', sh_pair, route_out_w) + atom_out_b[dst][None]
        chosen_w = jnp.take_along_axis(route_probs, chosen_route[..., None], axis=-1)
        chosen_cand = jnp.take_along_axis(route_candidates, chosen_route[:, :, None, None], axis=2)[:, :, 0]
        cls_out = chosen_cand * chosen_w.astype(chosen_cand.dtype)
        return jnp.concatenate([cls_out, patch_out], axis=1)
    edge_index = jnp.stack([src, dst])
    x = x + _L0_gnn_ref(_layernorm(x, axis=-1), edge_index, L0_gnn_W1, L0_gnn_att_src1, L0_gnn_att_dst1, L0_gnn_b1, L0_gnn_W2, L0_gnn_att_src2, L0_gnn_att_dst2, L0_gnn_b2)
    x = x + _L0_ffn_ref(_layernorm(x, axis=-1)[None], L0_ffn_fc1_w, L0_ffn_fc1_b, L0_ffn_fc2_w, L0_ffn_fc2_b, L0_ffn_gate_pair, L0_ffn_atom_in_w, L0_ffn_atom_in_b, L0_ffn_atom_out_w, L0_ffn_atom_out_b, L0_ffn_balance_bias)[0]
    return x

_drawn_inputs = setup_inputs


def setup_inputs(seed=0):
    import zlib

    import numpy as np

    out = dict(_drawn_inputs(seed))
    spreads = {'L0_gnn_b1': (0.0, 0.1),
     'L0_gnn_b2': (0.0, 0.1),
     'L0_ffn_fc1_b': (0.0, 0.334),
     'L0_ffn_fc2_b': (0.0, 0.1),
     'L0_ffn_balance_bias': (0.0, 0.8)}
    factors = {'L0_gnn_att_dst1': 5.077,
     'L0_gnn_att_src2': 7.814,
     'L0_gnn_att_dst2': 64.0,
     'L0_ffn_gate_pair': 64.0,
     'L0_ffn_atom_in_w': 8.0,
     'L0_ffn_atom_in_b': 30.805,
     'L0_ffn_atom_out_w': 8.0,
     'L0_ffn_atom_out_b': 64.0}
    for name, (base, spread) in spreads.items():
        noise = np.random.default_rng([zlib.crc32(name.encode()), seed]).standard_normal(out[name].shape)
        drawn = base * np.exp(spread * noise) if base else spread * noise
        out[name] = jnp.asarray(drawn.astype(out[name].dtype))
    for name, factor in factors.items():
        out[name] = (out[name] * factor).astype(out[name].dtype)
    return out
```

```python
from contextlib import ExitStack

import concourse.bass as bass
from concourse import mybir

F32 = mybir.dt.float32
F16 = mybir.dt.float16
I32 = mybir.dt.int32
ACT = mybir.ActivationFunctionType
ALU = mybir.AluOpType
RMAX = bass.bass_isa.ReduceOp.max

N, D = 1250, 768
H, C = 8, 128
HC = H * C
FH = 384
NE = 21250
NP = 125
NT = N // NP
NG = NT // 2
GW = 2 * NP
CE = 125
NCH = NE // CE
NS = NCH // 2
KD, KC, KF = D // 128, HC // 128, FH // 128
HALF = D // 2
NCLS, NATOM = 6, 5
SLOPE = 0.2
EPS = 1e-16
LN_EPS = 1e-5
NORM_EPS = 1e-12
FLOOR = -1e29
BANKS3 = [(0, 500), (500, 500), (1000, 250)]
PTSLOT = [0, 1, 0, 1, 2]
TBANK = [0, 1, 6, 7, 0]
TFREE = [0, -3, -2, -1, 1]
PTFREE = [2, 2, 1, 1, 4]
ATOM_SRC = [(0, 3), (0, 4), (1, 3), (1, 4), (2, 3), (2, 4)]


def ds(start, size):
    return bass.ds(start, size)


def alone(engine):
    engine.nop(nofuse=True)


def freed(engine, semaphore, value):
    if not (isinstance(value, int) and value <= 0):
        engine.wait_ge(semaphore, value)


def rounds(engine, stop, body):
    body(0)
    with engine.Fori(1, stop) as i:
        body(i)


def at(hh, k, lag):
    kk = k - lag
    return (kk // NG) % 2, kk % NG, 2 * NG * hh + kk, 2 * hh + kk // NG


def gnn_ffn_kernel(nc, x, src_cols, dst_cols, dst_rows, W1, W1T, as1T, ad1T, b1c, W2, W2T, as2T, ad2T,
                   b2, fc1T, fc1b, fc2T, fc2b, gate_pair, atom_inT, atom_inb, atom_outT, atom_outb,
                   balance, out):
    h1_d = nc.dram_tensor("h1_scratch", (N, HC), F32).ap()
    row_d = nc.dram_tensor("src_logit_rows", (H, 2, N), F32).ap()
    row2_d = nc.dram_tensor("src_logit_rows2", (1, 2, N), F32).ap()
    lc_d = nc.dram_tensor("log_count_scratch", (N, N), F32).ap()
    h1T_d = nc.dram_tensor("hidden_T_scratch", (H, C, N), F32).ap()

    ctx = ExitStack()
    with ctx:
        def sb(name, shape, dt=F32, where=ctx):
            return where.enter_context(nc.sbuf_tensor(name, shape, dt))

        def sem(name):
            return ctx.enter_context(nc.semaphore(name))

        ident = sb("ident", [128, 128])
        zeros16 = sb("zeros16", [NP, 128], F16)
        att1 = sb("att1", [C, 2, H])
        att2 = sb("att2", [128, 2, KD])
        watt1 = sb("watt1", [128, KD, 2 * H])
        watt2 = sb("watt2", [128, KC, 2])
        nad1 = sb("nad1", [NP, H, NT])
        nad2 = sb("nad2", [NP, NT])
        b1_sb = sb("b1_sb", [C, H])
        b2_sb = sb("b2_sb", [NP, D])
        fc1_sb = sb("fc1_sb", [128, KD, FH])
        fc1b_sb = sb("fc1b_sb", [128, KF])
        fc2_sb = sb("fc2_sb", [128, KF, D])
        fc2b_sb = sb("fc2b_sb", [NP, D])
        tiny = sb("tiny", [NP, 1])
        powers = sb("powers", [NP, 4])
        spans = sb("spans", [1, 3 * NT], I32)

        w2_ctx = ExitStack()
        w2_sb = sb("w2_sb", [128, KC, D + 1], F32, w2_ctx)
        w2_ctx.close()
        w2_end = ExitStack()
        atom_w = [sb(f"atom_w{i}", [128, KD * FH], F32, w2_end) for i in range(2)]
        pad_ = sb("w2_pad", [128, KC * (D + 1) - 2 * KD * FH], F32, w2_end)
        ctx.enter_context(w2_end)

        one_ctx = ExitStack()
        w1n_sb = sb("w1n_sb", [C, H, D], F32, one_ctx)
        w2n_sb = sb("w2n_sb", [128, KD, HC], F32, one_ctx)
        one_ctx.close()
        two_ctx = ExitStack()
        h2 = sb("h2", [NP, NT, D], F32, two_ctx)
        PT5 = sb("PT5", [NP, NT, GW], F32, two_ctx)
        two_ctx.close()
        LC = sb("LC", [NP, NT, N])

        p1 = ExitStack()
        w1_sb = sb("w1_sb", [128, KD, HC], F32, p1)
        xin = [sb(f"xin{p}", [NP, D], F32, p1) for p in range(2)]
        xn = [sb(f"xn{p}", [NP, D], F32, p1) for p in range(2)]
        xT = [sb(f"xT{p}", [128, KD, NP], F32, p1) for p in range(2)]
        h1st = [sb(f"h1st{p}", [NP, HC], F32, p1) for p in range(2)]
        rows1 = sb("rows1", [H, 2, N], F32, p1)
        stats = [sb(f"stats{p}", [NP, 2, 6], F32, p1) for p in range(2)]
        mv = [sb(f"mv{p}", [NP, 2], F32, p1) for p in range(2)]
        var = [sb(f"var{p}", [NP, 1], F32, p1) for p in range(2)]
        rstd = [sb(f"rstd{p}", [NP, 1], F32, p1) for p in range(2)]
        iota16 = sb("iota16", [CE, N], F16, p1)
        srci = sb("srci", [CE, NCH], I32, p1)
        dsti = sb("dsti", [CE, NCH], I32, p1)
        srcf = sb("srcf", [CE, NCH], F32, p1)
        dstf = sb("dstf", [CE, NCH], F32, p1)
        dsr = sb("dsr", [NS, 2 * CE], I32, p1)
        ohs = [sb(f"ohs{a}", [CE, N], F16, p1) for a in range(2)]
        ohd = [sb(f"ohd{a}", [CE, NP], F16, p1) for a in range(2)]
        cmin = sb("cmin", [NS, 1], F32, p1)
        cmax = sb("cmax", [NS, 1], F32, p1)
        tlo = sb("tlo", [NS, NT], F32, p1)
        cidx = sb("cidx", [NS, 2], F32, p1)
        a1 = sb("a1", [NS, NT], F32, p1)
        a2 = sb("a2", [NS, NT], F32, p1)
        a3 = sb("a3", [NS, NT], F32, p1)
        vv = sb("vv", [NS, 2 * NT], F32, p1)
        vr = sb("vr", [NS, 2 * NT], F32, p1)
        sp0 = sb("sp0", [1, 3 * NT], F32, p1)
        hi0 = sb("hi0", [1, NT], F32, p1)
        p1.close()

        p3 = ExitStack()
        L = [sb(f"L{r}", [NP, N], F32, p3) for r in range(5)]
        PT = [sb(f"PT{s}", [NP, NT, GW], F32, p3) for s in range(3)]
        h1Ts = [sb(f"h1Ts{q}", [C, N], F32, p3) for q in range(2)]
        nadh = [sb(f"nadh{q}", [NP, NT], F32, p3) for q in range(2)]
        b1h = [sb(f"b1h{q}", [C, 1], F32, p3) for q in range(2)]
        mx = [sb(f"mx{q}", [NP, NT], F32, p3) for q in range(2)]
        nm = [sb(f"nm{q}", [NP, NT], F32, p3) for q in range(2)]
        den = [sb(f"den{q}", [NP, NT], F32, p3) for q in range(2)]
        dn = [sb(f"dn{q}", [NP, NT], F32, p3) for q in range(2)]
        rden = [sb(f"rden{q}", [NP, NT], F32, p3) for q in range(2)]
        rdb = [sb(f"rdb{i}", [C, GW], F32, p3) for i in range(2)]
        tmp = [sb(f"tmp{i}", [C, GW], F32, p3) for i in range(2)]
        h1s = [sb(f"h1s{q}", [NP, NT, C], F32, p3) for q in range(2)]
        asb = [sb(f"asb{q}", [NP, 2, N], F32, p3) for q in range(2)]
        p3.close()

        p4 = ExitStack()
        L5 = [sb(f"L5_{j}", [NP, N], F32, p4) for j in range(2)]
        LCt = [sb(f"LCt{j}", [NP, N], F32, p4) for j in range(2)]
        asb2 = sb("asb2", [NP, 2, N], F32, p4)
        rows2 = sb("rows2", [1, 2, N], F32, p4)
        h1Tt = [sb(f"h1Tt{p}", [C, H, NP], F32, p4) for p in range(2)]
        x5 = [sb(f"x5_{j}", [NP, D], F32, p4) for j in range(2)]
        x2 = [sb(f"x2_{j}", [NP, D], F32, p4) for j in range(2)]
        y5 = [sb(f"y5_{j}", [NP, D], F32, p4) for j in range(2)]
        x2f = [sb(f"x2f{j}", [NP, D], F32, p4) for j in range(2)]
        ost = [sb(f"ost{j}", [NP, D], F32, p4) for j in range(2)]
        yT = sb("yT", [128, KD, 2, NP], F32, p4)
        gT = sb("gT", [128, KF, GW], F32, p4)
        mx5 = sb("mx5", [NP, 2], F32, p4)
        nm5 = sb("nm5", [NP, 2], F32, p4)
        den5 = sb("den5", [NP, 2], F32, p4)
        dn5 = sb("dn5", [NP, 2], F32, p4)
        rden5 = sb("rden5", [NP, 2], F32, p4)
        stats5 = [sb(f"stats5_{j}", [NP, 2, 6], F32, p4) for j in range(2)]
        mv5 = [sb(f"mv5_{j}", [NP, 2], F32, p4) for j in range(2)]
        var5 = [sb(f"var5_{j}", [NP, 1], F32, p4) for j in range(2)]
        rstd5 = [sb(f"rstd5_{j}", [NP, 1], F32, p4) for j in range(2)]
        atom_w += [sb(f"atom_w{i}", [128, KD * FH], F32, p4) for i in range(2, 3)]
        atom_b = sb("atom_b", [128, NATOM * KF], F32, p4)
        hid = sb("hid", [128, NATOM * KF, NCLS], F32, p4)
        pick = sb("pick", [128, NATOM, KF, NCLS], F32, p4)
        p4.close()
        p6 = ExitStack()
        gp = sb("gp", [NCLS, 2, D], F32, p6)
        bo = sb("bo", [NCLS, 2, D], F32, p6)
        scr = sb("scr", [NCLS, D], F32, p6)
        cw = sb("cw", [NCLS, 2, D], F32, p6)
        fin = sb("fin", [NCLS, D], F32, p6)
        bal = sb("bal", [NCLS, 2], F32, p6)
        sq = sb("sq", [NCLS, 3], F32, p6)
        nr = sb("nr", [NCLS, 3], F32, p6)
        sr = sb("sr", [NCLS, 3], F32, p6)
        dots = sb("dots", [NCLS, 2], F32, p6)
        lg = [sb(f"lg{i}", [NCLS, 2], F32, p6) for i in range(4)]
        g1 = [sb(f"g1_{i}", [NCLS, 1], F32, p6) for i in range(6)]
        p6.close()

        bank = [ctx.enter_context(nc.psum_tensor(f"bank{b}", [128, 512], F32)) for b in range(8)]

        consts_made = sem("consts_made")
        att_in, w1n_in, w1_in, w2n_in, w2_in = (sem(n) for n in ("att_in", "w1n_in", "w1_in", "w2n_in", "w2_in"))
        ffn_in, bias_in, edges_in = sem("ffn_in"), sem("bias_in"), sem("edges_in")
        wattp, watt_done = sem("wattp"), sem("watt_done")
        x_in = [sem(f"x_in{p}") for p in range(2)]
        stat_step, xn_ready = sem("stat_step"), [sem(f"xn_ready{p}") for p in range(2)]
        xt_full = [sem(f"xt_full{p}") for p in range(2)]
        xT_ready = [sem(f"xT_ready{p}") for p in range(2)]
        logit_full = [sem(f"logit_full{p}") for p in range(2)]
        logit_done = [sem(f"logit_done{p}") for p in range(2)]
        h1_full = [sem(f"h1_full{p}") for p in range(2)]
        h1a_done = [sem(f"h1a_done{p}") for p in range(2)]
        h1b_done = [sem(f"h1b_done{p}") for p in range(2)]
        h1_stored = [sem(f"h1_stored{p}") for p in range(2)]
        rows_stored = sem("rows_stored")
        span_step, span_max, spans_ready = sem("span_step"), sem("span_max"), sem("spans_ready")
        oh_ready = [sem(f"oh_ready{a}") for a in range(2)]
        oh_used = [sem(f"oh_used{a}") for a in range(2)]
        cnt_full = [sem(f"cnt_full{p}") for p in range(2)]
        ln_done = [sem(f"ln_done{p}") for p in range(2)]
        lc_even, lc_odd, lc_stored = sem("lc_even"), sem("lc_odd"), sem("lc_stored")
        head_in = [sem(f"head_in{q}") for q in range(2)]
        nadh_done, stt_done, max_done, nm_ready = (sem(n) for n in ("nadh_done", "stt_done", "max_done", "nm_ready"))
        exp_done, tb_full, tb_evac, agg_done = (sem(n) for n in ("exp_done", "tb_full", "tb_evac", "agg_done"))
        dn_done, rden_ready, rdb_full, rdb_ready = (sem(n) for n in ("dn_done", "rden_ready", "rdb_full", "rdb_ready"))
        mul_done, b1h_done, relu_done = sem("mul_done"), sem("b1h_done"), sem("relu_done")
        h1T_stored = [sem(f"h1T_stored{q}") for q in range(2)]
        tile_in = [sem(f"tile_in{p}") for p in range(2)]
        h2_full = [sem(f"h2_full{p}") for p in range(2)]
        h2a_done = [sem(f"h2a_done{p}") for p in range(2)]
        h2b_done = [sem(f"h2b_done{p}") for p in range(2)]
        rows2_stored, asb2_in = sem("rows2_stored"), sem("asb2_in")
        lct_in = [sem(f"lct_in{j}") for j in range(2)]
        stt5, max5, nm5_ready, exp5 = sem("stt5"), sem("max5"), sem("nm5_ready"), sem("exp5")
        t5_full, t5_evac, y_full, y_evac = sem("t5_full"), sem("t5_evac"), sem("y_full"), sem("y_evac")
        dn5_done, rden5_done, agg5 = sem("dn5_done"), sem("rden5_done"), sem("agg5")
        x5_in = [sem(f"x5_in{j}") for j in range(2)]
        xb_done = [sem(f"xb_done{j}") for j in range(2)]
        x2_done = [sem(f"x2_done{j}") for j in range(2)]
        ln_step, y_ready = sem("ln_step"), sem("y_ready")
        x2f_done = [sem(f"x2f_done{j}") for j in range(2)]
        hid_full, gelu_done, ffn_full = sem("hid_full"), sem("gelu_done"), sem("ffn_full")
        out_done = [sem(f"out_done{j}") for j in range(2)]
        out_stored = [sem(f"out_stored{j}") for j in range(2)]
        atom_in_sem = [sem(f"atom_in_sem{i}") for i in range(3)]
        atom_used, cls_in, hid_done = sem("atom_used"), sem("cls_in"), sem("hid_done")
        pick_zero, pick_done, gate_step, cls_done, cls_stored = (
            sem(n) for n in ("pick_zero", "pick_done", "gate_step", "cls_done", "cls_stored"))
        gate_exp, gate_root = sem("gate_exp"), sem("gate_root")
        powers_set, rstd_ready, rstd5_ready = sem("powers_set"), sem("rstd_ready"), sem("rstd5_ready")

        block = ctx.enter_context(nc.Block())

        @block.sync
        def _(sp):
            sp.dma_start(att1[:, 0, :], as1T).then_inc(att_in, 16)
            sp.dma_start(att1[:, 1, :], ad1T).then_inc(att_in, 16)

            def load_x(p, t):
                sp.dma_start(xin[p][:, :], x[ds(t * NP, NP), :]).then_inc(x_in[p], 16)

            def store_h1(p, i):
                sp.wait_ge(h1a_done[p], i + 1)
                sp.wait_ge(h1b_done[p], i + 1)
                sp.dma_start(h1_d[ds((2 * i + p) * NP, NP), :], h1st[p][:, :]).then_inc(h1_stored[p], 16)

            load_x(0, 0)
            load_x(1, 1)
            sp.dma_start(dsti[:, :], dst_cols).then_inc(edges_in, 16)
            sp.dma_start(srci[:, :], src_cols).then_inc(edges_in, 16)
            sp.dma_start(dsr[:, :], dst_rows).then_inc(edges_in, 16)
            with sp.Fori(0, NG - 1) as i:
                for p in range(2):
                    sp.wait_ge(xn_ready[p], i + 1)
                    load_x(p, 2 * i + p + 2)
                for p in range(2):
                    store_h1(p, i)
            for p in range(2):
                store_h1(p, NG - 1)
            for p in range(2):
                sp.wait_ge(logit_done[p], NG)
            sp.dma_start(row_d, rows1[:, :, :]).then_inc(rows_stored, 16)

            for p, done in ((0, lc_even), (1, lc_odd)):
                with sp.Fori(0, NG) as i:
                    sp.wait_ge(done, i + 1)
                    sp.dma_start(lc_d[ds((2 * i + p) * NP, NP), :], LC[:, ds(2 * i + p, 1), :]
                                 .rearrange("p t n -> p (t n)")).then_inc(lc_stored, 16)

            def load_head(q, h):
                sp.dma_start(h1s[q][:, :, :], h1_d[:, ds(h * C, C)].rearrange("(s p) c -> p s c", p=NP)
                             ).then_inc(head_in[q], 16)
                row = row_d[ds(h, 1), :, :].rearrange("a b n -> a (b n)")
                sp.dma_start(asb[q][:, :, :].rearrange("p b n -> p (b n)"), row.to_broadcast([NP, 2 * N])
                             ).then_inc(head_in[q], 16)

            def store_head(q, hh):
                sp.wait_ge(relu_done, NG * (2 * hh + q) + NG)
                sp.dma_start(h1T_d[ds(2 * hh + q, 1), :, :].rearrange("a c n -> (a c) n"), h1Ts[q][:, :]
                             ).then_inc(h1T_stored[q], 16)

            for p in range(2):
                sp.wait_ge(h1_stored[p], 16 * NG)
            sp.wait_ge(rows_stored, 16)
            sp.wait_ge(cnt_full[1], NG)
            for q in range(2):
                load_head(q, q)
            with sp.Fori(0, H // 2 - 1) as hh:
                for q in range(2):
                    sp.wait_ge(agg_done, NG * (2 * hh + q) + NG)
                    sp.wait_ge(stt_done, NT * (2 * hh + q) + NT)
                    load_head(q, 2 * hh + q + 2)
                    store_head(q, hh)
            for q in range(2):
                store_head(q, H // 2 - 1)

            for q in range(2):
                sp.wait_ge(h1T_stored[q], 16 * (H // 2))
            sp.wait_ge(relu_done, NG * H)
            def load_tile(p, t):
                sp.dma_start(h1Tt[p][:, :, :], h1T_d[:, :, ds(t * NP, NP)].rearrange("h c n -> c h n")
                             ).then_inc(tile_in[p], 16)
            sp.wait_ge(agg_done, NG * H)
            sp.wait_ge(mul_done, NG * H)
            sp.wait_ge(lc_stored, 16 * NT)
            load_tile(0, 0)
            load_tile(1, 1)
            for j in range(2):
                sp.dma_start(LCt[j][:, :], lc_d[(NT - 1 - j) * NP:(NT - j) * NP, :]).then_inc(lct_in[j], 16)
            with sp.Fori(0, NG - 1) as i:
                for p in range(2):
                    sp.wait_ge(h2_full[p], i + 1)
                    load_tile(p, 2 * i + p + 2)
            for p in range(2):
                sp.wait_ge(h2b_done[p], NG)
            sp.dma_start(row2_d, rows2[:, :, :]).then_inc(rows2_stored, 16)
            sp.wait_ge(rows2_stored, 16)
            sp.dma_start(asb2[:, :, :].rearrange("p b n -> p (b n)"),
                         row2_d.rearrange("a b n -> a (b n)").to_broadcast([NP, 2 * N])).then_inc(asb2_in, 16)

            def lc_load(i):
                for j in range(2):
                    sp.wait_ge(max5, 2 * i + j - 1)
                    alone(sp)
                    sp.dma_start(LCt[j][:, :], lc_d[ds((NT - 1 - j) * NP - i * GW, NP), :]).then_inc(lct_in[j], 16)

            def out_store(i):
                for j in range(2):
                    sp.wait_ge(out_done[j], i + 1)
                    alone(sp)
                    sp.dma_start(out[ds((NT - 1 - j) * NP - i * GW, NP), :], ost[j][:, :]
                                 ).then_inc(out_stored[j], 16)

            for i in range(1, 3):
                lc_load(i)
            with sp.Fori(3, NG) as i:
                lc_load(i)
                out_store(i + -3)
            for i in range(NG - 3, NG):
                out_store(i)
            for j in range(2):
                sp.wait_ge(out_stored[j], 16 * NG)
            sp.wait_ge(cls_done, 1)
            sp.dma_start(out[0:NCLS, :], fin[:, :]).then_inc(cls_stored, 16)
            sp.wait_ge(cls_stored, 16)

        @block.gpsimd
        def _(pool):
            pool.memset(ident[:, :], 0.0).then_inc(consts_made, 1)
            pool.wait_ge(consts_made, 1)
            pool.affine_select(out=ident[:, :], in_=ident[:, :], compare_op=ALU.not_equal, fill=1.0,
                               base=0, pattern=[[-1, 128]], channel_multiplier=1).then_inc(consts_made, 1)
            pool.memset(zeros16[:, :], 0.0).then_inc(consts_made, 1)
            pool.memset(tiny[:, :], 2.0 ** -60).then_inc(consts_made, 1)
            pool.iota(iota16[:, :], pattern=[[1, N]], base=0, channel_multiplier=0,
                      allow_small_or_imprecise_dtypes=True).then_inc(consts_made, 1)
            pool.iota(tlo[:, :], pattern=[[NP, NT]], base=0, channel_multiplier=0,
                      allow_small_or_imprecise_dtypes=True).then_inc(consts_made, 1)
            pool.iota(cidx[:, 0:1], pattern=[[0, 1]], base=NS, channel_multiplier=-1,
                      allow_small_or_imprecise_dtypes=True).then_inc(consts_made, 1)
            pool.iota(cidx[:, 1:2], pattern=[[0, 1]], base=1, channel_multiplier=1,
                      allow_small_or_imprecise_dtypes=True).then_inc(consts_made, 1)
            pool.memset(powers[:, 0:1], -0.5).then_inc(powers_set, 1)
            pool.memset(powers[:, 1:4], 0.5).then_inc(powers_set, 1)

            def rstd_of(p, i):
                pool.wait_ge(stat_step, 3 * (2 * i + p) + 3)
                freed(pool, xn_ready[p], i)
                pool.tensor_tensor(rstd[p][:, :], var[p][:, :], powers[:, 0:1], ALU.pow).then_inc(rstd_ready, 1)

            pool.wait_ge(powers_set, 2)
            rstd_of(0, 0)
            rstd_of(1, 0)
            pool.wait_ge(span_step, 8)
            pool.partition_all_reduce(vr[:, :], vv[:, :], NS, RMAX).then_inc(span_max, 1)
            with pool.Fori(1, NG) as i:
                rstd_of(0, i)
                rstd_of(1, i)

            def relu(hh, k, first=False, last=False):
                lag = 3
                if (first and k < lag) or (last and k - lag >= 2 * NG):
                    return
                q, g, n, h = at(hh, k, lag)
                if g == 0:
                    pool.tensor_copy(b1h[q][:, :], b1_sb[:, ds(h, 1)]).then_inc(b1h_done, 1)
                    pool.wait_ge(b1h_done, h + 1)
                    pool.wait_ge(h1T_stored[q], hh * 16)
                pool.wait_ge(mul_done, n + 1)
                alone(pool)
                pool.tensor_scalar(h1Ts[q][:, g * GW:(g + 1) * GW], tmp[(k - lag) % 2][:, :], b1h[q][:, 0:1],
                                   0.0, ALU.add, ALU.max).then_inc(relu_done, 1)

            pool.wait_ge(bias_in, 16 * 4)
            pool.wait_ge(cnt_full[1], NG)
            for k in range(2 * NG):
                relu(0, k, first=True)
            with pool.Fori(1, H // 2) as hh:
                for k in range(2 * NG):
                    relu(hh, k)
            for k in range(2 * NG, 2 * NG + 3):
                relu(H // 2 - 1, k, last=True)

            def load_x5(i, j):
                pool.dma_start(x5[j][:, :], x[ds((NT - 1 - j) * NP - i * GW, NP), :]).then_inc(x5_in[j], 16)

            def add_biases(i, last=False):
                for j in range(2):
                    pool.wait_ge(x5_in[j], 16 * (i + 1))
                    pool.tensor_tensor(x5[j][:, :], x5[j][:, :], b2_sb[:, :], ALU.add).then_inc(xb_done[j], 1)
                for j in range(2):
                    pool.wait_ge(x2_done[j], i + 1)
                    alone(pool)
                    if not last:
                        load_x5(i + 1, j)
                    pool.wait_ge(ln_step, 3 * (2 * i + j) + 3)
                    pool.tensor_tensor(rstd5[j][:, :], var5[j][:, :], powers[:, 0:1], ALU.pow).then_inc(rstd5_ready, 1)
                    freed(pool, out_done[j], i)
                    pool.tensor_tensor(x2f[j][:, :], x2[j][:, :], fc2b_sb[:, :], ALU.add).then_inc(x2f_done[j], 1)

            pool.wait_ge(h1T_stored[0], 16 * (H // 2))
            pool.wait_ge(h1T_stored[1], 16 * (H // 2))
            pool.wait_ge(agg_done, NG * H)
            for j in range(2):
                load_x5(0, j)
            rounds(pool, NG - 1, add_biases)
            add_biases(NG - 1, last=True)
            pool.memset(pick[:, :, :, :], 0.0).then_inc(pick_zero, 1)
            pool.wait_ge(gate_step, 5)
            pool.tensor_tensor(sr[:, :], sq[:, :], powers[0:NCLS, 1:4], ALU.pow).then_inc(gate_root, 1)

        @block.scalar
        def _(act):
            act.dma_start(w1n_sb[:, :, :], W1.rearrange("(h c) d -> c h d", c=C)).then_inc(w1n_in, 16)
            act.dma_start(w1_sb[:, :, :], W1T.rearrange("(k p) n -> p k n", p=128)).then_inc(w1_in, 16)
            act.dma_start(w2n_sb[:, :, :], W2.rearrange("(k p) n -> p k n", p=128)).then_inc(w2n_in, 16)
            act.dma_start(att2[:, 0, :], as2T).then_inc(att_in, 16)
            act.dma_start(att2[:, 1, :], ad2T).then_inc(att_in, 16)
            act.dma_start(w2_sb[:, :, 0:D], W2T.rearrange("(k p) n -> p k n", p=128)).then_inc(w2_in, 16)
            act.dma_start(fc1_sb[:, :, :], fc1T.rearrange("(k p) n -> p k n", p=128)).then_inc(ffn_in, 16)
            act.dma_start(fc2_sb[:, :, :], fc2T.rearrange("(k p) n -> p k n", p=128)).then_inc(ffn_in, 16)
            act.dma_start(b1_sb[:, :], b1c).then_inc(bias_in, 16)
            act.dma_start(fc1b_sb[:, :], fc1b).then_inc(bias_in, 16)
            act.dma_start(b2_sb[:, :], b2.to_broadcast([NP, D])).then_inc(bias_in, 16)
            act.dma_start(fc2b_sb[:, :], fc2b.to_broadcast([NP, D])).then_inc(bias_in, 16)

            def tile_features(i):
                for p in range(2):
                    act.wait_ge(xt_full[p], i + 1)
                    freed(act, h1_full[p], i)
                    act.copy(xT[p][:, 0:4, :], bank[2 * p][:, 0:4 * NP].rearrange("p (k n) -> p k n", k=4))
                    act.copy(xT[p][:, 4:6, :], bank[2 * p + 1][:, 0:2 * NP].rearrange("p (k n) -> p k n", k=2)
                             ).then_inc(xT_ready[p], 1)
                for p in range(2):
                    act.wait_ge(h1_full[p], i + 1)
                    freed(act, h1_stored[p], 16 * i)
                    act.copy(h1st[p][:, 0:512], bank[4 + 2 * p][0:NP, :]).then_inc(h1a_done[p], 1)

            rounds(act, NG, tile_features)

            act.wait_ge(consts_made, 4)
            act.wait_ge(watt_done, 2)
            with act.Fori(0, NG) as i:
                for p in range(2):
                    act.wait_ge(cnt_full[p], i + 1)
                    for b, (c0, w) in enumerate(BANKS3):
                        last = act.activation(LC[:, ds(2 * i + p, 1), c0:c0 + w].rearrange("p t n -> p (t n)"),
                                              bank[3 * p + b][0:NP, 0:w], ACT.Ln, bias=tiny[:, 0:1], scale=2.0)
                    last.then_inc(ln_done[p], 1)

            def exp(hh, k, first=False, last=False):
                if last:
                    return
                q, g, n, h = at(hh, k, 0)
                act.wait_ge(nm_ready, n + 1)
                for j in range(2):
                    r, t = (2 * k + j) % 5, 2 * g + j
                    e = act.activation(L[r][:, :], L[r][:, :], ACT.Exp, bias=nm[q][:, t:t + 1], scale=1.0,
                                       accum_out=den[q][:, t:t + 1])
                e.then_inc(exp_done, 1)

            def evac(hh, k, bs, first=False, last=False):
                lag = 1
                if (first and k < lag) or (last and k - lag >= 2 * NG):
                    return
                q, g, n, h = at(hh, k, lag)
                for b in bs:
                    act.wait_ge(tb_full, NG * n + b + 1)
                    if b == 0 and not (first and k - lag < PTFREE[g] + 1):
                        act.wait_ge(agg_done, n + -PTFREE[g])
                    act.copy(PT[PTSLOT[g]][:, 2 * b:2 * b + 2, :],
                             bank[TBANK[b]][0:NP, 0:2 * GW].rearrange("p (s n) -> p s n", s=2)
                             ).then_inc(tb_evac, 1)

            def rdb_copy(hh, k, first=False, last=False):
                lag = 2
                if (first and k < lag) or (last and k - lag >= 2 * NG):
                    return
                q, g, n, h = at(hh, k, lag)
                act.wait_ge(rdb_full, n + 1)
                if not (first and k - lag < 2):
                    act.wait_ge(mul_done, n + -1)
                i = (k - lag) % 2
                act.copy(rdb[i][:, :], bank[4 + i][:, 0:GW]).then_inc(rdb_ready, 1)

            def step(hh, k, **at_end):
                exp(hh, k, **at_end)
                evac(hh, k, [0, 1, 2], **at_end)
                evac(hh, k, [3, 4], **at_end)
                rdb_copy(hh, k, **at_end)

            for k in range(2 * NG):
                step(0, k, first=True)
            with act.Fori(1, H // 2) as hh:
                for k in range(2 * NG):
                    step(hh, k)
            for k in range(2 * NG, 2 * NG + 2):
                step(H // 2 - 1, k, last=True)

            act.wait_ge(stt_done, NT * H)
            act.wait_ge(max_done, NT * H)
            act.wait_ge(lc_stored, 16 * NT)
            with act.Fori(0, NG) as i:
                for p in range(2):
                    act.wait_ge(h2_full[p], i + 1)
                    act.copy(h2[:, ds(2 * i + p, 1), 0:HALF].rearrange("p t n -> p (t n)"),
                             bank[2 * p][0:NP, 0:HALF]).then_inc(h2a_done[p], 1)

            atoms = [(atom_inT, a) for a in range(NATOM)] + [(atom_outT, a) for a in range(NATOM)]

            def load_atom(s):
                which, a = atoms[s]
                if s >= 3:
                    act.wait_ge(atom_used, s - 2)
                act.dma_start(atom_w[s % 3][:, :].rearrange("p (k n) -> p k n", k=KD if s < NATOM else KF),
                              which[a].rearrange("(k p) n -> p k n", p=128)).then_inc(atom_in_sem[s % 3], 16)

            act.wait_ge(relu_done, NG * H)
            for q in range(2):
                act.wait_ge(h1T_stored[q], 16 * (H // 2))
            act.wait_ge(h2_full[1], NG)
            act.dma_start(atom_b[:, :], atom_inb).then_inc(cls_in, 16)
            for s in range(3):
                load_atom(s)

            def exp_5(i):
                act.wait_ge(nm5_ready, i + 1)
                for j in range(2):
                    e = act.activation(L5[j][:, :], L5[j][:, :], ACT.Exp, bias=nm5[:, j:j + 1], scale=1.0,
                                       accum_out=den5[:, j:j + 1])
                e.then_inc(exp5, 1)

            def evac_5(i, first=False):
                for b in range(5):
                    act.wait_ge(t5_full, 5 * i + b + 1)
                    if b == 0 and not first:
                        act.wait_ge(agg5, 2 * i)
                    act.copy(PT5[:, 2 * b:2 * b + 2, :],
                             bank[b % 2][0:NP, 0:2 * GW].rearrange("p (s n) -> p s n", s=2)).then_inc(t5_evac, 1)

            def ffn_5(i):
                for c in range(3):
                    act.wait_ge(y_full, 3 * i + c + 1)
                    act.copy(yT[:, 2 * c:2 * c + 2, :, :], bank[(c + 1) % 2][:, 0:2 * GW]
                             .rearrange("p (k j n) -> p k j n", k=2, j=2)).then_inc(y_evac, 1)
                act.wait_ge(hid_full, i + 1)
                for m in range(KF):
                    g = act.activation(gT[:, m, :], bank[6 + m // 2][:, (m % 2) * GW:(m % 2 + 1) * GW], ACT.Gelu,
                                       bias=fc1b_sb[:, m:m + 1], scale=1.0)
                g.then_inc(gelu_done, 1)

            exp_5(0)
            evac_5(0, first=True)
            with act.Fori(1, NG) as i:
                exp_5(i)
                evac_5(i)
                ffn_5(i + -1)
            ffn_5(NG - 1)

            act.wait_ge(t5_full, NG * NG)
            act.wait_ge(max5, NT)
            for r, rows in enumerate(([r for _, r in ATOM_SRC], [l for l, _ in ATOM_SRC])):
                for n in range(0, NCLS):
                    act.dma_start(bo[n:n + 1, r, :], atom_outb[rows[n]:rows[n] + 1, :]).then_inc(cls_in, 16)
            act.dma_start(gp[:, :, :], gate_pair).then_inc(cls_in, 16)
            act.dma_start(bal[:, :], balance).then_inc(cls_in, 16)
            for s in range(3, NATOM):
                load_atom(s)
            for a in range(NATOM):
                act.wait_ge(atom_used, a + 1)
                if a == 0:
                    act.wait_ge(cls_in, 16)
                for m in range(KF):
                    g = act.activation(hid[:, a * KF + m, :], bank[2 + a % 2][:, m * 8:m * 8 + NCLS], ACT.Gelu,
                                       bias=atom_b[:, a * KF + m:a * KF + m + 1], scale=1.0)
                g.then_inc(hid_done, 1)
                if a < 3:
                    load_atom(NATOM + a)
            act.wait_ge(gate_step, 12)
            act.activation(lg[2][:, :], lg[1][:, :], ACT.Exp).then_inc(gate_exp, 1)
            load_atom(NATOM + 3)
            load_atom(NATOM + 4)

        @block.tensor
        def _(pe):
            pe.wait_ge(att_in, 16 * 4)
            pe.wait_ge(w1n_in, 16)
            for h in range(H):
                for k in range(KD):
                    mm = pe.matmul(bank[6][:, 2 * H * k + h:2 * H * (k + 1):H], w1n_sb[:, h, k * 128:(k + 1) * 128],
                                   att1[:, :, h], start=True, stop=True)
            mm.then_inc(wattp, 1)
            pe.wait_ge(consts_made, 3)
            pe.wait_ge(watt_done, 1)
            pe.wait_ge(w1_in, 16)

            def turn(p, i):
                pe.wait_ge(xn_ready[p], i + 1)
                freed(pe, xT_ready[p], i)
                freed(pe, logit_done[p], i)
                for k in range(KD):
                    b, c = (2 * p, k) if k < 4 else (2 * p + 1, k - 4)
                    mm = pe.transpose(bank[b][:, c * NP:(c + 1) * NP], xn[p][:, k * 128:(k + 1) * 128],
                                      ident[0:NP, 0:NP])
                mm.then_inc(xt_full[p], 1)

            def products(p, i):
                pe.wait_ge(xT_ready[p], i + 1)
                lb = bank[2 * p + 1]
                for k in range(KD):
                    pe.matmul(lb[0:H, 256:256 + NP], watt1[:, k, 0:H], xT[p][:, k, :],
                              start=(k == 0), stop=(k == KD - 1))
                for k in range(KD):
                    mm = pe.matmul(lb[0:NP, 384:384 + H], xT[p][:, k, :], watt1[:, k, H:2 * H],
                                   start=(k == 0), stop=(k == KD - 1))
                mm.then_inc(logit_full[p], 1)
                freed(pe, h1a_done[p], i)
                freed(pe, h1b_done[p], i)
                for half in range(2):
                    for k in range(KD):
                        mm = pe.matmul(bank[4 + 2 * p + half][0:NP, :], xT[p][:, k, :],
                                       w1_sb[:, k, half * 512:(half + 1) * 512],
                                       start=(k == 0), stop=(k == KD - 1))
                mm.then_inc(h1_full[p], 1)

            def tile_products(i):
                turn(0, i)
                turn(1, i)
                products(0, i)
                products(1, i)

            rounds(pe, NG, tile_products)

            pe.wait_ge(w2n_in, 16)
            pe.wait_ge(h1b_done[1], NG)
            for c in range(KC):
                for k in range(KD):
                    mm = pe.matmul(bank[7][:, 2 * c:2 * c + 2], w2n_sb[:, k, c * 128:(c + 1) * 128],
                                   att2[:, :, k], start=(k == 0), stop=(k == KD - 1))
            mm.then_inc(wattp, 1)

            for p in range(2):
                pe.wait_ge(logit_done[p], NG)
                pe.wait_ge(h1a_done[p], NG)
                pe.wait_ge(h1b_done[p], NG)
            pe.wait_ge(spans_ready, 1)
            pe.wait_ge(consts_made, 5)

            def clear(p, begin):
                for b, (c0, w) in enumerate(BANKS3):
                    mm = pe.matmul(bank[3 * p + b][0:NP, 0:w], zeros16[:, 0:NP], iota16[:, c0:c0 + w],
                                   start=begin, stop=not begin, skip_group_check=True)
                return mm

            def count_edges(i):
                for p in range(2):
                    count = pe.value_load(spans[0:1, ds(2 * i + (NT + p), 1)], min_val=1, max_val=NS)
                    before = pe.value_load(spans[0:1, ds(2 * i + (2 * NT + p), 1)], min_val=0, max_val=NS * NT)
                    freed(pe, ln_done[p], i)
                    clear(p, True)
                    with pe.Fori(0, count) as c:
                        for a in range(2):
                            pe.wait_ge(oh_ready[a], before + c + 1)
                            for b, (c0, w) in enumerate(BANKS3):
                                mm = pe.matmul(bank[3 * p + b][0:NP, 0:w], ohd[a][:, :], ohs[a][:, c0:c0 + w],
                                               start=False, stop=False, skip_group_check=True)
                            mm.then_inc(oh_used[a], 1)
                    clear(p, False).then_inc(cnt_full[p], 1)

            rounds(pe, NG, count_edges)

            def turn_bank(hh, k, b, first=False, last=False):
                lag = 1
                if (first and k < lag) or (last and k - lag >= 2 * NG):
                    return
                q, g, n, h = at(hh, k, lag)
                if b == 0:
                    pe.wait_ge(exp_done, n + 1)
                if not (first and k == lag and b < 4):
                    pe.wait_ge(tb_evac, NG * n + TFREE[b])
                for s in range(2):
                    for j in range(2):
                        mm = pe.transpose(bank[TBANK[b]][0:NP, (2 * s + j) * NP:(2 * s + j + 1) * NP],
                                          L[(2 * (k - lag) + j) % 5][:, (2 * b + s) * NP:(2 * b + s + 1) * NP],
                                          ident[0:NP, 0:NP])
                mm.then_inc(tb_full, 1)

            def aggregate(hh, k, b, first=False, last=False):
                lag = 2
                if (first and k < lag) or (last and k - lag >= 2 * NG):
                    return
                q, g, n, h = at(hh, k, lag)
                if b == 0:
                    pe.wait_ge(tb_evac, NG * n + NG)
                    if g == 0:
                        pe.wait_ge(head_in[q], 32 * (hh + 1))
                    if not (first and k - lag < 2):
                        pe.wait_ge(mul_done, n + -1)
                for s in range(2 * b, 2 * b + 2):
                    mm = pe.matmul(bank[2 + (k - lag) % 2][:, 0:GW], h1s[q][:, s, :], PT[PTSLOT[g]][:, s, :],
                                   start=(s == 0), stop=(s == NT - 1))
                if b == 4:
                    mm.then_inc(agg_done, 1)

            def spread(hh, k, first=False, last=False):
                lag = 2
                if (first and k < lag) or (last and k - lag >= 2 * NG):
                    return
                q, g, n, h = at(hh, k, lag)
                pe.wait_ge(rden_ready, n + 1)
                if not (first and k - lag < 2):
                    pe.wait_ge(rdb_ready, n + -1)
                for j in range(2):
                    t = 2 * g + j
                    mm = pe.matmul(bank[4 + (k - lag) % 2][:, j * NP:(j + 1) * NP],
                                   rden[q][:, t:t + 1].to_broadcast([NP, C]), ident[0:NP, 0:NP],
                                   start=True, stop=True)
                mm.then_inc(rdb_full, 1)

            def step(hh, k, **at_end):
                for b in range(5):
                    turn_bank(hh, k, b, **at_end)
                    aggregate(hh, k, b, **at_end)
                    if b == 1:
                        spread(hh, k, **at_end)

            for p in range(2):
                pe.wait_ge(ln_done[p], NG)
            for k in range(2 * NG):
                step(0, k, first=True)
            with pe.Fori(1, H // 2) as hh:
                for k in range(2 * NG):
                    step(hh, k)
            for k in range(2 * NG, 2 * NG + 2):
                step(H // 2 - 1, k, last=True)

            pe.wait_ge(w2_in, 16)
            pe.wait_ge(watt_done, 3)
            pe.wait_ge(mul_done, NG * H)
            pe.wait_ge(rdb_ready, NG * H)
            pe.wait_ge(tb_evac, NG * NG * H)
            def second_features(i):
                for p in range(2):
                    pe.wait_ge(tile_in[p], 16 * (i + 1))
                    freed(pe, h2a_done[p], i)
                    freed(pe, h2b_done[p], i)
                    for k in range(KC):
                        pe.matmul(bank[4 + p][0:1, 0:NP], watt2[:, k, 0:1], h1Tt[p][:, k, :],
                                  start=(k == 0), stop=(k == KC - 1))
                    for b, (c0, w) in enumerate(((0, HALF), (HALF, HALF + 1))):
                        for k in range(KC):
                            mm = pe.matmul(bank[2 * p + b][0:NP, 0:w], h1Tt[p][:, k, :], w2_sb[:, k, c0:c0 + w],
                                           start=(k == 0), stop=(k == KC - 1))
                    mm.then_inc(h2_full[p], 1)

            rounds(pe, NG, second_features)

            for p in range(2):
                pe.wait_ge(h2a_done[p], NG)
                pe.wait_ge(h2b_done[p], NG)

            def turn_5(i, first=0):
                pe.wait_ge(exp5, i + 1)
                for b in range(5):
                    if b >= 2:
                        pe.wait_ge(t5_evac, 5 * i + (b - 1))
                    elif first < 1:
                        pe.wait_ge(t5_evac, 5 * i)
                        if first < 0:
                            pe.wait_ge(y_evac, 3 * i + -3)
                    for s in range(2):
                        for j in range(2):
                            mm = pe.transpose(bank[b % 2][0:NP, (2 * s + j) * NP:(2 * s + j + 1) * NP],
                                              L5[j][:, (2 * b + s) * NP:(2 * b + s + 1) * NP], ident[0:NP, 0:NP])
                    mm.then_inc(t5_full, 1)

            def aggregate_5(i, j):
                if j == 0:
                    pe.wait_ge(t5_evac, 5 * i + 5)
                freed(pe, x2_done[j], i)
                for b in range(2):
                    for s in range(NT):
                        mm = pe.matmul(bank[2 + 2 * j + b][0:NP, 0:HALF], PT5[:, s, j * NP:(j + 1) * NP],
                                       h2[:, s, b * HALF:(b + 1) * HALF], start=(s == 0), stop=(s == NT - 1))
                mm.then_inc(agg5, 1)

            def turn_y(i, first=False):
                pe.wait_ge(y_ready, 2 * i + 2)
                for c in range(3):
                    if c < 2:
                        if not first:
                            pe.wait_ge(t5_evac, 5 * i + (9 + c))
                    else:
                        pe.wait_ge(y_evac, 3 * i + 1)
                    for kk in range(2):
                        for j in range(2):
                            k = 2 * c + kk
                            mm = pe.transpose(bank[(c + 1) % 2][:, (2 * kk + j) * NP:(2 * kk + j + 1) * NP],
                                              y5[j][:, k * 128:(k + 1) * 128], ident[0:NP, 0:NP])
                    mm.then_inc(y_full, 1)

            def ffn_up(i, first=False):
                pe.wait_ge(y_evac, 3 * i + 3)
                freed(pe, out_done[1], i)
                for m in range(KF):
                    for k in range(KD):
                        mm = pe.matmul(bank[6 + m // 2][:, (m % 2) * GW:(m % 2 + 1) * GW],
                                       fc1_sb[:, k, m * 128:(m + 1) * 128],
                                       yT[:, k, :, :].rearrange("p j n -> p (j n)"),
                                       start=(k == 0), stop=(k == KD - 1))
                mm.then_inc(hid_full, 1)

            def ffn_down(i, j):
                if j == 0:
                    pe.wait_ge(gelu_done, i + 1)
                else:
                    pe.wait_ge(out_done[0], i + 1)
                for b in range(2):
                    for m in range(KF):
                        mm = pe.matmul(bank[6 + b][0:NP, 0:HALF], gT[:, m, j * NP:(j + 1) * NP],
                                       fc2_sb[:, m, b * HALF:(b + 1) * HALF], start=(m == 0), stop=(m == KF - 1))
                mm.then_inc(ffn_full, 1)

            pe.wait_ge(ffn_in, 32)
            turn_5(0, first=1)
            aggregate_5(0, 0)
            aggregate_5(0, 1)

            def step_5(i, first):
                turn_5(i, first=first)
                turn_y(i + -1)
                ffn_up(i + -1)
                aggregate_5(i, 0)
                ffn_down(i + -1, 0)
                aggregate_5(i, 1)
                ffn_down(i + -1, 1)

            step_5(1, 0)
            with pe.Fori(2, NG) as i:
                step_5(i, -1)
            turn_y(NG - 1, first=True)
            ffn_up(NG - 1)
            ffn_down(NG - 1, 0)
            ffn_down(NG - 1, 1)

            pe.wait_ge(x2_done[0], NG)
            pe.wait_ge(x2_done[1], NG)
            for a in range(NATOM):
                pe.wait_ge(atom_in_sem[a % 3], 16 * (a // 3 + 1))
                if a >= 2:
                    pe.wait_ge(hid_done, a - 1)
                w = atom_w[a % 3][:, :].rearrange("p (k n) -> p k n", k=KD)
                for m in range(KF):
                    for k in range(KD):
                        mm = pe.matmul(bank[2 + a % 2][:, m * 8:m * 8 + NCLS], w[:, k, m * 128:(m + 1) * 128],
                                       yT[:, k, 1, 0:NCLS], start=(k == 0), stop=(k == KD - 1))
                mm.then_inc(atom_used, 1)
            pe.wait_ge(pick_done, 12)
            pe.wait_ge(out_done[1], NG)
            for a in range(NATOM):
                s = NATOM + a
                pe.wait_ge(atom_in_sem[s % 3], 16 * (s // 3 + 1))
                w = atom_w[s % 3][:, :].rearrange("p (m n) -> p m n", m=KF)
                r = 1 if a < 3 else 0
                for b in range(2):
                    for m in range(KF):
                        mm = pe.matmul(bank[4 + 2 * r + b][0:NCLS, 0:HALF], pick[:, a, m, :],
                                       w[:, m, b * HALF:(b + 1) * HALF], start=(a in (0, 3) and m == 0),
                                       stop=(a in (2, 4) and m == KF - 1))
                mm.then_inc(atom_used, 1)

        @block.vector
        def _(dve):
            def normalise(p, i):
                n = 3 * (2 * i + p)
                dve.wait_ge(x_in[p], 16 * (i + 1))
                for b in range(2):
                    s = dve.bn_stats(stats[p][:, b, :], xin[p][:, b * HALF:(b + 1) * HALF])
                s.then_inc(stat_step, 1)
                dve.wait_ge(stat_step, n + 1)
                alone(dve)
                dve.bn_aggr(mv[p][:, :], stats[p][:, :, :]).then_inc(stat_step, 1)
                dve.wait_ge(stat_step, n + 2)
                dve.tensor_scalar(var[p][:, :], mv[p][:, 1:2], LN_EPS, None, ALU.add).then_inc(stat_step, 1)
                dve.wait_ge(rstd_ready, 2 * i + (p + 1))
                freed(dve, xt_full[p], i)
                dve.tensor_scalar(xn[p][:, :], xin[p][:, :], mv[p][:, 0:1], rstd[p][:, 0:1],
                                  ALU.subtract, ALU.mult).then_inc(xn_ready[p], 1)

            def out_of_psum(p, i):
                t = 2 * i + p
                dve.wait_ge(logit_full[p], i + 1)
                lb = bank[2 * p + 1]
                dve.tensor_copy(rows1[:, 0, ds(t * NP, NP)], lb[0:H, 256:256 + NP])
                dve.tensor_scalar(rows1[:, 1, ds(t * NP, NP)], lb[0:H, 256:256 + NP], SLOPE, None, ALU.mult)
                dve.tensor_scalar(nad1[:, :, ds(t, 1)].rearrange("p h t -> p (h t)"), lb[0:NP, 384:384 + H],
                                  SLOPE - 1.0, None, ALU.mult).then_inc(logit_done[p], 1)
                dve.wait_ge(h1_full[p], i + 1)
                freed(dve, h1_stored[p], 16 * i)
                dve.tensor_copy(h1st[p][:, 512:1024], bank[5 + 2 * p][0:NP, :]).then_inc(h1b_done[p], 1)

            normalise(0, 0)
            normalise(1, 0)

            dve.wait_ge(edges_in, 48)
            dve.tensor_copy(srcf[:, :], srci[:, :])
            dve.tensor_copy(dstf[:, :], dsti[:, :]).then_inc(span_step, 1)
            dve.tensor_reduce(cmin[:, :], dsr[:, :], mybir.AxisListType.X, ALU.min).then_inc(span_step, 1)
            dve.tensor_reduce(cmax[:, :], dsr[:, :], mybir.AxisListType.X, ALU.max).then_inc(span_step, 1)
            dve.wait_ge(span_step, 3)
            dve.wait_ge(consts_made, 8)
            dve.tensor_scalar(a1[:, :], tlo[:, :], cmax[:, 0:1], None, ALU.is_le).then_inc(span_step, 1)
            dve.tensor_scalar(a2[:, :], tlo[:, :], float(NP - 1), cmin[:, 0:1], ALU.add, ALU.is_ge
                              ).then_inc(span_step, 1)
            dve.wait_ge(span_step, 5)
            dve.tensor_tensor(a3[:, :], a1[:, :], a2[:, :], ALU.mult).then_inc(span_step, 1)
            dve.wait_ge(span_step, 6)
            dve.tensor_scalar(vv[:, 0:NT], a3[:, :], cidx[:, 0:1], None, ALU.mult).then_inc(span_step, 1)
            dve.tensor_scalar(vv[:, NT:2 * NT], a3[:, :], cidx[:, 1:2], None, ALU.mult).then_inc(span_step, 1)
            dve.wait_ge(wattp, 1)
            dve.tensor_copy(watt1[:, :, :], bank[6][:, 0:2 * H * KD].rearrange("p (k c) -> p k c", k=KD)
                            ).then_inc(watt_done, 1)

            def features(i):
                for p in range(2):
                    normalise(p, i + 1)
                for p in range(2):
                    out_of_psum(p, i)

            rounds(dve, NG - 1, features)
            for p in range(2):
                out_of_psum(p, NG - 1)
            dve.wait_ge(span_max, 1)
            dve.tensor_scalar(sp0[:, 0:NT], vr[0:1, 0:NT], -1.0, float(NS), ALU.mult, ALU.add).then_inc(span_step, 1)
            dve.wait_ge(span_step, 9)
            dve.tensor_scalar(sp0[:, 0:NT], sp0[:, 0:NT], float(NS - 1), None, ALU.min).then_inc(span_step, 1)
            dve.wait_ge(span_step, 10)
            dve.tensor_tensor(hi0[:, :], vr[0:1, NT:2 * NT], sp0[:, 0:NT], ALU.subtract).then_inc(span_step, 1)
            dve.wait_ge(span_step, 11)
            dve.tensor_scalar(sp0[:, NT:2 * NT], hi0[:, :], 1.0, None, ALU.max).then_inc(span_step, 1)
            dve.memset(sp0[:, 2 * NT:2 * NT + 1], 0.0).then_inc(span_step, 1)
            for t in range(1, NT):
                dve.wait_ge(span_step, 12 + t)
                dve.tensor_tensor(sp0[:, 2 * NT + t:2 * NT + t + 1], sp0[:, 2 * NT + t - 1:2 * NT + t],
                                  sp0[:, NT + t - 1:NT + t], ALU.add).then_inc(span_step, 1)
            dve.wait_ge(span_step, 12 + NT)
            dve.tensor_copy(spans[:, :], sp0[:, :]).then_inc(spans_ready, 1)
            for a in range(2):
                dve.memset(ohd[a][:, :], 0.0).then_inc(oh_used[a], 1)

            dve.wait_ge(wattp, 2)
            dve.tensor_copy(watt2[:, :, :], bank[7][:, 0:2 * KC].rearrange("p (k c) -> p k c", k=KC)
                            ).then_inc(watt_done, 1)
            dve.tensor_copy(w2_sb[:, :, D], bank[7][:, 1:2 * KC:2]).then_inc(watt_done, 1)

            def mend(p, i, done):
                dve.wait_ge(ln_done[p], i + 1)
                v = LC[:, ds(2 * i + p, 1), :].rearrange("p t n -> p (t n)")
                dve.scalar_tensor_tensor(v, v, 1e30, v, ALU.mult, ALU.min).then_inc(done, 1)

            dve.wait_ge(spans_ready, 1)
            with dve.Fori(0, NG) as i:
                for p in range(2):
                    start = dve.value_load(spans[0:1, ds(2 * i + p, 1)], min_val=0, max_val=NS - 1)
                    count = dve.value_load(spans[0:1, ds(2 * i + (NT + p), 1)], min_val=1, max_val=NS)
                    before = dve.value_load(spans[0:1, ds(2 * i + (2 * NT + p), 1)], min_val=0, max_val=NS * NT)
                    with dve.Fori(0, count) as c:
                        pair = (start + c).with_bounds(min_val=0, max_val=NS - 1)
                        for a in range(2):
                            dve.wait_ge(oh_used[a], before + c + 1)
                            dve.tensor_scalar(ohs[a][:, :], iota16[:, :], srcf[:, ds(2 * pair + a, 1)], None,
                                              ALU.is_equal)
                            dve.tensor_scalar(ohd[a][:, :], iota16[:, ds((2 * i + p) * NP, NP)],
                                              dstf[:, ds(2 * pair + a, 1)], None, ALU.is_equal
                                              ).then_inc(oh_ready[a], 1)
                mend(0, i, lc_even)
            with dve.Fori(0, NG) as i:
                mend(1, i, lc_odd)
            dve.wait_ge(lc_odd, NG)
            dve.wait_ge(lc_even, NG)

            def logits(hh, k, first=False, last=False):
                if last:
                    return
                q, g, n, h = at(hh, k, 0)
                if g == 0:
                    dve.wait_ge(head_in[q], 32 * (hh + 1))
                    dve.tensor_copy(nadh[q][:, :], nad1[:, ds(h, 1), :].rearrange("p h t -> p (h t)")
                                    ).then_inc(nadh_done, 1)
                    dve.wait_ge(nadh_done, h + 1)
                for j in range(2):
                    r, t = (2 * k + j) % 5, 2 * g + j
                    if not (first and 2 * k + j < 5):
                        dve.wait_ge(tb_full, NG * n + NG * (j - 2))
                    dve.scalar_tensor_tensor(L[r][:, :], asb[q][:, 1, :], nadh[q][:, t:t + 1], asb[q][:, 0, :],
                                             ALU.add, ALU.max).then_inc(stt_done, 1)
                for j in range(2):
                    r, t = (2 * k + j) % 5, 2 * g + j
                    dve.wait_ge(stt_done, 2 * n + (j + 1))
                    alone(dve)
                    dve.tensor_tensor_reduce(out=L[r][:, :], in0=L[r][:, :], in1=LC[:, t, :], scale=1.0,
                                             scalar=-3e38, op0=ALU.add, op1=ALU.max,
                                             accum_out=mx[q][:, t:t + 1]).then_inc(max_done, 1)
                dve.wait_ge(max_done, 2 * n + 2)
                dve.tensor_scalar(nm[q][:, 2 * g:2 * g + 2], mx[q][:, 2 * g:2 * g + 2], FLOOR, -1.0,
                                  ALU.max, ALU.mult).then_inc(nm_ready, 1)

            def reciprocals(hh, k, first=False, last=False):
                lag = 1
                if (first and k < lag) or (last and k - lag >= 2 * NG):
                    return
                q, g, n, h = at(hh, k, lag)
                dve.wait_ge(exp_done, n + 1)
                dve.tensor_scalar(dn[q][:, 2 * g:2 * g + 2], den[q][:, 2 * g:2 * g + 2], EPS, None, ALU.add
                                  ).then_inc(dn_done, 1)
                dve.wait_ge(dn_done, n + 1)
                dve.reciprocal(rden[q][:, 2 * g:2 * g + 2], dn[q][:, 2 * g:2 * g + 2]).then_inc(rden_ready, 1)

            def multiply(hh, k, first=False, last=False):
                lag = 3
                if (first and k < lag) or (last and k - lag >= 2 * NG):
                    return
                q, g, n, h = at(hh, k, lag)
                dve.wait_ge(agg_done, n + 1)
                dve.wait_ge(rdb_ready, n + 1)
                if not (first and k - lag < 2):
                    dve.wait_ge(relu_done, n + -1)
                i = (k - lag) % 2
                dve.tensor_tensor(tmp[i][:, :], bank[2 + i][:, 0:GW], rdb[i][:, :], ALU.mult).then_inc(mul_done, 1)

            def step(hh, k, **at_end):
                reciprocals(hh, k, **at_end)
                logits(hh, k, **at_end)
                multiply(hh, k, **at_end)

            for k in range(2 * NG):
                step(0, k, first=True)
            with dve.Fori(1, H // 2) as hh:
                for k in range(2 * NG):
                    step(hh, k)
            for k in range(2 * NG, 2 * NG + 3):
                step(H // 2 - 1, k, last=True)

            dve.wait_ge(lc_stored, 16 * NT)
            with dve.Fori(0, NG) as i:
                for p in range(2):
                    t = 2 * i + p
                    dve.wait_ge(h2_full[p], i + 1)
                    dve.tensor_copy(rows2[:, 0, ds(t * NP, NP)], bank[4 + p][0:1, 0:NP])
                    dve.tensor_scalar(rows2[:, 1, ds(t * NP, NP)], bank[4 + p][0:1, 0:NP], SLOPE, None, ALU.mult)
                    dve.tensor_scalar(nad2[:, ds(t, 1)], bank[2 * p + 1][0:NP, HALF:HALF + 1], SLOPE - 1.0, None,
                                      ALU.mult)
                    dve.tensor_copy(h2[:, ds(t, 1), HALF:D].rearrange("p t n -> p (t n)"),
                                    bank[2 * p + 1][0:NP, 0:HALF]).then_inc(h2b_done[p], 1)

            def reciprocals_5(i):
                dve.wait_ge(exp5, i + 1)
                dve.tensor_scalar(dn5[:, :], den5[:, :], EPS, None, ALU.add).then_inc(dn5_done, 1)
                dve.wait_ge(dn5_done, i + 1)
                dve.reciprocal(rden5[:, :], dn5[:, :]).then_inc(rden5_done, 1)

            def logits_5(i, first=False):
                for j in range(2):
                    if not first:
                        dve.wait_ge(t5_full, 5 * i)
                        alone(dve)
                    dve.scalar_tensor_tensor(L5[j][:, :], asb2[:, 1, :], nad2[:, ds((NT - 1 - j) - 2 * i, 1)],
                                             asb2[:, 0, :], ALU.add, ALU.max).then_inc(stt5, 1)
                for j in range(2):
                    dve.wait_ge(stt5, 2 * i + (j + 1))
                    dve.wait_ge(lct_in[j], 16 * (i + 1))
                    alone(dve)
                    dve.tensor_tensor_reduce(out=L5[j][:, :], in0=L5[j][:, :], in1=LCt[j][:, :], scale=1.0,
                                             scalar=-3e38, op0=ALU.add, op1=ALU.max,
                                             accum_out=mx5[:, j:j + 1]).then_inc(max5, 1)
                dve.wait_ge(max5, 2 * i + 2)
                dve.tensor_scalar(nm5[:, :], mx5[:, :], FLOOR, -1.0, ALU.max, ALU.mult).then_inc(nm5_ready, 1)

            def norm_5(i, j, first=False):
                n = 3 * (2 * i + j)
                dve.wait_ge(agg5, 2 * i + (j + 1))
                dve.wait_ge(xb_done[j], i + 1)
                dve.wait_ge(rden5_done, i + 1)
                if not first:
                    dve.wait_ge(x2f_done[j], i)
                for b in range(2):
                    c = slice(b * HALF, (b + 1) * HALF)
                    s = dve.scalar_tensor_tensor(x2[j][:, c], bank[2 + 2 * j + b][0:NP, 0:HALF], rden5[:, j:j + 1],
                                                 x5[j][:, c], ALU.mult, ALU.add)
                s.then_inc(x2_done[j], 1)
                dve.wait_ge(x2_done[j], i + 1)
                for b in range(2):
                    s = dve.bn_stats(stats5[j][:, b, :], x2[j][:, b * HALF:(b + 1) * HALF])
                s.then_inc(ln_step, 1)
                dve.wait_ge(ln_step, n + 1)
                alone(dve)
                dve.bn_aggr(mv5[j][:, :], stats5[j][:, :, :]).then_inc(ln_step, 1)
                dve.wait_ge(ln_step, n + 2)
                dve.tensor_scalar(var5[j][:, :], mv5[j][:, 1:2], LN_EPS, None, ALU.add).then_inc(ln_step, 1)
                dve.wait_ge(rstd5_ready, 2 * i + (j + 1))
                if not first:
                    dve.wait_ge(y_full, 3 * i)
                dve.tensor_scalar(y5[j][:, :], x2[j][:, :], mv5[j][:, 0:1], rstd5[j][:, 0:1],
                                  ALU.subtract, ALU.mult).then_inc(y_ready, 1)

            def out_5(i, j, first=False):
                dve.wait_ge(ffn_full, 2 * i + (j + 1))
                dve.wait_ge(x2f_done[j], i + 1)
                if not first:
                    dve.wait_ge(out_stored[j], 16 * i)
                for b in range(2):
                    c = slice(b * HALF, (b + 1) * HALF)
                    s = dve.tensor_tensor(ost[j][:, c], bank[6 + b][0:NP, 0:HALF], x2f[j][:, c], ALU.add)
                s.then_inc(out_done[j], 1)

            dve.wait_ge(asb2_in, 16)
            for p in range(2):
                dve.wait_ge(h2b_done[p], NG)
            logits_5(0, first=True)
            reciprocals_5(0)
            logits_5(1)
            for j in range(2):
                norm_5(0, j, first=True)
            reciprocals_5(1)
            logits_5(2)
            for j in range(2):
                norm_5(1, j)
                out_5(0, j, first=True)
            with dve.Fori(3, NG) as i:
                reciprocals_5(i + -1)
                logits_5(i)
                for j in range(2):
                    norm_5(i + -1, j)
                    out_5(i + -2, j)
            reciprocals_5(NG - 1)
            for j in range(2):
                norm_5(NG - 1, j)
                out_5(NG - 2, j)
            for j in range(2):
                out_5(NG - 1, j)

            steps = [0]

            def link(ins):
                steps[0] += 1
                ins.then_inc(gate_step, 1)
                dve.wait_ge(gate_step, steps[0])

            y, tok = y5[1][0:NCLS, :], x2[1][0:NCLS, :]
            dve.wait_ge(cls_in, 16 * 15)
            dve.wait_ge(y_ready, NT)
            dve.wait_ge(stt5, NT)
            for in0, in1, to in ((y, y, sq[:, 0:1]), (gp[:, 0, :], gp[:, 0, :], sq[:, 1:2]),
                                 (gp[:, 1, :], gp[:, 1, :], sq[:, 2:3]),
                                 (y, gp[:, 0, :], dots[:, 0:1]), (y, gp[:, 1, :], dots[:, 1:2])):
                link(dve.tensor_tensor_reduce(out=scr[:, :], in0=in0, in1=in1, scale=1.0, scalar=0.0,
                                              op0=ALU.mult, op1=ALU.add, accum_out=to))
            dve.wait_ge(gate_root, 1)
            link(dve.tensor_scalar(nr[:, :], sr[:, :], NORM_EPS, None, ALU.max))
            link(dve.tensor_scalar(lg[0][:, :], nr[:, 1:3], nr[:, 0:1], None, ALU.mult))
            link(dve.reciprocal(lg[1][:, :], lg[0][:, :]))
            link(dve.tensor_tensor(lg[2][:, :], dots[:, :], lg[1][:, :], ALU.mult))
            link(dve.tensor_tensor(lg[0][:, :], lg[2][:, :], bal[:, :], ALU.add))
            link(dve.tensor_reduce(g1[0][:, :], lg[0][:, :], mybir.AxisListType.X, ALU.max))
            link(dve.tensor_scalar(lg[1][:, :], lg[0][:, :], g1[0][:, 0:1], None, ALU.subtract))
            dve.wait_ge(gate_exp, 1)
            link(dve.tensor_reduce(g1[1][:, :], lg[2][:, :], mybir.AxisListType.X, ALU.add))
            link(dve.reciprocal(g1[2][:, :], g1[1][:, :]))
            link(dve.tensor_scalar(lg[3][:, :], lg[2][:, :], g1[2][:, 0:1], None, ALU.mult))
            link(dve.tensor_tensor(g1[3][:, :], lg[3][:, 1:2], lg[3][:, 0:1], ALU.is_gt))
            link(dve.tensor_scalar(g1[4][:, :], g1[3][:, :], -1.0, 1.0, ALU.mult, ALU.add))
            link(dve.tensor_tensor(g1[5][:, :], g1[3][:, :], lg[3][:, 1:2], ALU.mult))
            link(dve.tensor_tensor(g1[0][:, :], g1[4][:, :], lg[3][:, 0:1], ALU.mult))

            dve.wait_ge(pick_zero, 1)
            dve.wait_ge(hid_done, NATOM)
            for n, (l, r) in enumerate(ATOM_SRC):
                for a_from, a_to in ((l, r), (r, l)):
                    dve.tensor_copy(pick[:, a_to, :, n], hid[:, a_from * KF:(a_from + 1) * KF, n]
                                    ).then_inc(pick_done, 1)

            for r, used in ((1, NATOM + 3), (0, NATOM + 5)):
                dve.wait_ge(atom_used, used)
                for b in range(2):
                    c = slice(b * HALF, (b + 1) * HALF)
                    s = dve.tensor_tensor(cw[:, r, c], bank[4 + 2 * r + b][0:NCLS, 0:HALF], bo[:, r, c], ALU.add)
                link(s)
            link(dve.scalar_tensor_tensor(scr[:, :], cw[:, 0, :], g1[0][:, 0:1], tok, ALU.mult, ALU.add))
            dve.scalar_tensor_tensor(fin[:, :], cw[:, 1, :], g1[5][:, 0:1], scr[:, :], ALU.mult, ALU.add
                                     ).then_inc(cls_done, 1)


def kernel(**inputs):
    import numpy as np
    import concourse.bacc as bacc
    from concourse.bass_utils import run_bass_kernel_spmd

    a = {k: np.asarray(v) for k, v in inputs.items()}
    W1, W2 = a["L0_gnn_W1"], a["L0_gnn_W2"]
    fed = {
        "x": a["x"],
        "src_cols": a["src"].reshape(NCH, CE).T,
        "dst_cols": a["dst"].reshape(NCH, CE).T,
        "dst_rows": a["dst"].reshape(NS, 2 * CE),
        "W1": W1,
        "W1T": W1.T,
        "as1T": a["L0_gnn_att_src1"].T,
        "ad1T": a["L0_gnn_att_dst1"].T,
        "b1c": a["L0_gnn_b1"].reshape(H, C).T,
        "W2": W2,
        "W2T": W2.T,
        "as2T": a["L0_gnn_att_src2"].reshape(KD, 128).T,
        "ad2T": a["L0_gnn_att_dst2"].reshape(KD, 128).T,
        "b2": a["L0_gnn_b2"].reshape(1, D),
        "fc1T": a["L0_ffn_fc1_w"].T,
        "fc1b": a["L0_ffn_fc1_b"].reshape(KF, 128).T,
        "fc2T": a["L0_ffn_fc2_w"].T,
        "fc2b": a["L0_ffn_fc2_b"].reshape(1, D),
        "gate_pair": a["L0_ffn_gate_pair"],
        "atom_inT": a["L0_ffn_atom_in_w"].transpose(0, 2, 1),
        "atom_inb": a["L0_ffn_atom_in_b"].reshape(NATOM * KF, 128).T,
        "atom_outT": a["L0_ffn_atom_out_w"].transpose(0, 2, 1),
        "atom_outb": a["L0_ffn_atom_out_b"],
        "balance": a["L0_ffn_balance_bias"],
    }
    nc = bacc.Bacc("TRN2", target_bir_lowering=False, num_devices=1)
    arrays, args = {}, []
    for name, value in fed.items():
        value = np.ascontiguousarray(value)
        arrays[f"in_{name}"] = value
        args.append(nc.dram_tensor(f"in_{name}", value.shape, mybir.dt.from_np(value.dtype), kind="ExternalInput").ap())
    out = nc.dram_tensor("out_0", (N, D), F32, kind="ExternalOutput").ap()
    gnn_ffn_kernel(nc, *args, out)
    r = run_bass_kernel_spmd(nc, [arrays], core_ids=[0])
    return r.results[0]["out_0"]
```

```python
from contextlib import ExitStack

import concourse.bass as bass
from concourse import mybir

F32 = mybir.dt.float32
F16 = mybir.dt.float16
I32 = mybir.dt.int32
ACT = mybir.ActivationFunctionType
ALU = mybir.AluOpType
RMAX = bass.bass_isa.ReduceOp.max

N, D = 1250, 768
H, C = 8, 128
HC = H * C
FH = 384
NE = 21250
NP = 125
NT = N // NP
NG = NT // 2
GW = 2 * NP
CE = 125
NCH = NE // CE
NS = NCH // 2
NQ = (NS + 1) // 2
RING = 4
KD, KC, KF = D // 128, HC // 128, FH // 128
HALF = D // 2
NCLS, NATOM = 6, 5
SLOPE = 0.2
EPS = 1e-16
LN_EPS = 1e-5
NORM_EPS = 1e-12
FLOOR = -1e29
BANKS3 = [(0, 500), (500, 500), (1000, 250)]
TBANK = [0, 1, 6, 7, 0]
TFREE = [0, -3, -2, -1, 1]
ATOM_SRC = [(0, 3), (0, 4), (1, 3), (1, 4), (2, 3), (2, 4)]


def ds(start, size):
    return bass.ds(start, size)


def alone(engine):
    engine.nop(nofuse=True)


def freed(engine, semaphore, value):
    if not (isinstance(value, int) and value <= 0):
        engine.wait_ge(semaphore, value)


def rounds(engine, stop, body):
    body(0)
    with engine.Fori(1, stop) as i:
        body(i)


def at(hh, k, lag):
    kk = k - lag
    return (kk // NG) % 2, kk % NG, 2 * NG * hh + kk, 2 * hh + kk // NG


def gnn_ffn_kernel(nc, x, src_cols, dst_cols, dst_rows, W1, W1T, as1T, ad1T, b1c, W2, W2T, as2T, ad2T,
                   b2, fc1T, fc1b, fc2T, fc2b, gate_pair, atom_inT, atom_inb, atom_outT, atom_outb,
                   balance, out):
    h1_d = nc.dram_tensor("h1_scratch", (N, HC), F32).ap()
    row_d = nc.dram_tensor("src_logit_rows", (H, 2, N), F32).ap()
    row2_d = nc.dram_tensor("src_logit_rows2", (1, 2, N), F32).ap()
    lc_d = nc.dram_tensor("log_count_scratch", (N, N), F32).ap()
    h1T_d = nc.dram_tensor("hidden_T_scratch", (H, C, N), F32).ap()

    ctx = ExitStack()
    with ctx:
        def sb(name, shape, dt=F32, where=ctx):
            return where.enter_context(nc.sbuf_tensor(name, shape, dt))

        def sem(name):
            return ctx.enter_context(nc.semaphore(name))

        ident = sb("ident", [128, 128])
        zeros16 = sb("zeros16", [NP, 128], F16)
        att1 = sb("att1", [C, 2, H])
        att2 = sb("att2", [128, 2, KD])
        watt1 = sb("watt1", [128, KD, 2 * H])
        watt2 = sb("watt2", [128, KC, 2])
        nad1 = sb("nad1", [NP, H, NT])
        nad2 = sb("nad2", [NP, NT])
        b1_sb = sb("b1_sb", [C, H])
        b2_sb = sb("b2_sb", [NP, D])
        fc1_sb = sb("fc1_sb", [128, KD, FH])
        fc1b_sb = sb("fc1b_sb", [128, KF])
        fc2_sb = sb("fc2_sb", [128, KF, D])
        fc2b_sb = sb("fc2b_sb", [NP, D])
        tiny = sb("tiny", [NP, 1])
        powers = sb("powers", [NP, 4])
        spans = sb("spans", [1, 3 * NT], I32)

        w_ctx = ExitStack()
        w1n_sb = sb("w1n_sb", [C, H, D], F32, w_ctx)
        w_ctx.close()
        w_ctx = ExitStack()
        w2n_sb = sb("w2n_sb", [128, KD, HC], F32, w_ctx)
        w_ctx.close()
        w_ctx = ExitStack()
        atom_w = [sb(f"atom_w{i}", [128, KD * FH], F32, w_ctx) for i in range(2)]
        w_ctx.close()
        w2_sb = sb("w2_sb", [128, KC, D + 1])

        two_ctx = ExitStack()
        h2 = sb("h2", [NP, NT, D], F32, two_ctx)
        PT5 = sb("PT5", [NP, NT, GW], F32, two_ctx)
        two_ctx.close()
        LC = sb("LC", [NP, NT, N])

        p1 = ExitStack()
        w1_sb = sb("w1_sb", [128, KD, HC], F32, p1)
        xT = [sb(f"xT{p}", [128, KD, NP], F32, p1) for p in range(2)]
        h1st = [sb(f"h1st{p}", [NP, HC], F32, p1) for p in range(2)]
        xin = [sb(f"xin{p}", [NP, D], F32, p1) for p in range(2)]
        xn = [sb(f"xn{p}", [NP, D], F32, p1) for p in range(2)]
        rows1 = sb("rows1", [H, 2, N], F32, p1)
        iota16 = sb("iota16", [CE, N], F16, p1)
        srci = sb("srci", [CE, NCH], I32, p1)
        dsti = sb("dsti", [CE, NCH], I32, p1)
        srcf = sb("srcf", [CE, NCH + 2], F32, p1)
        dstf = sb("dstf", [CE, NCH + 2], F32, p1)
        dsr = sb("dsr", [NS, 2 * CE], I32, p1)
        ohs = [sb(f"ohs{a}", [CE, N], F16, p1) for a in range(RING)]
        ohd = [sb(f"ohd{a}", [CE, NP], F16, p1) for a in range(RING)]
        stats = [sb(f"stats{p}", [NP, 2, 6], F32, p1) for p in range(2)]
        mv = [sb(f"mv{p}", [NP, 2], F32, p1) for p in range(2)]
        var = [sb(f"var{p}", [NP, 1], F32, p1) for p in range(2)]
        rstd = [sb(f"rstd{p}", [NP, 1], F32, p1) for p in range(2)]
        cmin = sb("cmin", [NS, 1], F32, p1)
        cmax = sb("cmax", [NS, 1], F32, p1)
        tlo = sb("tlo", [NS, NT], F32, p1)
        cidx = sb("cidx", [NS, 2], F32, p1)
        a1 = sb("a1", [NS, NT], F32, p1)
        a2 = sb("a2", [NS, NT], F32, p1)
        a3 = sb("a3", [NS, NT], F32, p1)
        vv = sb("vv", [NS, 2 * NT], F32, p1)
        vr = sb("vr", [NS, 2 * NT], F32, p1)
        sp0 = sb("sp0", [1, 3 * NT], F32, p1)
        hi0 = sb("hi0", [1, NT], F32, p1)
        p1.close()

        p3 = ExitStack()
        PT = [sb(f"PT{s}", [NP, NT, GW], F32, p3) for s in range(2)]
        h1Ts = [sb(f"h1Ts{q}", [C, N], F32, p3) for q in range(2)]
        rdb = [sb(f"rdb{i}", [C, GW], F32, p3) for i in range(2)]
        tmp = [sb(f"tmp{i}", [C, GW], F32, p3) for i in range(2)]
        pad = sb("pad", [128, 1024], F32, p3)
        h1s = [sb(f"h1s{q}", [NP, NT, C], F32, p3) for q in range(2)]
        L = [sb(f"L{r}", [NP, N], F32, p3) for r in range(4)]
        asb = [sb(f"asb{q}", [NP, 2, N], F32, p3) for q in range(2)]
        nadh = [sb(f"nadh{q}", [NP, NT], F32, p3) for q in range(2)]
        b1h = [sb(f"b1h{q}", [C, 1], F32, p3) for q in range(2)]
        mx = [sb(f"mx{q}", [NP, NT], F32, p3) for q in range(2)]
        nm = [sb(f"nm{q}", [NP, NT], F32, p3) for q in range(2)]
        den = [sb(f"den{q}", [NP, NT], F32, p3) for q in range(2)]
        dn = [sb(f"dn{q}", [NP, NT], F32, p3) for q in range(2)]
        rden = [sb(f"rden{q}", [NP, NT], F32, p3) for q in range(2)]
        p3.close()

        p4 = ExitStack()
        L5 = [sb(f"L5_{j}", [NP, N], F32, p4) for j in range(2)]
        LCt = [sb(f"LCt{j}", [NP, N], F32, p4) for j in range(2)]
        asb2 = sb("asb2", [NP, 2, N], F32, p4)
        rows2 = sb("rows2", [1, 2, N], F32, p4)
        h1Tt = [sb(f"h1Tt{p}", [C, H, NP], F32, p4) for p in range(2)]
        x5 = [sb(f"x5_{j}", [NP, D], F32, p4) for j in range(2)]
        x2 = [sb(f"x2_{j}", [NP, D], F32, p4) for j in range(2)]
        y5 = [sb(f"y5_{j}", [NP, D], F32, p4) for j in range(2)]
        x2f = [sb(f"x2f{j}", [NP, D], F32, p4) for j in range(2)]
        ost = [sb(f"ost{j}", [NP, D], F32, p4) for j in range(2)]
        yT = sb("yT", [128, KD, 2, NP], F32, p4)
        gT = sb("gT", [128, KF, GW], F32, p4)
        mx5 = sb("mx5", [NP, 2], F32, p4)
        nm5 = sb("nm5", [NP, 2], F32, p4)
        den5 = sb("den5", [NP, 2], F32, p4)
        dn5 = sb("dn5", [NP, 2], F32, p4)
        rden5 = sb("rden5", [NP, 2], F32, p4)
        stats5 = [sb(f"stats5_{j}", [NP, 2, 6], F32, p4) for j in range(2)]
        mv5 = [sb(f"mv5_{j}", [NP, 2], F32, p4) for j in range(2)]
        var5 = [sb(f"var5_{j}", [NP, 1], F32, p4) for j in range(2)]
        rstd5 = [sb(f"rstd5_{j}", [NP, 1], F32, p4) for j in range(2)]
        atom_w.append(sb("atom_w2", [128, KD * FH], F32, p4))
        atom_b = sb("atom_b", [128, NATOM * KF], F32, p4)
        hid = sb("hid", [128, NATOM * KF, NCLS], F32, p4)
        pick = sb("pick", [128, NATOM, KF, NCLS], F32, p4)
        p4.close()
        p6 = ExitStack()
        gp = sb("gp", [NCLS, 2, D], F32, p6)
        bo = sb("bo", [NCLS, 2, D], F32, p6)
        scr = sb("scr", [NCLS, D], F32, p6)
        cw = sb("cw", [NCLS, 2, D], F32, p6)
        fin = sb("fin", [NCLS, D], F32, p6)
        bal = sb("bal", [NCLS, 2], F32, p6)
        sq = sb("sq", [NCLS, 3], F32, p6)
        nr = sb("nr", [NCLS, 3], F32, p6)
        sr = sb("sr", [NCLS, 3], F32, p6)
        dots = sb("dots", [NCLS, 2], F32, p6)
        lg = [sb(f"lg{i}", [NCLS, 2], F32, p6) for i in range(4)]
        g1 = [sb(f"g1_{i}", [NCLS, 1], F32, p6) for i in range(6)]
        p6.close()

        bank = [ctx.enter_context(nc.psum_tensor(f"bank{b}", [128, 512], F32)) for b in range(8)]

        consts_made = sem("consts_made")
        att_in, w1n_in, w1_in, w2n_in, w2_in = (sem(n) for n in ("att_in", "w1n_in", "w1_in", "w2n_in", "w2_in"))
        ffn_in, bias_in, edges_in = sem("ffn_in"), sem("bias_in"), sem("edges_in")
        wattp, watt_done = sem("wattp"), sem("watt_done")
        x_in = [sem(f"x_in{p}") for p in range(2)]
        stat_step, rstd_ready, xn_ready, xt_full, xT_ready = (
            sem(n) for n in ("stat_step", "rstd_ready", "xn_ready", "xt_full", "xT_ready"))
        logit_full, logit_done, h1_full, h1_out = (sem(n) for n in ("logit_full", "logit_done", "h1_full", "h1_out"))
        h1_stored = [sem(f"h1_stored{p}") for p in range(2)]
        rows_stored = sem("rows_stored")
        span_step, span_max, spans_ready = sem("span_step"), sem("span_max"), sem("spans_ready")
        oh_ready = [sem(f"oh_ready{a}") for a in range(RING)]
        oh_used = [sem(f"oh_used{a}") for a in range(RING)]
        cnt_full, ln_done, lc_done, lc_stored = (sem(n) for n in ("cnt_full", "ln_done", "lc_done", "lc_stored"))
        head_in = [sem(f"head_in{q}") for q in range(2)]
        asb_in = [sem(f"asb_in{q}") for q in range(2)]
        nadh_done, stt_done, max_done, nm_ready = (sem(n) for n in ("nadh_done", "stt_done", "max_done", "nm_ready"))
        exp_done, tb_full, tb_evac, agg_done = (sem(n) for n in ("exp_done", "tb_full", "tb_evac", "agg_done"))
        dn_done, rden_ready, rdb_full, rdb_ready = (sem(n) for n in ("dn_done", "rden_ready", "rdb_full", "rdb_ready"))
        mul_done, b1h_done, relu_done = sem("mul_done"), sem("b1h_done"), sem("relu_done")
        h1T_stored = [sem(f"h1T_stored{q}") for q in range(2)]
        tile_in = [sem(f"tile_in{p}") for p in range(2)]
        h2_full = [sem(f"h2_full{p}") for p in range(2)]
        h2a_done = [sem(f"h2a_done{p}") for p in range(2)]
        h2b_done = [sem(f"h2b_done{p}") for p in range(2)]
        rows2_stored, asb2_in = sem("rows2_stored"), sem("asb2_in")
        lct_in = [sem(f"lct_in{j}") for j in range(2)]
        stt5, max5, nm5_ready, exp5 = sem("stt5"), sem("max5"), sem("nm5_ready"), sem("exp5")
        t5_full, t5_evac, y_full, y_evac = sem("t5_full"), sem("t5_evac"), sem("y_full"), sem("y_evac")
        dn5_done, rden5_done, agg5 = sem("dn5_done"), sem("rden5_done"), sem("agg5")
        x5_in = [sem(f"x5_in{j}") for j in range(2)]
        xb_done = [sem(f"xb_done{j}") for j in range(2)]
        x2_done = [sem(f"x2_done{j}") for j in range(2)]
        ln_step, y_ready = sem("ln_step"), sem("y_ready")
        x2f_done = [sem(f"x2f_done{j}") for j in range(2)]
        hid_full, gelu_done, ffn_full = sem("hid_full"), sem("gelu_done"), sem("ffn_full")
        out_done = [sem(f"out_done{j}") for j in range(2)]
        out_stored = [sem(f"out_stored{j}") for j in range(2)]
        atom_in_sem = [sem(f"atom_in_sem{i}") for i in range(3)]
        atom_used, cls_in, hid_done = sem("atom_used"), sem("cls_in"), sem("hid_done")
        pick_zero, pick_done, gate_step, cls_done, cls_stored = (
            sem(n) for n in ("pick_zero", "pick_done", "gate_step", "cls_done", "cls_stored"))
        gate_exp, gate_root = sem("gate_exp"), sem("gate_root")
        powers_set, rstd5_ready = sem("powers_set"), sem("rstd5_ready")

        block = ctx.enter_context(nc.Block())

        @block.sync
        def _(sp):
            def load_x(p, t):
                sp.dma_start(xin[p][:, :], x[ds(t * NP, NP), :]).then_inc(x_in[p], 16)

            def store_h1(p, i):
                sp.wait_ge(h1_out, 2 * i + (p + 1))
                sp.dma_start(h1_d[ds((2 * i + p) * NP, NP), :], h1st[p][:, :]).then_inc(h1_stored[p], 16)

            def store_lc(p, i):
                sp.wait_ge(lc_done, 2 * i + (p + 1))
                sp.dma_start(lc_d[ds((2 * i + p) * NP, NP), :], LC[:, ds(2 * i + p, 1), :]
                             .rearrange("p t n -> p (t n)")).then_inc(lc_stored, 16)

            sp.dma_start(dsr[:, :], dst_rows).then_inc(edges_in, 16)
            sp.dma_start(dsti[:, :], dst_cols).then_inc(edges_in, 16)
            sp.dma_start(srci[:, :], src_cols).then_inc(edges_in, 16)
            load_x(0, 0)
            load_x(1, 1)
            sp.dma_start(att1[:, 0, :], as1T).then_inc(att_in, 16)
            sp.dma_start(att1[:, 1, :], ad1T).then_inc(att_in, 16)
            sp.dma_start(att2[:, 0, :], as2T).then_inc(att_in, 16)
            sp.dma_start(att2[:, 1, :], ad2T).then_inc(att_in, 16)
            for p in range(2):
                store_lc(p, 0)
            sp.wait_ge(wattp, 1)
            sp.dma_start(w2n_sb[:, :, :], W2.rearrange("(k p) n -> p k n", p=128)).then_inc(w2n_in, 16)
            with sp.Fori(0, NG - 1) as i:
                for p in range(2):
                    sp.wait_ge(xn_ready, 2 * i + (p + 1))
                    load_x(p, 2 * i + p + 2)
                    store_lc(p, i + 1)
                    store_h1(p, i)
            sp.wait_ge(logit_done, NT)
            sp.dma_start(row_d, rows1[:, :, :]).then_inc(rows_stored, 16)

            def load_features(q, h):
                sp.dma_start(h1s[q][:, :, :], h1_d[:, ds(h * C, C)].rearrange("(s p) c -> p s c", p=NP)
                             ).then_inc(head_in[q], 16)

            def load_logits(q, h):
                row = row_d[ds(h, 1), :, :].rearrange("a b n -> a (b n)")
                sp.dma_start(asb[q][:, :, :].rearrange("p b n -> p (b n)"), row.to_broadcast([NP, 2 * N])
                             ).then_inc(asb_in[q], 16)

            def store_head(q, hh):
                sp.wait_ge(relu_done, NG * (2 * hh + q) + NG)
                sp.dma_start(h1T_d[ds(2 * hh + q, 1), :, :].rearrange("a c n -> (a c) n"), h1Ts[q][:, :]
                             ).then_inc(h1T_stored[q], 16)

            sp.wait_ge(rows_stored, 16)
            sp.wait_ge(ln_done, NT)
            for q in range(2):
                load_logits(q, q)
            sp.wait_ge(wattp, 2)
            sp.dma_start(w2_sb[:, :, 0:D], W2T.rearrange("(k p) n -> p k n", p=128)).then_inc(w2_in, 16)
            for p in range(2):
                store_h1(p, NG - 1)
            for p in range(2):
                sp.wait_ge(h1_stored[p], 16 * NG)
            for q in range(2):
                load_features(q, q)
            with sp.Fori(0, H // 2 - 1) as hh:
                for q in range(2):
                    sp.wait_ge(stt_done, NT * (2 * hh + q) + NT)
                    load_logits(q, 2 * hh + q + 2)
                    sp.wait_ge(agg_done, NG * (2 * hh + q) + NG)
                    load_features(q, 2 * hh + q + 2)
                    store_head(q, hh)
            for q in range(2):
                store_head(q, H // 2 - 1)

            for q in range(2):
                sp.wait_ge(h1T_stored[q], 16 * (H // 2))
            sp.wait_ge(relu_done, NG * H)
            def load_tile(p, t):
                sp.dma_start(h1Tt[p][:, :, :], h1T_d[:, :, ds(t * NP, NP)].rearrange("h c n -> c h n")
                             ).then_inc(tile_in[p], 16)
            sp.wait_ge(agg_done, NG * H)
            sp.wait_ge(mul_done, NG * H)
            sp.wait_ge(lc_stored, 16 * NT)
            load_tile(0, 0)
            load_tile(1, 1)
            for j in range(2):
                sp.dma_start(LCt[j][:, :], lc_d[(NT - 1 - j) * NP:(NT - j) * NP, :]).then_inc(lct_in[j], 16)
            with sp.Fori(0, NG - 1) as i:
                for p in range(2):
                    sp.wait_ge(h2_full[p], i + 1)
                    load_tile(p, 2 * i + p + 2)
            for p in range(2):
                sp.wait_ge(h2b_done[p], NG)
            sp.dma_start(row2_d, rows2[:, :, :]).then_inc(rows2_stored, 16)
            sp.wait_ge(rows2_stored, 16)
            sp.dma_start(asb2[:, :, :].rearrange("p b n -> p (b n)"),
                         row2_d.rearrange("a b n -> a (b n)").to_broadcast([NP, 2 * N])).then_inc(asb2_in, 16)

            def lc_load(i):
                for j in range(2):
                    sp.wait_ge(max5, 2 * i + j - 1)
                    alone(sp)
                    sp.dma_start(LCt[j][:, :], lc_d[ds((NT - 1 - j) * NP - i * GW, NP), :]).then_inc(lct_in[j], 16)

            def out_store(i):
                for j in range(2):
                    sp.wait_ge(out_done[j], i + 1)
                    alone(sp)
                    sp.dma_start(out[ds((NT - 1 - j) * NP - i * GW, NP), :], ost[j][:, :]
                                 ).then_inc(out_stored[j], 16)

            for i in range(1, 3):
                lc_load(i)
            with sp.Fori(3, NG) as i:
                lc_load(i)
                out_store(i + -3)
            for i in range(NG - 3, NG):
                out_store(i)
            for j in range(2):
                sp.wait_ge(out_stored[j], 16 * NG)
            sp.wait_ge(cls_done, 1)
            sp.dma_start(out[0:NCLS, :], fin[:, :]).then_inc(cls_stored, 16)
            sp.wait_ge(cls_stored, 16)

        @block.gpsimd
        def _(pool):
            pool.memset(ident[:, :], 0.0).then_inc(consts_made, 1)
            pool.wait_ge(consts_made, 1)
            pool.affine_select(out=ident[:, :], in_=ident[:, :], compare_op=ALU.not_equal, fill=1.0,
                               base=0, pattern=[[-1, 128]], channel_multiplier=1).then_inc(consts_made, 1)
            pool.memset(zeros16[:, :], 0.0).then_inc(consts_made, 1)
            pool.memset(tiny[:, :], 2.0 ** -60).then_inc(consts_made, 1)
            pool.iota(iota16[:, :], pattern=[[1, N]], base=0, channel_multiplier=0,
                      allow_small_or_imprecise_dtypes=True).then_inc(consts_made, 1)
            pool.iota(tlo[:, :], pattern=[[NP, NT]], base=0, channel_multiplier=0,
                      allow_small_or_imprecise_dtypes=True).then_inc(consts_made, 1)
            pool.iota(cidx[:, 0:1], pattern=[[0, 1]], base=NS, channel_multiplier=-1,
                      allow_small_or_imprecise_dtypes=True).then_inc(consts_made, 1)
            pool.iota(cidx[:, 1:2], pattern=[[0, 1]], base=1, channel_multiplier=1,
                      allow_small_or_imprecise_dtypes=True).then_inc(consts_made, 1)
            pool.memset(powers[:, 0:1], -0.5).then_inc(powers_set, 1)
            pool.memset(powers[:, 1:4], 0.5).then_inc(powers_set, 1)

            def rstd_of(p, i):
                pool.wait_ge(stat_step, 3 * (2 * i + p) + 3)
                pool.tensor_tensor(rstd[p][:, :], var[p][:, :], powers[:, 0:1], ALU.pow).then_inc(rstd_ready, 1)

            pool.wait_ge(span_step, 8)
            pool.partition_all_reduce(vr[:, :], vv[:, :], NS, RMAX).then_inc(span_max, 1)
            pool.wait_ge(powers_set, 2)
            rstd_of(0, 0)
            with pool.Fori(0, NG - 1) as i:
                rstd_of(1, i)
                rstd_of(0, i + 1)
            rstd_of(1, NG - 1)

            def relu(hh, k, first=False, last=False):
                lag = 3
                if (first and k < lag) or (last and k - lag >= 2 * NG):
                    return
                q, g, n, h = at(hh, k, lag)
                if g == 0:
                    pool.tensor_copy(b1h[q][:, :], b1_sb[:, ds(h, 1)]).then_inc(b1h_done, 1)
                    pool.wait_ge(b1h_done, h + 1)
                    pool.wait_ge(h1T_stored[q], hh * 16)
                pool.wait_ge(mul_done, n + 1)
                alone(pool)
                pool.tensor_scalar(h1Ts[q][:, g * GW:(g + 1) * GW], tmp[(k - lag) % 2][:, :], b1h[q][:, 0:1],
                                   0.0, ALU.add, ALU.max).then_inc(relu_done, 1)

            pool.wait_ge(bias_in, 16 * 4)
            for p in range(2):
                pool.wait_ge(h1_stored[p], 16 * NG)
            for k in range(2 * NG):
                relu(0, k, first=True)
            with pool.Fori(1, H // 2) as hh:
                for k in range(2 * NG):
                    relu(hh, k)
            for k in range(2 * NG, 2 * NG + 3):
                relu(H // 2 - 1, k, last=True)

            def load_x5(i, j):
                pool.dma_start(x5[j][:, :], x[ds((NT - 1 - j) * NP - i * GW, NP), :]).then_inc(x5_in[j], 16)

            def add_biases(i, last=False):
                for j in range(2):
                    pool.wait_ge(x5_in[j], 16 * (i + 1))
                    pool.tensor_tensor(x5[j][:, :], x5[j][:, :], b2_sb[:, :], ALU.add).then_inc(xb_done[j], 1)
                for j in range(2):
                    pool.wait_ge(x2_done[j], i + 1)
                    alone(pool)
                    if not last:
                        load_x5(i + 1, j)
                    pool.wait_ge(ln_step, 3 * (2 * i + j) + 3)
                    pool.tensor_tensor(rstd5[j][:, :], var5[j][:, :], powers[:, 0:1], ALU.pow).then_inc(rstd5_ready, 1)
                    freed(pool, out_done[j], i)
                    pool.tensor_tensor(x2f[j][:, :], x2[j][:, :], fc2b_sb[:, :], ALU.add).then_inc(x2f_done[j], 1)

            pool.wait_ge(h1T_stored[0], 16 * (H // 2))
            pool.wait_ge(h1T_stored[1], 16 * (H // 2))
            pool.wait_ge(agg_done, NG * H)
            for j in range(2):
                load_x5(0, j)
            rounds(pool, NG - 1, add_biases)
            add_biases(NG - 1, last=True)
            pool.memset(pick[:, :, :, :], 0.0).then_inc(pick_zero, 1)
            pool.wait_ge(gate_step, 5)
            pool.tensor_tensor(sr[:, :], sq[:, :], powers[0:NCLS, 1:4], ALU.pow).then_inc(gate_root, 1)

        @block.scalar
        def _(act):
            act.dma_start(w1n_sb[:, :, :], W1.rearrange("(h c) d -> c h d", c=C)).then_inc(w1n_in, 16)
            act.dma_start(w1_sb[:, :, :], W1T.rearrange("(k p) n -> p k n", p=128)).then_inc(w1_in, 16)
            act.dma_start(fc1_sb[:, :, :], fc1T.rearrange("(k p) n -> p k n", p=128)).then_inc(ffn_in, 16)
            act.dma_start(fc2_sb[:, :, :], fc2T.rearrange("(k p) n -> p k n", p=128)).then_inc(ffn_in, 16)
            act.dma_start(b1_sb[:, :], b1c).then_inc(bias_in, 16)
            act.dma_start(fc1b_sb[:, :], fc1b).then_inc(bias_in, 16)
            act.dma_start(b2_sb[:, :], b2.to_broadcast([NP, D])).then_inc(bias_in, 16)
            act.dma_start(fc2b_sb[:, :], fc2b.to_broadcast([NP, D])).then_inc(bias_in, 16)

            def rows_turned(p, i):
                act.wait_ge(xt_full, 2 * i + (p + 1))
                freed(act, h1_full, 2 * i + (p - 1))
                act.copy(xT[p][:, 0:4, :], bank[3][:, 0:4 * NP].rearrange("p (k n) -> p k n", k=4))
                act.copy(xT[p][:, 4:6, :], bank[4][:, 0:2 * NP].rearrange("p (k n) -> p k n", k=2)
                         ).then_inc(xT_ready, 1)

            def log_counts(p, i):
                act.wait_ge(cnt_full, 2 * i + (p + 1))
                for b, (c0, w) in enumerate(BANKS3):
                    last = act.activation(LC[:, ds(2 * i + p, 1), c0:c0 + w].rearrange("p t n -> p (t n)"),
                                          bank[b][0:NP, 0:w], ACT.Ln, bias=tiny[:, 0:1], scale=2.0)
                last.then_inc(ln_done, 1)

            def features_out(p, i):
                act.wait_ge(h1_full, 2 * i + (p + 1))
                freed(act, h1_stored[p], 16 * i)
                for half in range(2):
                    c = act.copy(h1st[p][:, half * 512:(half + 1) * 512], bank[6 + half][0:NP, :])
                c.then_inc(h1_out, 1)

            def tile_out(i):
                for p in range(2):
                    rows_turned(p, i)
                    log_counts(p, i + 1)
                    features_out(p, i)

            act.wait_ge(consts_made, 4)
            for p in range(2):
                log_counts(p, 0)
            rounds(act, NG - 1, tile_out)
            for p in range(2):
                rows_turned(p, NG - 1)
            for p in range(2):
                features_out(p, NG - 1)

            def exp(hh, k, first=False, last=False):
                if last:
                    return
                q, g, n, h = at(hh, k, 0)
                act.wait_ge(nm_ready, n + 1)
                for j in range(2):
                    r, t = (2 * k + j) % 4, 2 * g + j
                    e = act.activation(L[r][:, :], L[r][:, :], ACT.Exp, bias=nm[q][:, t:t + 1], scale=1.0,
                                       accum_out=den[q][:, t:t + 1])
                e.then_inc(exp_done, 1)

            def evac(hh, k, first=False, last=False):
                lag = 1
                if (first and k < lag) or (last and k - lag >= 2 * NG):
                    return
                q, g, n, h = at(hh, k, lag)
                for b in range(5):
                    act.wait_ge(tb_full, NG * n + b + 1)
                    if b == 0 and not (first and k - lag < 2):
                        act.wait_ge(agg_done, n + -1)
                    act.copy(PT[(k - lag) % 2][:, 2 * b:2 * b + 2, :],
                             bank[TBANK[b]][0:NP, 0:2 * GW].rearrange("p (s n) -> p s n", s=2)
                             ).then_inc(tb_evac, 1)

            def rdb_copy(hh, k, first=False, last=False):
                lag = 2
                if (first and k < lag) or (last and k - lag >= 2 * NG):
                    return
                q, g, n, h = at(hh, k, lag)
                act.wait_ge(rdb_full, n + 1)
                if not (first and k - lag < 2):
                    act.wait_ge(mul_done, n + -1)
                i = (k - lag) % 2
                act.copy(rdb[i][:, :], bank[4 + i][:, 0:GW]).then_inc(rdb_ready, 1)

            def step(hh, k, **at_end):
                evac(hh, k, **at_end)
                rdb_copy(hh, k, **at_end)
                exp(hh, k, **at_end)

            for k in range(2 * NG):
                step(0, k, first=True)
            with act.Fori(1, H // 2) as hh:
                for k in range(2 * NG):
                    step(hh, k)
            for k in range(2 * NG, 2 * NG + 2):
                step(H // 2 - 1, k, last=True)

            act.wait_ge(stt_done, NT * H)
            act.wait_ge(max_done, NT * H)
            act.wait_ge(lc_stored, 16 * NT)
            with act.Fori(0, NG) as i:
                for p in range(2):
                    act.wait_ge(h2_full[p], i + 1)
                    act.copy(h2[:, ds(2 * i + p, 1), 0:HALF].rearrange("p t n -> p (t n)"),
                             bank[2 * p][0:NP, 0:HALF]).then_inc(h2a_done[p], 1)

            atoms = [(atom_inT, a) for a in range(NATOM)] + [(atom_outT, a) for a in range(NATOM)]

            def load_atom(s):
                which, a = atoms[s]
                if s >= 3:
                    act.wait_ge(atom_used, s - 2)
                act.dma_start(atom_w[s % 3][:, :].rearrange("p (k n) -> p k n", k=KD if s < NATOM else KF),
                              which[a].rearrange("(k p) n -> p k n", p=128)).then_inc(atom_in_sem[s % 3], 16)

            act.wait_ge(relu_done, NG * H)
            for q in range(2):
                act.wait_ge(h1T_stored[q], 16 * (H // 2))
            act.wait_ge(h2_full[1], NG)
            act.dma_start(atom_b[:, :], atom_inb).then_inc(cls_in, 16)
            for s in range(3):
                load_atom(s)

            def exp_5(i):
                act.wait_ge(nm5_ready, i + 1)
                for j in range(2):
                    e = act.activation(L5[j][:, :], L5[j][:, :], ACT.Exp, bias=nm5[:, j:j + 1], scale=1.0,
                                       accum_out=den5[:, j:j + 1])
                e.then_inc(exp5, 1)

            def evac_5(i, first=False):
                for b in range(5):
                    act.wait_ge(t5_full, 5 * i + b + 1)
                    if b == 0 and not first:
                        act.wait_ge(agg5, 2 * i)
                    act.copy(PT5[:, 2 * b:2 * b + 2, :],
                             bank[b % 2][0:NP, 0:2 * GW].rearrange("p (s n) -> p s n", s=2)).then_inc(t5_evac, 1)

            def ffn_5(i):
                for c in range(3):
                    act.wait_ge(y_full, 3 * i + c + 1)
                    act.copy(yT[:, 2 * c:2 * c + 2, :, :], bank[(c + 1) % 2][:, 0:2 * GW]
                             .rearrange("p (k j n) -> p k j n", k=2, j=2)).then_inc(y_evac, 1)
                act.wait_ge(hid_full, i + 1)
                for m in range(KF):
                    g = act.activation(gT[:, m, :], bank[6 + m // 2][:, (m % 2) * GW:(m % 2 + 1) * GW], ACT.Gelu,
                                       bias=fc1b_sb[:, m:m + 1], scale=1.0)
                g.then_inc(gelu_done, 1)

            exp_5(0)
            evac_5(0, first=True)
            with act.Fori(1, NG) as i:
                exp_5(i)
                evac_5(i)
                ffn_5(i + -1)
            ffn_5(NG - 1)

            act.wait_ge(t5_full, NG * NG)
            act.wait_ge(max5, NT)
            for r, rows in enumerate(([r for _, r in ATOM_SRC], [l for l, _ in ATOM_SRC])):
                for n in range(0, NCLS):
                    act.dma_start(bo[n:n + 1, r, :], atom_outb[rows[n]:rows[n] + 1, :]).then_inc(cls_in, 16)
            act.dma_start(gp[:, :, :], gate_pair).then_inc(cls_in, 16)
            act.dma_start(bal[:, :], balance).then_inc(cls_in, 16)
            for s in range(3, NATOM):
                load_atom(s)
            for a in range(NATOM):
                act.wait_ge(atom_used, a + 1)
                if a == 0:
                    act.wait_ge(cls_in, 16)
                for m in range(KF):
                    g = act.activation(hid[:, a * KF + m, :], bank[2 + a % 2][:, m * 8:m * 8 + NCLS], ACT.Gelu,
                                       bias=atom_b[:, a * KF + m:a * KF + m + 1], scale=1.0)
                g.then_inc(hid_done, 1)
                if a < 3:
                    load_atom(NATOM + a)
            act.wait_ge(gate_step, 12)
            act.activation(lg[2][:, :], lg[1][:, :], ACT.Exp).then_inc(gate_exp, 1)
            load_atom(NATOM + 3)
            load_atom(NATOM + 4)

        @block.tensor
        def _(pe):
            def clear(begin):
                for b, (c0, w) in enumerate(BANKS3):
                    mm = pe.matmul(bank[b][0:NP, 0:w], zeros16[:, 0:NP], iota16[:, c0:c0 + w],
                                   start=begin, stop=not begin, skip_group_check=True)
                return mm

            def count_edges(p, i):
                count = pe.value_load(spans[0:1, ds(2 * i + (NT + p), 1)], min_val=1, max_val=NQ)
                before = pe.value_load(spans[0:1, ds(2 * i + (2 * NT + p), 1)], min_val=0, max_val=NQ * NT)
                freed(pe, ln_done, 2 * i + p)
                clear(True)
                with pe.Fori(0, count) as c:
                    for a in range(RING):
                        pe.wait_ge(oh_ready[a], before + c + 1)
                        for b, (c0, w) in enumerate(BANKS3):
                            mm = pe.matmul(bank[b][0:NP, 0:w], ohd[a][:, :], ohs[a][:, c0:c0 + w],
                                           start=False, stop=False, skip_group_check=True)
                        mm.then_inc(oh_used[a], 1)
                clear(False).then_inc(cnt_full, 1)

            pe.wait_ge(consts_made, 5)
            pe.wait_ge(spans_ready, 1)
            count_edges(0, 0)
            count_edges(1, 0)

            pe.wait_ge(att_in, 16 * 4)
            pe.wait_ge(w1n_in, 16)
            for h in range(H):
                for k in range(KD):
                    mm = pe.matmul(bank[6][:, 2 * H * k + h:2 * H * (k + 1):H], w1n_sb[:, h, k * 128:(k + 1) * 128],
                                   att1[:, :, h], start=True, stop=True)
            mm.then_inc(wattp, 1)
            pe.wait_ge(watt_done, 1)
            pe.wait_ge(w1_in, 16)

            def turn(p, i):
                pe.wait_ge(xn_ready, 2 * i + (p + 1))
                freed(pe, xT_ready, 2 * i + p)
                for k in range(KD):
                    b, c = (3, k) if k < 4 else (4, k - 4)
                    mm = pe.transpose(bank[b][:, c * NP:(c + 1) * NP], xn[p][:, k * 128:(k + 1) * 128],
                                      ident[0:NP, 0:NP])
                mm.then_inc(xt_full, 1)

            def logit_products(p, i):
                pe.wait_ge(xT_ready, 2 * i + (p + 1))
                freed(pe, logit_done, 2 * i + p)
                for k in range(KD):
                    pe.matmul(bank[5][0:H, 0:NP], watt1[:, k, 0:H], xT[p][:, k, :],
                              start=(k == 0), stop=(k == KD - 1))
                for k in range(KD):
                    mm = pe.matmul(bank[5][0:NP, 128:128 + H], xT[p][:, k, :], watt1[:, k, H:2 * H],
                                   start=(k == 0), stop=(k == KD - 1))
                mm.then_inc(logit_full, 1)

            def products(p, i):
                freed(pe, h1_out, 2 * i + p)
                for half in range(2):
                    for k in range(KD):
                        mm = pe.matmul(bank[6 + half][0:NP, :], xT[p][:, k, :],
                                       w1_sb[:, k, half * 512:(half + 1) * 512],
                                       start=(k == 0), stop=(k == KD - 1))
                mm.then_inc(h1_full, 1)

            def tile_products(i):
                for p in range(2):
                    turn(p, i)
                    count_edges(p, i + 1)
                    logit_products(p, i)
                    products(p, i)

            rounds(pe, NG - 1, tile_products)
            for p in range(2):
                turn(p, NG - 1)
                logit_products(p, NG - 1)
            for p in range(2):
                products(p, NG - 1)

            pe.wait_ge(w2n_in, 16)
            pe.wait_ge(ln_done, NT)
            for c in range(KC):
                for k in range(KD):
                    mm = pe.matmul(bank[0][:, 2 * c:2 * c + 2], w2n_sb[:, k, c * 128:(c + 1) * 128],
                                   att2[:, :, k], start=(k == 0), stop=(k == KD - 1))
            mm.then_inc(wattp, 1)

            def turn_bank(hh, k, b, first=False, last=False):
                lag = 1
                if (first and k < lag) or (last and k - lag >= 2 * NG):
                    return
                q, g, n, h = at(hh, k, lag)
                if b == 0:
                    pe.wait_ge(exp_done, n + 1)
                if not (first and k == lag and b < 4):
                    pe.wait_ge(tb_evac, NG * n + TFREE[b])
                for s in range(2):
                    for j in range(2):
                        mm = pe.transpose(bank[TBANK[b]][0:NP, (2 * s + j) * NP:(2 * s + j + 1) * NP],
                                          L[(2 * (k - lag) + j) % 4][:, (2 * b + s) * NP:(2 * b + s + 1) * NP],
                                          ident[0:NP, 0:NP])
                mm.then_inc(tb_full, 1)

            def aggregate(hh, k, b, first=False, last=False):
                lag = 2
                if (first and k < lag) or (last and k - lag >= 2 * NG):
                    return
                q, g, n, h = at(hh, k, lag)
                if b == 0:
                    pe.wait_ge(tb_evac, NG * n + NG)
                    if g == 0:
                        pe.wait_ge(head_in[q], 16 * (hh + 1))
                    if not (first and k - lag < 2):
                        pe.wait_ge(mul_done, n + -1)
                for s in range(2 * b, 2 * b + 2):
                    mm = pe.matmul(bank[2 + (k - lag) % 2][:, 0:GW], h1s[q][:, s, :], PT[(k - lag) % 2][:, s, :],
                                   start=(s == 0), stop=(s == NT - 1))
                if b == 4:
                    mm.then_inc(agg_done, 1)

            def spread(hh, k, first=False, last=False):
                lag = 2
                if (first and k < lag) or (last and k - lag >= 2 * NG):
                    return
                q, g, n, h = at(hh, k, lag)
                pe.wait_ge(rden_ready, n + 1)
                if not (first and k - lag < 2):
                    pe.wait_ge(rdb_ready, n + -1)
                for j in range(2):
                    t = 2 * g + j
                    mm = pe.matmul(bank[4 + (k - lag) % 2][:, j * NP:(j + 1) * NP],
                                   rden[q][:, t:t + 1].to_broadcast([NP, C]), ident[0:NP, 0:NP],
                                   start=True, stop=True)
                mm.then_inc(rdb_full, 1)

            def step(hh, k, **at_end):
                for b in range(4):
                    turn_bank(hh, k, b, **at_end)
                spread(hh, k, **at_end)
                aggregate(hh, k, 0, **at_end)
                turn_bank(hh, k, 4, **at_end)
                for b in range(1, 5):
                    aggregate(hh, k, b, **at_end)

            pe.wait_ge(watt_done, 3)
            pe.wait_ge(h1_out, NT)
            for k in range(2 * NG):
                step(0, k, first=True)
            with pe.Fori(1, H // 2) as hh:
                for k in range(2 * NG):
                    step(hh, k)
            for k in range(2 * NG, 2 * NG + 2):
                step(H // 2 - 1, k, last=True)

            pe.wait_ge(w2_in, 16)
            pe.wait_ge(watt_done, 3)
            pe.wait_ge(mul_done, NG * H)
            pe.wait_ge(rdb_ready, NG * H)
            pe.wait_ge(tb_evac, NG * NG * H)
            def second_features(i):
                for p in range(2):
                    pe.wait_ge(tile_in[p], 16 * (i + 1))
                    freed(pe, h2a_done[p], i)
                    freed(pe, h2b_done[p], i)
                    for k in range(KC):
                        pe.matmul(bank[4 + p][0:1, 0:NP], watt2[:, k, 0:1], h1Tt[p][:, k, :],
                                  start=(k == 0), stop=(k == KC - 1))
                    for b, (c0, w) in enumerate(((0, HALF), (HALF, HALF + 1))):
                        for k in range(KC):
                            mm = pe.matmul(bank[2 * p + b][0:NP, 0:w], h1Tt[p][:, k, :], w2_sb[:, k, c0:c0 + w],
                                           start=(k == 0), stop=(k == KC - 1))
                    mm.then_inc(h2_full[p], 1)

            rounds(pe, NG, second_features)

            for p in range(2):
                pe.wait_ge(h2a_done[p], NG)
                pe.wait_ge(h2b_done[p], NG)

            def turn_5(i, first=0):
                pe.wait_ge(exp5, i + 1)
                for b in range(5):
                    if b >= 2:
                        pe.wait_ge(t5_evac, 5 * i + (b - 1))
                    elif first < 1:
                        pe.wait_ge(t5_evac, 5 * i)
                        if first < 0:
                            pe.wait_ge(y_evac, 3 * i + -3)
                    for s in range(2):
                        for j in range(2):
                            mm = pe.transpose(bank[b % 2][0:NP, (2 * s + j) * NP:(2 * s + j + 1) * NP],
                                              L5[j][:, (2 * b + s) * NP:(2 * b + s + 1) * NP], ident[0:NP, 0:NP])
                    mm.then_inc(t5_full, 1)

            def aggregate_5(i, j):
                if j == 0:
                    pe.wait_ge(t5_evac, 5 * i + 5)
                freed(pe, x2_done[j], i)
                for b in range(2):
                    for s in range(NT):
                        mm = pe.matmul(bank[2 + 2 * j + b][0:NP, 0:HALF], PT5[:, s, j * NP:(j + 1) * NP],
                                       h2[:, s, b * HALF:(b + 1) * HALF], start=(s == 0), stop=(s == NT - 1))
                mm.then_inc(agg5, 1)

            def turn_y(i, first=False):
                pe.wait_ge(y_ready, 2 * i + 2)
                for c in range(3):
                    if c < 2:
                        if not first:
                            pe.wait_ge(t5_evac, 5 * i + (9 + c))
                    else:
                        pe.wait_ge(y_evac, 3 * i + 1)
                    for kk in range(2):
                        for j in range(2):
                            k = 2 * c + kk
                            mm = pe.transpose(bank[(c + 1) % 2][:, (2 * kk + j) * NP:(2 * kk + j + 1) * NP],
                                              y5[j][:, k * 128:(k + 1) * 128], ident[0:NP, 0:NP])
                    mm.then_inc(y_full, 1)

            def ffn_up(i, first=False):
                pe.wait_ge(y_evac, 3 * i + 3)
                freed(pe, out_done[1], i)
                for m in range(KF):
                    for k in range(KD):
                        mm = pe.matmul(bank[6 + m // 2][:, (m % 2) * GW:(m % 2 + 1) * GW],
                                       fc1_sb[:, k, m * 128:(m + 1) * 128],
                                       yT[:, k, :, :].rearrange("p j n -> p (j n)"),
                                       start=(k == 0), stop=(k == KD - 1))
                mm.then_inc(hid_full, 1)

            def ffn_down(i, j):
                if j == 0:
                    pe.wait_ge(gelu_done, i + 1)
                else:
                    pe.wait_ge(out_done[0], i + 1)
                for b in range(2):
                    for m in range(KF):
                        mm = pe.matmul(bank[6 + b][0:NP, 0:HALF], gT[:, m, j * NP:(j + 1) * NP],
                                       fc2_sb[:, m, b * HALF:(b + 1) * HALF], start=(m == 0), stop=(m == KF - 1))
                mm.then_inc(ffn_full, 1)

            pe.wait_ge(ffn_in, 32)
            turn_5(0, first=1)
            aggregate_5(0, 0)
            aggregate_5(0, 1)

            def step_5(i, first):
                turn_5(i, first=first)
                turn_y(i + -1)
                ffn_up(i + -1)
                aggregate_5(i, 0)
                ffn_down(i + -1, 0)
                aggregate_5(i, 1)
                ffn_down(i + -1, 1)

            step_5(1, 0)
            with pe.Fori(2, NG) as i:
                step_5(i, -1)
            turn_y(NG - 1, first=True)
            ffn_up(NG - 1)
            ffn_down(NG - 1, 0)
            ffn_down(NG - 1, 1)

            pe.wait_ge(x2_done[0], NG)
            pe.wait_ge(x2_done[1], NG)
            for a in range(NATOM):
                pe.wait_ge(atom_in_sem[a % 3], 16 * (a // 3 + 1))
                if a >= 2:
                    pe.wait_ge(hid_done, a - 1)
                w = atom_w[a % 3][:, :].rearrange("p (k n) -> p k n", k=KD)
                for m in range(KF):
                    for k in range(KD):
                        mm = pe.matmul(bank[2 + a % 2][:, m * 8:m * 8 + NCLS], w[:, k, m * 128:(m + 1) * 128],
                                       yT[:, k, 1, 0:NCLS], start=(k == 0), stop=(k == KD - 1))
                mm.then_inc(atom_used, 1)
            pe.wait_ge(pick_done, 12)
            pe.wait_ge(out_done[1], NG)
            for a in range(NATOM):
                s = NATOM + a
                pe.wait_ge(atom_in_sem[s % 3], 16 * (s // 3 + 1))
                w = atom_w[s % 3][:, :].rearrange("p (m n) -> p m n", m=KF)
                r = 1 if a < 3 else 0
                for b in range(2):
                    for m in range(KF):
                        mm = pe.matmul(bank[4 + 2 * r + b][0:NCLS, 0:HALF], pick[:, a, m, :],
                                       w[:, m, b * HALF:(b + 1) * HALF], start=(a in (0, 3) and m == 0),
                                       stop=(a in (2, 4) and m == KF - 1))
                mm.then_inc(atom_used, 1)

        @block.vector
        def _(dve):
            dve.wait_ge(edges_in, 48)
            dve.tensor_reduce(cmin[:, :], dsr[:, :], mybir.AxisListType.X, ALU.min).then_inc(span_step, 1)
            dve.tensor_reduce(cmax[:, :], dsr[:, :], mybir.AxisListType.X, ALU.max).then_inc(span_step, 1)
            dve.wait_ge(span_step, 2)
            dve.wait_ge(consts_made, 8)
            dve.tensor_scalar(a1[:, :], tlo[:, :], cmax[:, 0:1], None, ALU.is_le).then_inc(span_step, 1)
            dve.tensor_scalar(a2[:, :], tlo[:, :], float(NP - 1), cmin[:, 0:1], ALU.add, ALU.is_ge
                              ).then_inc(span_step, 1)
            dve.wait_ge(span_step, 4)
            dve.tensor_tensor(a3[:, :], a1[:, :], a2[:, :], ALU.mult).then_inc(span_step, 1)
            dve.wait_ge(span_step, 5)
            dve.tensor_scalar(vv[:, 0:NT], a3[:, :], cidx[:, 0:1], None, ALU.mult).then_inc(span_step, 1)
            dve.tensor_scalar(vv[:, NT:2 * NT], a3[:, :], cidx[:, 1:2], None, ALU.mult).then_inc(span_step, 1)
            dve.memset(srcf[:, NCH:NCH + 2], -1.0)
            dve.memset(dstf[:, NCH:NCH + 2], -1.0)
            dve.tensor_copy(srcf[:, 0:NCH], srci[:, :])
            dve.tensor_copy(dstf[:, 0:NCH], dsti[:, :]).then_inc(span_step, 1)
            for a in range(RING):
                dve.memset(ohd[a][:, :], 0.0).then_inc(oh_used[a], 1)
            dve.wait_ge(span_max, 1)
            dve.tensor_scalar(sp0[:, 0:NT], vr[0:1, 0:NT], -1.0, float(NS), ALU.mult, ALU.add).then_inc(span_step, 1)
            dve.wait_ge(span_step, 9)
            dve.tensor_scalar(sp0[:, 0:NT], sp0[:, 0:NT], float(NS - 1), None, ALU.min).then_inc(span_step, 1)
            dve.wait_ge(span_step, 10)
            dve.tensor_tensor(hi0[:, :], vr[0:1, NT:2 * NT], sp0[:, 0:NT], ALU.subtract).then_inc(span_step, 1)
            dve.wait_ge(span_step, 11)
            dve.tensor_scalar(hi0[:, :], hi0[:, :], 1.0, 0.5, ALU.max, ALU.mult).then_inc(span_step, 1)
            dve.wait_ge(span_step, 12)
            dve.tensor_scalar(hi0[:, :], hi0[:, :], 0.25, None, ALU.add).then_inc(span_step, 1)
            dve.wait_ge(span_step, 13)
            dve.tensor_scalar(hi0[:, :], hi0[:, :], 2.0 ** 23, None, ALU.add).then_inc(span_step, 1)
            dve.wait_ge(span_step, 14)
            dve.tensor_scalar(sp0[:, NT:2 * NT], hi0[:, :], -2.0 ** 23, None, ALU.add).then_inc(span_step, 1)
            dve.memset(sp0[:, 2 * NT:2 * NT + 1], 0.0).then_inc(span_step, 1)
            for t in range(1, NT):
                dve.wait_ge(span_step, 15 + t)
                dve.tensor_tensor(sp0[:, 2 * NT + t:2 * NT + t + 1], sp0[:, 2 * NT + t - 1:2 * NT + t],
                                  sp0[:, NT + t - 1:NT + t], ALU.add).then_inc(span_step, 1)
            dve.wait_ge(span_step, 15 + NT)
            dve.tensor_copy(spans[:, :], sp0[:, :]).then_inc(spans_ready, 1)

            def one_hots(p, i):
                start = dve.value_load(spans[0:1, ds(2 * i + p, 1)], min_val=0, max_val=NS - 1)
                count = dve.value_load(spans[0:1, ds(2 * i + (NT + p), 1)], min_val=1, max_val=NQ)
                before = dve.value_load(spans[0:1, ds(2 * i + (2 * NT + p), 1)], min_val=0, max_val=NQ * NT)
                with dve.Fori(0, count) as c:
                    pair = (start + 2 * c).with_bounds(min_val=0, max_val=NS - 1)
                    for a in range(RING):
                        dve.wait_ge(oh_used[a], before + c + 1)
                        dve.tensor_scalar(ohs[a][:, :], iota16[:, :], srcf[:, ds(2 * pair + a, 1)], None,
                                          ALU.is_equal)
                        dve.tensor_scalar(ohd[a][:, :], iota16[:, ds((2 * i + p) * NP, NP)],
                                          dstf[:, ds(2 * pair + a, 1)], None, ALU.is_equal
                                          ).then_inc(oh_ready[a], 1)

            def mend(p, i):
                dve.wait_ge(ln_done, 2 * i + (p + 1))
                v = LC[:, ds(2 * i + p, 1), :].rearrange("p t n -> p (t n)")
                dve.scalar_tensor_tensor(v, v, 1e30, v, ALU.mult, ALU.min).then_inc(lc_done, 1)

            def normalise(p, i):
                t = 2 * i + p
                dve.wait_ge(x_in[p], 16 * (i + 1))
                for b in range(2):
                    s = dve.bn_stats(stats[p][:, b, :], xin[p][:, b * HALF:(b + 1) * HALF])
                s.then_inc(stat_step, 1)
                dve.wait_ge(stat_step, 3 * t + 1)
                alone(dve)
                dve.bn_aggr(mv[p][:, :], stats[p][:, :, :]).then_inc(stat_step, 1)
                dve.wait_ge(stat_step, 3 * t + 2)
                dve.tensor_scalar(var[p][:, :], mv[p][:, 1:2], LN_EPS, None, ALU.add).then_inc(stat_step, 1)
                dve.wait_ge(rstd_ready, t + 1)
                freed(dve, xt_full, t - 1)
                dve.tensor_scalar(xn[p][:, :], xin[p][:, :], mv[p][:, 0:1], rstd[p][:, 0:1],
                                  ALU.subtract, ALU.mult).then_inc(xn_ready, 1)

            def logits_out(p, i):
                t = 2 * i + p
                dve.wait_ge(logit_full, t + 1)
                dve.tensor_copy(rows1[:, 0, ds(t * NP, NP)], bank[5][0:H, 0:NP])
                dve.tensor_scalar(rows1[:, 1, ds(t * NP, NP)], bank[5][0:H, 0:NP], SLOPE, None, ALU.mult)
                dve.tensor_scalar(nad1[:, :, ds(t, 1)].rearrange("p h t -> p (h t)"), bank[5][0:NP, 128:128 + H],
                                  SLOPE - 1.0, None, ALU.mult).then_inc(logit_done, 1)

            normalise(0, 0)
            for p in range(2):
                one_hots(p, 0)
                mend(p, 0)
            dve.wait_ge(wattp, 1)
            dve.tensor_copy(watt1[:, :, :], bank[6][:, 0:2 * H * KD].rearrange("p (k c) -> p k c", k=KD)
                            ).then_inc(watt_done, 1)

            def features(i):
                for p in range(2):
                    one_hots(p, i + 1)
                    normalise(1 - p, i + p)
                    mend(p, i + 1)
                    logits_out(p, i)

            rounds(dve, NG - 1, features)
            normalise(1, NG - 1)
            for p in range(2):
                logits_out(p, NG - 1)
            dve.wait_ge(wattp, 2)
            dve.tensor_copy(watt2[:, :, :], bank[0][:, 0:2 * KC].rearrange("p (k c) -> p k c", k=KC)
                            ).then_inc(watt_done, 1)
            dve.tensor_copy(w2_sb[:, :, D], bank[0][:, 1:2 * KC:2]).then_inc(watt_done, 1)
            dve.wait_ge(lc_done, NT)
            dve.wait_ge(rows_stored, 16)

            def logits(hh, k, first=False, last=False):
                if last:
                    return
                q, g, n, h = at(hh, k, 0)
                if g == 0:
                    dve.wait_ge(asb_in[q], 16 * (hh + 1))
                    dve.tensor_copy(nadh[q][:, :], nad1[:, ds(h, 1), :].rearrange("p h t -> p (h t)")
                                    ).then_inc(nadh_done, 1)
                    dve.wait_ge(nadh_done, h + 1)
                for j in range(2):
                    r, t = (2 * k + j) % 4, 2 * g + j
                    if not (first and k < 2):
                        dve.wait_ge(tb_full, NG * n + -NG)
                    dve.scalar_tensor_tensor(L[r][:, :], asb[q][:, 1, :], nadh[q][:, t:t + 1], asb[q][:, 0, :],
                                             ALU.add, ALU.max).then_inc(stt_done, 1)
                for j in range(2):
                    r, t = (2 * k + j) % 4, 2 * g + j
                    dve.wait_ge(stt_done, 2 * n + (j + 1))
                    alone(dve)
                    dve.tensor_tensor_reduce(out=L[r][:, :], in0=L[r][:, :], in1=LC[:, t, :], scale=1.0,
                                             scalar=-3e38, op0=ALU.add, op1=ALU.max,
                                             accum_out=mx[q][:, t:t + 1]).then_inc(max_done, 1)
                dve.wait_ge(max_done, 2 * n + 2)
                dve.tensor_scalar(nm[q][:, 2 * g:2 * g + 2], mx[q][:, 2 * g:2 * g + 2], FLOOR, -1.0,
                                  ALU.max, ALU.mult).then_inc(nm_ready, 1)

            def reciprocals(hh, k, first=False, last=False):
                lag = 1
                if (first and k < lag) or (last and k - lag >= 2 * NG):
                    return
                q, g, n, h = at(hh, k, lag)
                dve.wait_ge(exp_done, n + 1)
                dve.tensor_scalar(dn[q][:, 2 * g:2 * g + 2], den[q][:, 2 * g:2 * g + 2], EPS, None, ALU.add
                                  ).then_inc(dn_done, 1)
                dve.wait_ge(dn_done, n + 1)
                dve.reciprocal(rden[q][:, 2 * g:2 * g + 2], dn[q][:, 2 * g:2 * g + 2]).then_inc(rden_ready, 1)

            def multiply(hh, k, first=False, last=False):
                lag = 3
                if (first and k < lag) or (last and k - lag >= 2 * NG):
                    return
                q, g, n, h = at(hh, k, lag)
                dve.wait_ge(agg_done, n + 1)
                dve.wait_ge(rdb_ready, n + 1)
                if not (first and k - lag < 2):
                    dve.wait_ge(relu_done, n + -1)
                i = (k - lag) % 2
                dve.tensor_tensor(tmp[i][:, :], bank[2 + i][:, 0:GW], rdb[i][:, :], ALU.mult).then_inc(mul_done, 1)

            def step(hh, k, **at_end):
                logits(hh, k, **at_end)
                reciprocals(hh, k, **at_end)
                multiply(hh, k, **at_end)

            for k in range(2 * NG):
                step(0, k, first=True)
            with dve.Fori(1, H // 2) as hh:
                for k in range(2 * NG):
                    step(hh, k)
            for k in range(2 * NG, 2 * NG + 3):
                step(H // 2 - 1, k, last=True)

            dve.wait_ge(lc_stored, 16 * NT)
            with dve.Fori(0, NG) as i:
                for p in range(2):
                    t = 2 * i + p
                    dve.wait_ge(h2_full[p], i + 1)
                    dve.tensor_copy(rows2[:, 0, ds(t * NP, NP)], bank[4 + p][0:1, 0:NP])
                    dve.tensor_scalar(rows2[:, 1, ds(t * NP, NP)], bank[4 + p][0:1, 0:NP], SLOPE, None, ALU.mult)
                    dve.tensor_scalar(nad2[:, ds(t, 1)], bank[2 * p + 1][0:NP, HALF:HALF + 1], SLOPE - 1.0, None,
                                      ALU.mult)
                    dve.tensor_copy(h2[:, ds(t, 1), HALF:D].rearrange("p t n -> p (t n)"),
                                    bank[2 * p + 1][0:NP, 0:HALF]).then_inc(h2b_done[p], 1)

            def reciprocals_5(i):
                dve.wait_ge(exp5, i + 1)
                dve.tensor_scalar(dn5[:, :], den5[:, :], EPS, None, ALU.add).then_inc(dn5_done, 1)
                dve.wait_ge(dn5_done, i + 1)
                dve.reciprocal(rden5[:, :], dn5[:, :]).then_inc(rden5_done, 1)

            def logits_5(i, first=False):
                for j in range(2):
                    if not first:
                        dve.wait_ge(t5_full, 5 * i)
                        alone(dve)
                    dve.scalar_tensor_tensor(L5[j][:, :], asb2[:, 1, :], nad2[:, ds((NT - 1 - j) - 2 * i, 1)],
                                             asb2[:, 0, :], ALU.add, ALU.max).then_inc(stt5, 1)
                for j in range(2):
                    dve.wait_ge(stt5, 2 * i + (j + 1))
                    dve.wait_ge(lct_in[j], 16 * (i + 1))
                    alone(dve)
                    dve.tensor_tensor_reduce(out=L5[j][:, :], in0=L5[j][:, :], in1=LCt[j][:, :], scale=1.0,
                                             scalar=-3e38, op0=ALU.add, op1=ALU.max,
                                             accum_out=mx5[:, j:j + 1]).then_inc(max5, 1)
                dve.wait_ge(max5, 2 * i + 2)
                dve.tensor_scalar(nm5[:, :], mx5[:, :], FLOOR, -1.0, ALU.max, ALU.mult).then_inc(nm5_ready, 1)

            def norm_5(i, j, first=False):
                n = 3 * (2 * i + j)
                dve.wait_ge(agg5, 2 * i + (j + 1))
                dve.wait_ge(xb_done[j], i + 1)
                dve.wait_ge(rden5_done, i + 1)
                if not first:
                    dve.wait_ge(x2f_done[j], i)
                for b in range(2):
                    c = slice(b * HALF, (b + 1) * HALF)
                    s = dve.scalar_tensor_tensor(x2[j][:, c], bank[2 + 2 * j + b][0:NP, 0:HALF], rden5[:, j:j + 1],
                                                 x5[j][:, c], ALU.mult, ALU.add)
                s.then_inc(x2_done[j], 1)
                dve.wait_ge(x2_done[j], i + 1)
                for b in range(2):
                    s = dve.bn_stats(stats5[j][:, b, :], x2[j][:, b * HALF:(b + 1) * HALF])
                s.then_inc(ln_step, 1)
                dve.wait_ge(ln_step, n + 1)
                alone(dve)
                dve.bn_aggr(mv5[j][:, :], stats5[j][:, :, :]).then_inc(ln_step, 1)
                dve.wait_ge(ln_step, n + 2)
                dve.tensor_scalar(var5[j][:, :], mv5[j][:, 1:2], LN_EPS, None, ALU.add).then_inc(ln_step, 1)
                dve.wait_ge(rstd5_ready, 2 * i + (j + 1))
                if not first:
                    dve.wait_ge(y_full, 3 * i)
                dve.tensor_scalar(y5[j][:, :], x2[j][:, :], mv5[j][:, 0:1], rstd5[j][:, 0:1],
                                  ALU.subtract, ALU.mult).then_inc(y_ready, 1)

            def out_5(i, j, first=False):
                dve.wait_ge(ffn_full, 2 * i + (j + 1))
                dve.wait_ge(x2f_done[j], i + 1)
                if not first:
                    dve.wait_ge(out_stored[j], 16 * i)
                for b in range(2):
                    c = slice(b * HALF, (b + 1) * HALF)
                    s = dve.tensor_tensor(ost[j][:, c], bank[6 + b][0:NP, 0:HALF], x2f[j][:, c], ALU.add)
                s.then_inc(out_done[j], 1)

            dve.wait_ge(asb2_in, 16)
            for p in range(2):
                dve.wait_ge(h2b_done[p], NG)
            logits_5(0, first=True)
            reciprocals_5(0)
            logits_5(1)
            for j in range(2):
                norm_5(0, j, first=True)
            reciprocals_5(1)
            logits_5(2)
            for j in range(2):
                norm_5(1, j)
                out_5(0, j, first=True)
            with dve.Fori(3, NG) as i:
                reciprocals_5(i + -1)
                logits_5(i)
                for j in range(2):
                    norm_5(i + -1, j)
                    out_5(i + -2, j)
            reciprocals_5(NG - 1)
            for j in range(2):
                norm_5(NG - 1, j)
                out_5(NG - 2, j)
            for j in range(2):
                out_5(NG - 1, j)

            steps = [0]

            def link(ins):
                steps[0] += 1
                ins.then_inc(gate_step, 1)
                dve.wait_ge(gate_step, steps[0])

            y, tok = y5[1][0:NCLS, :], x2[1][0:NCLS, :]
            dve.wait_ge(cls_in, 16 * 15)
            dve.wait_ge(y_ready, NT)
            dve.wait_ge(stt5, NT)
            for in0, in1, to in ((y, y, sq[:, 0:1]), (gp[:, 0, :], gp[:, 0, :], sq[:, 1:2]),
                                 (gp[:, 1, :], gp[:, 1, :], sq[:, 2:3]),
                                 (y, gp[:, 0, :], dots[:, 0:1]), (y, gp[:, 1, :], dots[:, 1:2])):
                link(dve.tensor_tensor_reduce(out=scr[:, :], in0=in0, in1=in1, scale=1.0, scalar=0.0,
                                              op0=ALU.mult, op1=ALU.add, accum_out=to))
            dve.wait_ge(gate_root, 1)
            link(dve.tensor_scalar(nr[:, :], sr[:, :], NORM_EPS, None, ALU.max))
            link(dve.tensor_scalar(lg[0][:, :], nr[:, 1:3], nr[:, 0:1], None, ALU.mult))
            link(dve.reciprocal(lg[1][:, :], lg[0][:, :]))
            link(dve.tensor_tensor(lg[2][:, :], dots[:, :], lg[1][:, :], ALU.mult))
            link(dve.tensor_tensor(lg[0][:, :], lg[2][:, :], bal[:, :], ALU.add))
            link(dve.tensor_reduce(g1[0][:, :], lg[0][:, :], mybir.AxisListType.X, ALU.max))
            link(dve.tensor_scalar(lg[1][:, :], lg[0][:, :], g1[0][:, 0:1], None, ALU.subtract))
            dve.wait_ge(gate_exp, 1)
            link(dve.tensor_reduce(g1[1][:, :], lg[2][:, :], mybir.AxisListType.X, ALU.add))
            link(dve.reciprocal(g1[2][:, :], g1[1][:, :]))
            link(dve.tensor_scalar(lg[3][:, :], lg[2][:, :], g1[2][:, 0:1], None, ALU.mult))
            link(dve.tensor_tensor(g1[3][:, :], lg[3][:, 1:2], lg[3][:, 0:1], ALU.is_gt))
            link(dve.tensor_scalar(g1[4][:, :], g1[3][:, :], -1.0, 1.0, ALU.mult, ALU.add))
            link(dve.tensor_tensor(g1[5][:, :], g1[3][:, :], lg[3][:, 1:2], ALU.mult))
            link(dve.tensor_tensor(g1[0][:, :], g1[4][:, :], lg[3][:, 0:1], ALU.mult))

            dve.wait_ge(pick_zero, 1)
            dve.wait_ge(hid_done, NATOM)
            for n, (l, r) in enumerate(ATOM_SRC):
                for a_from, a_to in ((l, r), (r, l)):
                    dve.tensor_copy(pick[:, a_to, :, n], hid[:, a_from * KF:(a_from + 1) * KF, n]
                                    ).then_inc(pick_done, 1)

            for r, used in ((1, NATOM + 3), (0, NATOM + 5)):
                dve.wait_ge(atom_used, used)
                for b in range(2):
                    c = slice(b * HALF, (b + 1) * HALF)
                    s = dve.tensor_tensor(cw[:, r, c], bank[4 + 2 * r + b][0:NCLS, 0:HALF], bo[:, r, c], ALU.add)
                link(s)
            link(dve.scalar_tensor_tensor(scr[:, :], cw[:, 0, :], g1[0][:, 0:1], tok, ALU.mult, ALU.add))
            dve.scalar_tensor_tensor(fin[:, :], cw[:, 1, :], g1[5][:, 0:1], scr[:, :], ALU.mult, ALU.add
                                     ).then_inc(cls_done, 1)


def kernel(**inputs):
    import numpy as np
    import concourse.bacc as bacc
    from concourse.bass_utils import run_bass_kernel_spmd

    a = {k: np.asarray(v) for k, v in inputs.items()}
    W1, W2 = a["L0_gnn_W1"], a["L0_gnn_W2"]
    fed = {
        "x": a["x"],
        "src_cols": a["src"].reshape(NCH, CE).T,
        "dst_cols": a["dst"].reshape(NCH, CE).T,
        "dst_rows": a["dst"].reshape(NS, 2 * CE),
        "W1": W1,
        "W1T": W1.T,
        "as1T": a["L0_gnn_att_src1"].T,
        "ad1T": a["L0_gnn_att_dst1"].T,
        "b1c": a["L0_gnn_b1"].reshape(H, C).T,
        "W2": W2,
        "W2T": W2.T,
        "as2T": a["L0_gnn_att_src2"].reshape(KD, 128).T,
        "ad2T": a["L0_gnn_att_dst2"].reshape(KD, 128).T,
        "b2": a["L0_gnn_b2"].reshape(1, D),
        "fc1T": a["L0_ffn_fc1_w"].T,
        "fc1b": a["L0_ffn_fc1_b"].reshape(KF, 128).T,
        "fc2T": a["L0_ffn_fc2_w"].T,
        "fc2b": a["L0_ffn_fc2_b"].reshape(1, D),
        "gate_pair": a["L0_ffn_gate_pair"],
        "atom_inT": a["L0_ffn_atom_in_w"].transpose(0, 2, 1),
        "atom_inb": a["L0_ffn_atom_in_b"].reshape(NATOM * KF, 128).T,
        "atom_outT": a["L0_ffn_atom_out_w"].transpose(0, 2, 1),
        "atom_outb": a["L0_ffn_atom_out_b"],
        "balance": a["L0_ffn_balance_bias"],
    }
    nc = bacc.Bacc("TRN2", target_bir_lowering=False, num_devices=1)
    arrays, args = {}, []
    for name, value in fed.items():
        value = np.ascontiguousarray(value)
        arrays[f"in_{name}"] = value
        args.append(nc.dram_tensor(f"in_{name}", value.shape, mybir.dt.from_np(value.dtype), kind="ExternalInput").ap())
    out = nc.dram_tensor("out_0", (N, D), F32, kind="ExternalOutput").ap()
    gnn_ffn_kernel(nc, *args, out)
    r = run_bass_kernel_spmd(nc, [arrays], core_ids=[0])
    return r.results[0]["out_0"]
```

```python
from contextlib import ExitStack

import concourse.bass as bass
from concourse import mybir

F32 = mybir.dt.float32
F32R = mybir.dt.float32r
F16 = mybir.dt.float16
I32 = mybir.dt.int32
ACT = mybir.ActivationFunctionType
ALU = mybir.AluOpType
RMAX = bass.bass_isa.ReduceOp.max

N, D = 1250, 768
H, C = 8, 128
HC = H * C
FH = 384
NE = 21250
NP = 125
NT = N // NP
NG = NT // 2
GW = 2 * NP
CE = 125
NCH = NE // CE
NS = NCH // 2
NQ = (NS + 1) // 2
CLOSE = 16
RING = 4
KD, KC, KF = D // 128, HC // 128, FH // 128
HALF = D // 2
NCLS, NATOM = 6, 5
SLOPE = 0.2
EPS = 1e-16
LN_EPS = 1e-5
NORM_EPS = 1e-12
FLOOR = -1e29
BANKS3 = [(0, 500), (500, 500), (1000, 250)]
TBANK = [0, 1, 6, 7, 0]
TFREE = [0, -3, -2, -1, 1]
ATOM_SRC = [(0, 3), (0, 4), (1, 3), (1, 4), (2, 3), (2, 4)]


def ds(start, size):
    return bass.ds(start, size)


def alone(engine):
    engine.nop(nofuse=True)


def freed(engine, semaphore, value):
    if not (isinstance(value, int) and value <= 0):
        engine.wait_ge(semaphore, value)


def rounds(engine, stop, body):
    body(0)
    with engine.Fori(1, stop) as i:
        body(i)


def at(hh, k, lag):
    kk = k - lag
    return (kk // NG) % 2, kk % NG, 2 * NG * hh + kk, 2 * hh + kk // NG


def down_bank(i, j):
    return 2 if (i, j) == (NG - 1, 1) else 6


def gnn_ffn_kernel(nc, x, src_cols, dst_cols, dst_rows, W1, W1T, as1T, ad1T, b1c, W2, W2T, as2T, ad2T,
                   b2, fc1T, fc1b, fc2T, fc2b, gate_pair, atom_inT, atom_inb, atom_outT, atom_outb,
                   balance, out):
    h1_d = nc.dram_tensor("h1_scratch", (N, HC), F32).ap()
    row_d = nc.dram_tensor("src_logit_rows", (H, 2, N), F32).ap()
    lc_d = nc.dram_tensor("log_count_scratch", (N, N), F32).ap()

    ctx = ExitStack()
    with ctx:
        def sb(name, shape, dt=F32, where=ctx):
            return where.enter_context(nc.sbuf_tensor(name, shape, dt))

        def sem(name):
            return ctx.enter_context(nc.semaphore(name))

        ident = sb("ident", [128, 128])
        zeros16 = sb("zeros16", [NP, 128], F16)
        att1 = sb("att1", [C, 2, H])
        att2 = sb("att2", [128, 2, KD])
        attz = sb("attz", [C, H, 2 * H])
        watt1 = sb("watt1", [128, KD, 2 * H])
        watt2 = sb("watt2", [128, KC, 2])
        nad1 = sb("nad1", [NP, H, NT])
        nad2 = sb("nad2", [NP, NT])
        b1_sb = sb("b1_sb", [C, H])
        fc1b_sb = sb("fc1b_sb", [128, KF])
        tiny = sb("tiny", [NP, 1])
        powers = sb("powers", [NP, 4])
        spans = sb("spans", [1, 3 * NT], I32)

        w_ctx = ExitStack()
        w1n_sb = sb("w1n_sb", [C, H, D], F32, w_ctx)
        w_ctx.close()
        w_ctx = ExitStack()
        w2n_sb = sb("w2n_sb", [128, KD, HC], F32, w_ctx)
        w_ctx.close()
        w_ctx = ExitStack()
        atom_w = [sb(f"atom_w{i}", [128, KD * FH], F32, w_ctx) for i in range(2)]
        w_ctx.close()
        w_ctx = ExitStack()
        w2_sb = sb("w2_sb", [128, KC, D + 2], F32, w_ctx)
        w_ctx.close()
        w2_lo = sb("w2_lo", [128, KC, D + 2], F32R)

        two_ctx = ExitStack()
        h2 = sb("h2", [NP, NT, D], F32, two_ctx)
        PT5 = sb("PT5", [NP, NT, GW], F32, two_ctx)
        lo_ctx = ExitStack()
        h1Tt_lo = [sb(f"h1Tt_lo{p}", [C, H, NP], F32R, lo_ctx) for p in range(2)]
        lo_ctx.close()
        scr = sb("scr", [NCLS, D], F32, two_ctx)
        tok_y = sb("tok_y", [NCLS, D], F32, two_ctx)
        tok_x = sb("tok_x", [NCLS, D], F32, two_ctx)
        two_ctx.close()
        LC = sb("LC", [NP, NT, N])

        p1 = ExitStack()
        w1_hi = sb("w1_hi", [128, KD, HC], F32R, p1)
        xT_hi = [sb(f"xT_hi{p}", [128, KD, NP], F32R, p1) for p in range(2)]
        whole = ExitStack()
        w1_sb = sb("w1_sb", [128, KD, HC], F32, whole)
        xT = [sb(f"xT{p}", [128, KD, NP], F32, whole) for p in range(2)]
        whole.close()
        w1_lo = sb("w1_lo", [128, KD, HC], F32R, p1)
        xT_lo = [sb(f"xT_lo{p}", [128, KD, NP], F32R, p1) for p in range(2)]
        h1st = [sb(f"h1st{p}", [NP, HC], F32, p1) for p in range(2)]
        pad1 = sb("pad1", [128, 1120], F32, p1)
        wrow1 = sb("wrow1", [2 * H, D], F32, p1)
        wrow2 = sb("wrow2", [2, HC], F32, p1)
        xin = [sb(f"xin{p}", [NP, D], F32, p1) for p in range(2)]
        xn = [sb(f"xn{p}", [NP, D], F32, p1) for p in range(2)]
        rows1 = sb("rows1", [H, 2, N], F32, p1)
        tile_rows = [sb(f"tile_rows{p}", [2 * H, NP], F32, p1) for p in range(2)]
        iota16 = sb("iota16", [CE, N], F16, p1)
        srci = sb("srci", [CE, NCH], I32, p1)
        dsti = sb("dsti", [CE, NCH], I32, p1)
        srcf = sb("srcf", [CE, NCH + 6], F32, p1)
        dstf = sb("dstf", [CE, NCH + 6], F32, p1)
        dsr = sb("dsr", [NS, 2 * CE], I32, p1)
        ohs = [sb(f"ohs{a}", [CE, N], F16, p1) for a in range(RING)]
        ohd = [sb(f"ohd{a}", [CE, NP], F16, p1) for a in range(RING)]
        stats = [sb(f"stats{p}", [NP, 2, 6], F32, p1) for p in range(2)]
        mv = [sb(f"mv{p}", [NP, 2], F32, p1) for p in range(2)]
        var = [sb(f"var{p}", [NP, 1], F32, p1) for p in range(2)]
        rstd = [sb(f"rstd{p}", [NP, 1], F32, p1) for p in range(2)]
        cmin = sb("cmin", [NS, 1], F32, p1)
        cmax = sb("cmax", [NS, 1], F32, p1)
        tlo = sb("tlo", [NS, NT], F32, p1)
        cidx = sb("cidx", [NS, 2], F32, p1)
        a1 = sb("a1", [NS, NT], F32, p1)
        a2 = sb("a2", [NS, NT], F32, p1)
        a3 = sb("a3", [NS, NT], F32, p1)
        vv = sb("vv", [NS, 2 * NT], F32, p1)
        vr = sb("vr", [NS, 2 * NT], F32, p1)
        sp0 = sb("sp0", [1, 3 * NT], F32, p1)
        hi0 = sb("hi0", [1, NT], F32, p1)
        p1.close()

        p3 = ExitStack()
        hT = sb("hT", [C, H, N], F32, p3)
        PT = [sb(f"PT{s}", [NP, NT, GW], F32, p3) for s in range(2)]
        rdb = [sb(f"rdb{i}", [C, GW], F32, p3) for i in range(2)]
        tmp = [sb(f"tmp{i}", [C, GW], F32, p3) for i in range(2)]
        asb = [None, sb("asb1", [NP, 2, N], F32, p3)]
        h1s = [sb(f"h1s{q}", [NP, NT, C], F32, p3) for q in range(2)]
        L = [sb(f"L{r}", [NP, N], F32, p3) for r in range(4)]
        asb[0] = sb("asb0", [NP, 2, N], F32, p3)
        nadh = [sb(f"nadh{q}", [NP, NT], F32, p3) for q in range(2)]
        mx = [sb(f"mx{q}", [NP, NT], F32, p3) for q in range(2)]
        nm = [sb(f"nm{q}", [NP, NT], F32, p3) for q in range(2)]
        den = [sb(f"den{q}", [NP, NT], F32, p3) for q in range(2)]
        dn = [sb(f"dn{q}", [NP, NT], F32, p3) for q in range(2)]
        rden = [sb(f"rden{q}", [NP, NT], F32, p3) for q in range(2)]
        p3.close()

        p4 = ExitStack()
        x2f = [sb(f"x2f{j}", [NP, D], F32, p4) for j in range(2)]
        y5 = [sb(f"y5_{j}", [NP, D], F32, p4) for j in range(2)]
        ost = [sb(f"ost{j}", [NP, D], F32, p4) for j in range(2)]
        yT = sb("yT", [128, KD, 2, NP], F32, p4)
        gT = sb("gT", [128, KF, GW], F32, p4)
        atom_w.append(sb("atom_w2", [128, KD * FH], F32, p4))
        b2_sb = sb("b2_sb", [NP, D], F32, p4)
        pad4 = sb("pad4", [128, 90], F32, p4)
        tok_ctx = ExitStack()
        gp = sb("gp", [NCLS, 2, D], F32, tok_ctx)
        tok_ctx.close()
        tok_ctx = ExitStack()
        cw = sb("cw", [NCLS, 2, D], F32, tok_ctx)
        tok_ctx.close()
        h1Tt_hi = [sb(f"h1Tt_hi{p}", [C, H, NP], F32R, p4) for p in range(2)]
        L5 = [sb(f"L5_{j}", [NP, N], F32, p4) for j in range(2)]
        LCt = [sb(f"LCt{j}", [NP, N], F32, p4) for j in range(2)]
        asb2 = sb("asb2", [NP, 2, N], F32, p4)
        x5 = [sb(f"x5_{j}", [NP, D], F32, p4) for j in range(2)]
        as2c = [sb(f"as2c{p}", [NP, 1], F32, p4) for p in range(2)]
        mx5 = sb("mx5", [NP, 2], F32, p4)
        nm5 = sb("nm5", [NP, 2], F32, p4)
        den5 = sb("den5", [NP, 2], F32, p4)
        dn5 = sb("dn5", [NP, 2], F32, p4)
        rden5 = sb("rden5", [NP, 2], F32, p4)
        stats5 = [sb(f"stats5_{j}", [NP, 2, 6], F32, p4) for j in range(2)]
        mv5 = [sb(f"mv5_{j}", [NP, 2], F32, p4) for j in range(2)]
        var5 = [sb(f"var5_{j}", [NP, 1], F32, p4) for j in range(2)]
        rstd5 = [sb(f"rstd5_{j}", [NP, 1], F32, p4) for j in range(2)]
        atom_b = sb("atom_b", [128, NATOM * KF], F32, p4)
        tokT = sb("tokT", [128, KD, NCLS], F32, p4)
        hid = sb("hid", [128, NATOM * KF, NCLS], F32, p4)
        pick = sb("pick", [128, NATOM, KF, NCLS], F32, p4)
        bal = sb("bal", [NCLS, 2], F32, p4)
        sq = sb("sq", [NCLS, 3], F32, p4)
        nr = sb("nr", [NCLS, 3], F32, p4)
        sr = sb("sr", [NCLS, 3], F32, p4)
        dots = sb("dots", [NCLS, 2], F32, p4)
        lg = [sb(f"lg{i}", [NCLS, 2], F32, p4) for i in range(4)]
        g1 = [sb(f"g1_{i}", [NCLS, 1], F32, p4) for i in range(6)]
        w2_ctx = ExitStack()
        w2_hi = sb("w2_hi", [128, KC, D + 2], F32R, w2_ctx)
        w2_ctx.close()
        x2 = [sb(f"x2_{j}", [NP, D], F32, p4) for j in range(2)]
        fc1_sb = sb("fc1_sb", [128, KD, FH], F32, p4)
        fc2_sb = sb("fc2_sb", [128, KF, D], F32, p4)
        fc2b_sb = sb("fc2b_sb", [NP, D], F32, p4)
        bo = sb("bo", [NCLS, 2, D], F32, p4)
        p4.close()

        bank = [ctx.enter_context(nc.psum_tensor(f"bank{b}", [128, 512], F32)) for b in range(8)]

        consts_made = sem("consts_made")
        att_in, w1n_in, w1_in, w2n_in, w2_in = (sem(n) for n in ("att_in", "w1n_in", "w1_in", "w2n_in", "w2_in"))
        ffn_in, bias_in, edges_in = sem("ffn_in"), sem("bias_in"), sem("edges_in")
        attz_set = sem("attz_set")
        wattp, watt_done = sem("wattp"), sem("watt_done")
        x_in = [sem(f"x_in{p}") for p in range(2)]
        stat_step, rstd_ready, xn_ready, xt_full, xT_ready = (
            sem(n) for n in ("stat_step", "rstd_ready", "xn_ready", "xt_full", "xT_ready"))
        logit_full, logit_rows, column_full, logit_done, h1_full, h1_out = (
            sem(n) for n in ("logit_full", "logit_rows", "column_full", "logit_done", "h1_full", "h1_out"))
        h1_stored = [sem(f"h1_stored{p}") for p in range(2)]
        rows_stored = sem("rows_stored")
        span_step, span_max, spans_ready = sem("span_step"), sem("span_max"), sem("spans_ready")
        oh_ready = [sem(f"oh_ready{a}") for a in range(RING)]
        oh_used = [sem(f"oh_used{a}") for a in range(RING)]
        cnt_full, ln_done, lc_done, lc_stored = (sem(n) for n in ("cnt_full", "ln_done", "lc_done", "lc_stored"))
        head_in = [sem(f"head_in{q}") for q in range(2)]
        asb_in = [sem(f"asb_in{q}") for q in range(2)]
        nadh_done, stt_done, max_done, nm_ready = (sem(n) for n in ("nadh_done", "stt_done", "max_done", "nm_ready"))
        exp_done, tb_full, tb_evac, agg_done = (sem(n) for n in ("exp_done", "tb_full", "tb_evac", "agg_done"))
        dn_done, rden_ready, rdb_full, rdb_ready = (sem(n) for n in ("dn_done", "rden_ready", "rdb_full", "rdb_ready"))
        mul_done, relu_done = sem("mul_done"), sem("relu_done")
        tile_ready, h2_full, h2a_done, h2b_done = (sem(n) for n in ("tile_ready", "h2_full", "h2a_done", "h2b_done"))
        row_full, row_out = sem("row_full"), sem("row_out")
        lct_in = [sem(f"lct_in{j}") for j in range(2)]
        stt5, max5, nm5_ready, exp5 = sem("stt5"), sem("max5"), sem("nm5_ready"), sem("exp5")
        t5_full, t5_evac, y_full, y_evac = sem("t5_full"), sem("t5_evac"), sem("y_full"), sem("y_evac")
        dn5_done, rden5_done, agg5 = sem("dn5_done"), sem("rden5_done"), sem("agg5")
        x5_in = [sem(f"x5_in{j}") for j in range(2)]
        xb_done = [sem(f"xb_done{j}") for j in range(2)]
        x2_done = [sem(f"x2_done{j}") for j in range(2)]
        ln_step, y_ready = sem("ln_step"), sem("y_ready")
        x2f_done = [sem(f"x2f_done{j}") for j in range(2)]
        hid_full, gelu_done, ffn_full = sem("hid_full"), sem("gelu_done"), sem("ffn_full")
        out_done = [sem(f"out_done{j}") for j in range(2)]
        out_stored = [sem(f"out_stored{j}") for j in range(2)]
        atom_in_sem = [sem(f"atom_in_sem{i}") for i in range(3)]
        atom_used, cls_in, hid_done = sem("atom_used"), sem("cls_in"), sem("hid_done")
        tokT_done, tok_saved, cand_read = sem("tokT_done"), sem("tok_saved"), sem("cand_read")
        pick_zero, pick_done, gate_step, cls_done, cls_stored = (
            sem(n) for n in ("pick_zero", "pick_done", "gate_step", "cls_done", "cls_stored"))
        gate_exp, gate_root = sem("gate_exp"), sem("gate_root")
        w2_hi_done, w2_lo_done, tile_lo_done = sem("w2_hi_done"), sem("w2_lo_done"), sem("tile_lo_done")
        w1_hi_done, w1_lo_done, xT_lo_done = sem("w1_hi_done"), sem("w1_lo_done"), sem("xT_lo_done")
        powers_set, rstd5_ready = sem("powers_set"), sem("rstd5_ready")

        block = ctx.enter_context(nc.Block())

        @block.sync
        def _(sp):
            def load_x(p, t):
                sp.dma_start(xin[p][:, :], x[ds(t * NP, NP), :]).then_inc(x_in[p], 16)

            def store_h1(p, i):
                sp.wait_ge(h1_out, 2 * i + (p + 1))
                sp.dma_start(h1_d[ds((2 * i + p) * NP, NP), :], h1st[p][:, :]).then_inc(h1_stored[p], 16)

            def store_lc(p, i):
                sp.wait_ge(lc_done, 2 * i + (p + 1))
                sp.dma_start(lc_d[ds((2 * i + p) * NP, NP), :], LC[:, ds(2 * i + p, 1), :]
                             .rearrange("p t n -> p (t n)")).then_inc(lc_stored, 16)

            sp.dma_start(dsr[:, :], dst_rows).then_inc(edges_in, 16)
            sp.dma_start(dsti[:, :], dst_cols).then_inc(edges_in, 16)
            sp.dma_start(srci[:, :], src_cols).then_inc(edges_in, 16)
            load_x(0, 0)
            load_x(1, 1)
            sp.dma_start(att1[:, 0, :], as1T).then_inc(att_in, 16)
            sp.dma_start(att1[:, 1, :], ad1T).then_inc(att_in, 16)
            sp.dma_start(att2[:, 0, :], as2T).then_inc(att_in, 16)
            sp.dma_start(att2[:, 1, :], ad2T).then_inc(att_in, 16)
            for p in range(2):
                store_lc(p, 0)
            sp.wait_ge(wattp, 1)
            sp.dma_start(w2n_sb[:, :, :], W2.rearrange("(k p) n -> p k n", p=128)).then_inc(w2n_in, 16)
            with sp.Fori(0, NG - 1) as i:
                for p in range(2):
                    sp.wait_ge(xn_ready, 2 * i + (p + 1))
                    load_x(p, 2 * i + p + 2)
                    store_lc(p, i + 1)
                    store_h1(p, i)
            sp.wait_ge(logit_rows, NT)
            sp.dma_start(row_d, rows1[:, :, :]).then_inc(rows_stored, 16)

            def load_features(q, h):
                sp.dma_start(h1s[q][:, :, :], h1_d[:, ds(h * C, C)].rearrange("(s p) c -> p s c", p=NP)
                             ).then_inc(head_in[q], 16)

            def load_logits(q, h):
                row = row_d[ds(h, 1), :, :].rearrange("a b n -> a (b n)")
                sp.dma_start(asb[q][:, :, :].rearrange("p b n -> p (b n)"), row.to_broadcast([NP, 2 * N])
                             ).then_inc(asb_in[q], 16)

            sp.wait_ge(rows_stored, 16)
            sp.wait_ge(ln_done, NT)
            load_logits(0, 0)
            for p in range(2):
                store_h1(p, NG - 1)
            for p in range(2):
                sp.wait_ge(h1_stored[p], 16 * NG)
            load_features(0, 0)
            load_logits(1, 1)
            load_features(1, 1)
            sp.wait_ge(wattp, 3)
            sp.dma_start(w2_sb[:, :, 0:D], W2T.rearrange("(k p) n -> p k n", p=128)).then_inc(w2_in, 16)
            with sp.Fori(0, H // 2 - 1) as hh:
                for q in range(2):
                    sp.wait_ge(stt_done, NT * (2 * hh + q) + NT)
                    load_logits(q, 2 * hh + q + 2)
                    sp.wait_ge(agg_done, NG * (2 * hh + q) + NG)
                    load_features(q, 2 * hh + q + 2)

            sp.wait_ge(agg_done, NG * H)
            sp.wait_ge(mul_done, NG * H)
            sp.wait_ge(relu_done, NG * H)
            sp.wait_ge(lc_stored, 16 * NT)

            def lc_load(i):
                for j in range(2):
                    if i > 0:
                        sp.wait_ge(max5, 2 * i + j - 1)
                    t = 2 * i + j
                    sp.dma_start(LCt[j][:, :], lc_d[t * NP:(t + 1) * NP, :]).then_inc(lct_in[j], 16)

            def out_store(i):
                for j in range(2):
                    first = NCLS if i == j == 0 else 0
                    t = 2 * i + j
                    sp.wait_ge(out_done[j], i + 1)
                    sp.dma_start(out[t * NP + first:(t + 1) * NP, :], ost[j][first:NP, :]
                                 ).then_inc(out_stored[j], 16)

            atoms = [(atom_inT, a) for a in range(NATOM)] + [(atom_outT, a) for a in range(NATOM)]

            def load_atom(s):
                which, a = atoms[s]
                if s >= 3:
                    sp.wait_ge(atom_used, s - 2)
                sp.dma_start(atom_w[s % 3][:, :].rearrange("p (k n) -> p k n", k=KD if s < NATOM else KF),
                             which[a].rearrange("(k p) n -> p k n", p=128)).then_inc(atom_in_sem[s % 3], 16)

            lc_load(0)
            sp.dma_start(atom_b[:, :], atom_inb).then_inc(cls_in, 16)
            lc_load(1)
            sp.wait_ge(h2_full, NT)
            sp.dma_start(b2_sb[:, :], b2.to_broadcast([NP, D])).then_inc(bias_in, 16)
            sp.dma_start(fc2b_sb[:, :], fc2b.to_broadcast([NP, D])).then_inc(bias_in, 16)
            sp.dma_start(fc1_sb[:, :, :], fc1T.rearrange("(k p) n -> p k n", p=128)).then_inc(ffn_in, 16)
            sp.dma_start(fc2_sb[:, :, :], fc2T.rearrange("(k p) n -> p k n", p=128)).then_inc(ffn_in, 16)
            for s in range(3):
                load_atom(s)
            sp.dma_start(gp[:, :, :], gate_pair).then_inc(cls_in, 16)
            sp.dma_start(bal[:, :], balance).then_inc(cls_in, 16)
            for r, rows in enumerate(([r for _, r in ATOM_SRC], [l for l, _ in ATOM_SRC])):
                for n in range(0, NCLS):
                    sp.dma_start(bo[n:n + 1, r, :], atom_outb[rows[n]:rows[n] + 1, :]).then_inc(cls_in, 16)
            lc_load(2)
            for s in range(3, 6):
                load_atom(s)
            lc_load(3)
            out_store(0)
            for s in range(6, 8):
                load_atom(s)
            lc_load(4)
            out_store(1)
            for s in range(8, 10):
                load_atom(s)
            out_store(2)
            out_store(3)
            sp.wait_ge(cls_done, 1)
            sp.dma_start(out[0:NCLS, :], tok_x[:, :]).then_inc(cls_stored, 16)
            out_store(NG - 1)
            for j in range(2):
                sp.wait_ge(out_stored[j], 16 * NG)
            sp.wait_ge(cls_stored, 16)

        @block.gpsimd
        def _(pool):
            pool.memset(ident[:, :], 0.0).then_inc(consts_made, 1)
            pool.wait_ge(consts_made, 1)
            pool.affine_select(out=ident[:, :], in_=ident[:, :], compare_op=ALU.not_equal, fill=1.0,
                               base=0, pattern=[[-1, 128]], channel_multiplier=1).then_inc(consts_made, 1)
            pool.memset(zeros16[:, :], 0.0).then_inc(consts_made, 1)
            pool.memset(tiny[:, :], 2.0 ** -60).then_inc(consts_made, 1)
            pool.iota(iota16[:, :], pattern=[[1, N]], base=0, channel_multiplier=0,
                      allow_small_or_imprecise_dtypes=True).then_inc(consts_made, 1)
            pool.iota(tlo[:, :], pattern=[[NP, NT]], base=0, channel_multiplier=0,
                      allow_small_or_imprecise_dtypes=True).then_inc(consts_made, 1)
            pool.iota(cidx[:, 0:1], pattern=[[0, 1]], base=NS, channel_multiplier=-1,
                      allow_small_or_imprecise_dtypes=True).then_inc(consts_made, 1)
            pool.iota(cidx[:, 1:2], pattern=[[0, 1]], base=1, channel_multiplier=1,
                      allow_small_or_imprecise_dtypes=True).then_inc(consts_made, 1)
            pool.memset(powers[:, 0:1], -0.5).then_inc(powers_set, 1)
            pool.memset(powers[:, 1:4], 0.5).then_inc(powers_set, 1)

            def rstd_of(p, i):
                pool.wait_ge(stat_step, 3 * (2 * i + p) + 3)
                pool.tensor_tensor(rstd[p][:, :], var[p][:, :], powers[:, 0:1], ALU.pow).then_inc(rstd_ready, 1)

            pool.wait_ge(span_step, 8)
            pool.partition_all_reduce(vr[:, :], vv[:, :], NS, RMAX).then_inc(span_max, 1)
            for k in range(KD):
                pool.wait_ge(w1_hi_done, k + 1)
                pool.tensor_tensor(w1_lo[:, k, :], w1_sb[:, k, :], w1_hi[:, k, :].bitcast(F32), ALU.subtract
                                   ).then_inc(w1_lo_done, 1)
            pool.wait_ge(powers_set, 2)
            rstd_of(0, 0)
            with pool.Fori(0, NG - 1) as i:
                rstd_of(1, i)
                rstd_of(0, i + 1)
            rstd_of(1, NG - 1)

            def load_x5(i, j):
                t = 2 * i + j
                pool.dma_start(x5[j][:, :], x[t * NP:(t + 1) * NP, :]).then_inc(x5_in[j], 16)

            def add_biases(i):
                for j in range(2):
                    pool.wait_ge(x5_in[j], 16 * (i + 1))
                    pool.tensor_tensor(x5[j][:, :], x5[j][:, :], b2_sb[:, :], ALU.add).then_inc(xb_done[j], 1)
                for j in range(2):
                    pool.wait_ge(x2_done[j], i + 1)
                    if i < NG - 1:
                        load_x5(i + 1, j)
                    pool.wait_ge(ln_step, 3 * (2 * i + j) + 3)
                    pool.tensor_tensor(rstd5[j][:, :], var5[j][:, :], powers[:, 0:1], ALU.pow).then_inc(rstd5_ready, 1)
                    if i > 0:
                        pool.wait_ge(out_done[j], i)
                    pool.tensor_tensor(x2f[j][:, :], x2[j][:, :], fc2b_sb[:, :], ALU.add).then_inc(x2f_done[j], 1)

            pool.wait_ge(agg_done, NG * H)
            pool.wait_ge(mul_done, NG * H)
            pool.wait_ge(relu_done, NG * H)
            pool.memset(pick[:, :, :, :], 0.0).then_inc(pick_zero, 1)
            for j in range(2):
                load_x5(0, j)
            pool.wait_ge(bias_in, 16 * 4)
            add_biases(0)
            pool.wait_ge(gate_step, 5)
            pool.tensor_tensor(sr[:, :], sq[:, :], powers[0:NCLS, 1:4], ALU.pow).then_inc(gate_root, 1)
            for i in range(1, NG):
                add_biases(i)

        @block.scalar
        def _(act):
            act.wait_ge(edges_in, 48)
            act.dma_start(w1n_sb[:, :, :], W1.rearrange("(h c) d -> c h d", c=C)).then_inc(w1n_in, 16)
            act.dma_start(w1_sb[:, :, :], W1T.rearrange("(k p) n -> p k n", p=128)).then_inc(w1_in, 16)
            act.dma_start(b1_sb[:, :], b1c).then_inc(bias_in, 16)
            act.dma_start(fc1b_sb[:, :], fc1b).then_inc(bias_in, 16)

            def rows_turned(p, i):
                act.wait_ge(xt_full, 2 * i + (p + 1))
                freed(act, h1_full, 2 * i + (p - 1))
                act.copy(xT[p][:, 0:4, :], bank[3][:, 0:4 * NP].rearrange("p (k n) -> p k n", k=4))
                act.copy(xT[p][:, 4:6, :], bank[4][:, 0:2 * NP].rearrange("p (k n) -> p k n", k=2))
                act.copy(xT_hi[p][:, 0:4, :], bank[3][:, 0:4 * NP].rearrange("p (k n) -> p k n", k=4))
                act.copy(xT_hi[p][:, 4:6, :], bank[4][:, 0:2 * NP].rearrange("p (k n) -> p k n", k=2)
                         ).then_inc(xT_ready, 1)

            def log_counts(p, i):
                act.wait_ge(cnt_full, 2 * i + (p + 1))
                for b, (c0, w) in enumerate(BANKS3):
                    last = act.activation(LC[:, ds(2 * i + p, 1), c0:c0 + w].rearrange("p t n -> p (t n)"),
                                          bank[b][0:NP, 0:w], ACT.Ln, bias=tiny[:, 0:1], scale=2.0)
                last.then_inc(ln_done, 1)

            def features_out(p, i):
                act.wait_ge(h1_full, 2 * i + (p + 1))
                freed(act, h1_stored[p], 16 * i)
                for half in range(2):
                    c = act.copy(h1st[p][:, half * 512:(half + 1) * 512], bank[6 + half][0:NP, :])
                c.then_inc(h1_out, 1)

            def tile_out(i):
                for p in range(2):
                    rows_turned(p, i)
                    log_counts(p, i + 1)
                    features_out(p, i)

            act.wait_ge(consts_made, 4)
            log_counts(0, 0)
            act.wait_ge(w1_in, 16)
            for k in range(KD):
                act.copy(w1_hi[:, k, :], w1_sb[:, k, :]).then_inc(w1_hi_done, 1)
            log_counts(1, 0)
            rounds(act, NG - 1, tile_out)
            for p in range(2):
                rows_turned(p, NG - 1)
            def exp(hh, k, first=False, last=False):
                if last:
                    return
                q, g, n, h = at(hh, k, 0)
                act.wait_ge(nm_ready, n + 1)
                for j in range(2):
                    r, t = (2 * k + j) % 4, 2 * g + j
                    e = act.activation(L[r][:, :], L[r][:, :], ACT.Exp, bias=nm[q][:, t:t + 1], scale=1.0,
                                       accum_out=den[q][:, t:t + 1])
                e.then_inc(exp_done, 1)

            def evac(hh, k, first=False, last=False):
                lag = 1
                if (first and k < lag) or (last and k - lag >= 2 * NG):
                    return
                q, g, n, h = at(hh, k, lag)
                for b in range(5):
                    act.wait_ge(tb_full, NG * n + b + 1)
                    if b == 0 and not (first and k - lag < 2):
                        act.wait_ge(agg_done, n + -1)
                    act.copy(PT[(k - lag) % 2][:, 2 * b:2 * b + 2, :],
                             bank[TBANK[b]][0:NP, 0:2 * GW].rearrange("p (s n) -> p s n", s=2)
                             ).then_inc(tb_evac, 1)

            def rdb_copy(hh, k, first=False, last=False):
                lag = 2
                if (first and k < lag) or (last and k - lag >= 2 * NG):
                    return
                q, g, n, h = at(hh, k, lag)
                act.wait_ge(rdb_full, n + 1)
                if not (first and k - lag < 2):
                    act.wait_ge(mul_done, n + -1)
                i = (k - lag) % 2
                act.copy(rdb[i][:, :], bank[4 + i][:, 0:GW]).then_inc(rdb_ready, 1)

            def relu(hh, k, first=False, last=False):
                lag = 4
                if (first and k < lag) or (last and k - lag >= 2 * NG):
                    return
                q, g, n, h = at(hh, k, lag)
                if first and k == lag:
                    act.wait_ge(bias_in, 16 * 2)
                    for p in range(2):
                        act.wait_ge(h1_stored[p], 16 * NG)
                act.wait_ge(mul_done, n + 1)
                act.activation(hT[:, ds(h, 1), g * GW:(g + 1) * GW].rearrange("c h n -> c (h n)"),
                               tmp[(k - lag) % 2][:, :], ACT.Relu, bias=b1_sb[:, ds(h, 1)], scale=1.0
                               ).then_inc(relu_done, 1)

            def step(hh, k, **at_end):
                evac(hh, k, **at_end)
                rdb_copy(hh, k, **at_end)
                if not (at_end.get("first") and k == 0):
                    exp(hh, k, **at_end)
                relu(hh, k, **at_end)


            features_out(0, NG - 1)
            exp(0, 0)
            features_out(1, NG - 1)
            for k in range(2 * NG):
                step(0, k, first=True)
            with act.Fori(1, H // 2) as hh:
                for k in range(2 * NG):
                    step(hh, k)
            step(H // 2 - 1, 2 * NG, last=True)
            act.wait_ge(w2_in, 16)
            act.wait_ge(watt_done, 5)
            act.wait_ge(tb_full, NG * NG * H)
            act.wait_ge(stt_done, NT * H)
            for k in range(KC):
                act.copy(w2_hi[:, k, :], w2_sb[:, k, :]).then_inc(w2_hi_done, 1)
            for k in range(2 * NG + 1, 2 * NG + 4):
                step(H // 2 - 1, k, last=True)

            act.wait_ge(max_done, NT * H)
            act.wait_ge(lc_stored, 16 * NT)
            act.wait_ge(relu_done, NG * H)
            act.wait_ge(agg_done, NG * H)

            def tile_of_hT(p, i):
                freed(act, h2_full, 2 * i + (p - 1))
                act.copy(h1Tt_hi[p][:, :, :], hT[:, :, ds((2 * i + p) * NP, NP)]).then_inc(tile_ready, 1)

            def h2_out(p, i):
                act.wait_ge(h2_full, 2 * i + (p + 1))
                act.copy(h2[:, ds(2 * i + p, 1), 0:HALF].rearrange("p t n -> p (t n)"),
                         bank[2 * p][0:NP, 0:HALF]).then_inc(h2a_done, 1)

            tile_of_hT(0, 0)
            tile_of_hT(1, 0)
            with act.Fori(0, NG - 1) as i:
                for p in range(2):
                    h2_out(p, i)
                    tile_of_hT(p, i + 1)

            def exp_5(i):
                act.wait_ge(nm5_ready, i + 1)
                for j in range(2):
                    e = act.activation(L5[j][:, :], L5[j][:, :], ACT.Exp, bias=nm5[:, j:j + 1], scale=1.0,
                                       accum_out=den5[:, j:j + 1])
                e.then_inc(exp5, 1)

            def evac_5(i, first=False):
                for b in range(5):
                    act.wait_ge(t5_full, 5 * i + b + 1)
                    if b == 0 and not first:
                        act.wait_ge(agg5, 2 * i)
                    act.copy(PT5[:, 2 * b:2 * b + 2, :],
                             bank[b % 2][0:NP, 0:2 * GW].rearrange("p (s n) -> p s n", s=2)).then_inc(t5_evac, 1)

            def ffn_5(i, tokens=False):
                for c in range(3):
                    act.wait_ge(y_full, 3 * i + c + 1)
                    act.copy(yT[:, 2 * c:2 * c + 2, :, :], bank[(c + 1) % 2][:, 0:2 * GW]
                             .rearrange("p (k j n) -> p k j n", k=2, j=2)).then_inc(y_evac, 1)
                if tokens:
                    act.wait_ge(y_evac, 3)
                    act.copy(tokT[:, :, :], yT[:, :, 0, 0:NCLS]).then_inc(tokT_done, 1)
                act.wait_ge(hid_full, i + 1)
                for m in range(KF):
                    g = act.activation(gT[:, m, :], bank[6 + m // 2][:, (m % 2) * GW:(m % 2 + 1) * GW], ACT.Gelu,
                                       bias=fc1b_sb[:, m:m + 1], scale=1.0)
                g.then_inc(gelu_done, 1)

            def hidden_of_atoms(atoms_from, atoms_to):
                for a in range(atoms_from, atoms_to):
                    for m in range(KF):
                        c = HALF + (a * KF + m) * 8
                        g = act.activation(hid[:, a * KF + m, :], bank[7][:, c:c + NCLS], ACT.Gelu,
                                           bias=atom_b[:, a * KF + m:a * KF + m + 1], scale=1.0)
                    g.then_inc(hid_done, 1)

            exp_5(0)
            for p in range(2):
                h2_out(p, NG - 1)
            evac_5(0, first=True)
            exp_5(1)
            evac_5(1)
            ffn_5(0, tokens=True)
            act.wait_ge(cls_in, 16 * 15)
            hidden_of_atoms(0, 3)
            exp_5(2)
            evac_5(2)
            ffn_5(1)
            hidden_of_atoms(3, NATOM)
            act.wait_ge(gate_step, 12)
            act.activation(lg[2][:, :], lg[1][:, :], ACT.Exp).then_inc(gate_exp, 1)
            exp_5(3)
            evac_5(3)
            ffn_5(2)
            exp_5(4)
            evac_5(4)
            ffn_5(3)
            ffn_5(4)

        @block.tensor
        def _(pe):
            def add_chunks(a, first=False):
                for b, (c0, w) in enumerate(BANKS3):
                    mm = pe.matmul(bank[b][0:NP, 0:w], ohd[a][:, :], ohs[a][:, c0:c0 + w],
                                   start=first, stop=False, skip_group_check=True)
                mm.then_inc(oh_used[a], 1)

            def count_edges(p, i):
                count = pe.value_load(spans[0:1, ds(2 * i + (NT + p), 1)], min_val=2, max_val=NQ)
                before = pe.value_load(spans[0:1, ds(2 * i + (2 * NT + p), 1)], min_val=0, max_val=NQ * NT)
                freed(pe, ln_done, 2 * i + p)
                for a in range(RING):
                    pe.wait_ge(oh_ready[a], before + 1)
                    add_chunks(a, first=(a == 0))
                with pe.Fori(1, count) as c:
                    for a in range(RING):
                        pe.wait_ge(oh_ready[a], before + c + 1)
                        add_chunks(a)
                for b, (c0, w) in enumerate(BANKS3):
                    mm = pe.matmul(bank[b][0:NP, 0:CLOSE], zeros16[:, 0:NP], iota16[:, 0:CLOSE],
                                   start=False, stop=True, skip_group_check=True)
                mm.then_inc(cnt_full, 1)

            pe.wait_ge(consts_made, 5)
            pe.wait_ge(spans_ready, 1)
            count_edges(0, 0)
            count_edges(1, 0)

            pe.wait_ge(w1n_in, 16)
            pe.wait_ge(attz_set, 3)
            for b in range(2):
                for h in range(H):
                    mm = pe.matmul(bank[6 + b][0:2 * H, 0:HALF], attz[:, h, :], w1n_sb[:, h, b * HALF:(b + 1) * HALF],
                                   start=(h == 0), stop=(h == H - 1))
            mm.then_inc(wattp, 1)
            pe.wait_ge(watt_done, 1)
            for k in range(KD):
                mm = pe.transpose(bank[5][:, 2 * H * k:2 * H * (k + 1)], wrow1[:, k * 128:(k + 1) * 128],
                                  ident[0:2 * H, 0:2 * H])
            mm.then_inc(wattp, 1)
            pe.wait_ge(watt_done, 2)
            pe.wait_ge(w1_lo_done, KD)

            def turn(p, i):
                pe.wait_ge(xn_ready, 2 * i + (p + 1))
                freed(pe, xT_ready, 2 * i + p)
                for k in range(KD):
                    b, c = (3, k) if k < 4 else (4, k - 4)
                    mm = pe.transpose(bank[b][:, c * NP:(c + 1) * NP], xn[p][:, k * 128:(k + 1) * 128],
                                      ident[0:NP, 0:NP])
                mm.then_inc(xt_full, 1)

            def logit_products(p, i):
                pe.wait_ge(xT_ready, 2 * i + (p + 1))
                freed(pe, logit_done, 2 * i + p)
                for k in range(KD):
                    mm = pe.matmul(bank[5][0:2 * H, 0:NP], watt1[:, k, :], xT[p][:, k, :],
                                   start=(k == 0), stop=(k == KD - 1))
                mm.then_inc(logit_full, 1)

            def logit_columns(p, i):
                pe.wait_ge(logit_rows, 2 * i + (p + 1))
                alone(pe)
                pe.transpose(bank[5][0:NP, 128:128 + 2 * H], tile_rows[p][:, :], ident[0:2 * H, 0:2 * H]
                             ).then_inc(column_full, 1)

            def products(p, i, columns):
                freed(pe, h1_out, 2 * i + p)
                for part, (rows, weights) in enumerate(((xT_hi, w1_hi), (xT_hi, w1_lo), (xT_lo, w1_hi))):
                    if part == 2:
                        pe.wait_ge(xT_lo_done, 2 * i + (p + 1))
                    for half in range(2):
                        for k in range(KD):
                            mm = pe.matmul(bank[6 + half][0:NP, :], rows[p][:, k, :],
                                           weights[:, k, half * 512:(half + 1) * 512],
                                           start=(part == 0 and k == 0), stop=(part == 2 and k == KD - 1))
                    if part == 1 and columns is not None:
                        logit_columns(columns, i)
                mm.then_inc(h1_full, 1)

            def tile_products(i):
                for p in range(2):
                    turn(p, i)
                    count_edges(p, i + 1)
                    logit_products(p, i)
                    products(p, i, columns=p)

            rounds(pe, NG - 1, tile_products)

            pe.wait_ge(w2n_in, 16)
            pe.wait_ge(att_in, 16 * 4)
            pe.wait_ge(ln_done, NT)
            for b in range(2):
                for k in range(KD):
                    mm = pe.matmul(bank[b][0:2, :], att2[:, :, k], w2n_sb[:, k, b * 512:(b + 1) * 512],
                                   start=(k == 0), stop=(k == KD - 1))
            mm.then_inc(wattp, 1)

            for p in range(2):
                turn(p, NG - 1)
                if p == 1:
                    logit_columns(0, NG - 1)
                    pe.wait_ge(watt_done, 3)
                    for c in range(KC):
                        mm = pe.transpose(bank[2][:, 2 * c:2 * c + 2], wrow2[:, c * 128:(c + 1) * 128],
                                          ident[0:2, 0:2])
                    mm.then_inc(wattp, 1)
                logit_products(p, NG - 1)
            products(0, NG - 1, columns=1)
            products(1, NG - 1, columns=None)

            def turn_bank(hh, k, b, first=False, last=False):
                lag = 1
                if (first and k < lag) or (last and k - lag >= 2 * NG):
                    return
                q, g, n, h = at(hh, k, lag)
                if b == 0:
                    pe.wait_ge(exp_done, n + 1)
                if not (first and k == lag and b < 4):
                    pe.wait_ge(tb_evac, NG * n + TFREE[b])
                for s in range(2):
                    for j in range(2):
                        mm = pe.transpose(bank[TBANK[b]][0:NP, (2 * s + j) * NP:(2 * s + j + 1) * NP],
                                          L[(2 * (k - lag) + j) % 4][:, (2 * b + s) * NP:(2 * b + s + 1) * NP],
                                          ident[0:NP, 0:NP])
                mm.then_inc(tb_full, 1)

            def aggregate(hh, k, b, first=False, last=False):
                lag = 2
                if (first and k < lag) or (last and k - lag >= 2 * NG):
                    return
                q, g, n, h = at(hh, k, lag)
                if b == 0:
                    pe.wait_ge(tb_evac, NG * n + NG)
                    if g == 0:
                        pe.wait_ge(head_in[q], 16 * (hh + 1))
                    if not (first and k - lag < 2):
                        pe.wait_ge(mul_done, n + -1)
                for s in range(2 * b, 2 * b + 2):
                    mm = pe.matmul(bank[2 + (k - lag) % 2][:, 0:GW], h1s[q][:, s, :], PT[(k - lag) % 2][:, s, :],
                                   start=(s == 0), stop=(s == NT - 1))
                if b == 4:
                    mm.then_inc(agg_done, 1)

            def spread(hh, k, first=False, last=False):
                lag = 2
                if (first and k < lag) or (last and k - lag >= 2 * NG):
                    return
                q, g, n, h = at(hh, k, lag)
                pe.wait_ge(rden_ready, n + 1)
                if not (first and k - lag < 2):
                    pe.wait_ge(rdb_ready, n + -1)
                for j in range(2):
                    t = 2 * g + j
                    mm = pe.matmul(bank[4 + (k - lag) % 2][:, j * NP:(j + 1) * NP],
                                   rden[q][:, t:t + 1].to_broadcast([NP, C]), ident[0:NP, 0:NP],
                                   start=True, stop=True)
                mm.then_inc(rdb_full, 1)

            def step(hh, k, **at_end):
                for b in range(4):
                    turn_bank(hh, k, b, **at_end)
                spread(hh, k, **at_end)
                aggregate(hh, k, 0, **at_end)
                turn_bank(hh, k, 4, **at_end)
                for b in range(1, 5):
                    aggregate(hh, k, b, **at_end)

            pe.wait_ge(watt_done, 5)
            pe.wait_ge(h1_out, NT)
            for k in range(2 * NG):
                step(0, k, first=True)
            with pe.Fori(1, H // 2) as hh:
                for k in range(2 * NG):
                    step(hh, k)
            for k in range(2 * NG, 2 * NG + 2):
                step(H // 2 - 1, k, last=True)

            pe.wait_ge(mul_done, NG * H)
            pe.wait_ge(rdb_ready, NG * H)
            pe.wait_ge(tb_evac, NG * NG * H)

            def second_features(p, i):
                pe.wait_ge(tile_ready, 2 * i + (p + 1))
                freed(pe, h2a_done, 2 * i + (p - 1))
                freed(pe, h2b_done, 2 * i + (p - 1))
                for part, (rows, weights, split) in enumerate(((h1Tt_hi, w2_hi, w2_hi_done), (h1Tt_hi, w2_lo, w2_lo_done),
                                                               (h1Tt_lo, w2_hi, None))):
                    if part == 2:
                        pe.wait_ge(tile_lo_done, 2 * i + (p + 1))
                    for k in range(KC):
                        if part < 2 and p == 0 and isinstance(i, int) and i == 0:
                            pe.wait_ge(split, k + 1)
                        for b, (c0, w) in enumerate(((0, HALF), (HALF, HALF + 2))):
                            mm = pe.matmul(bank[2 * p + b][0:NP, 0:w], rows[p][:, k, :], weights[:, k, c0:c0 + w],
                                           start=(part == 0 and k == 0), stop=(part == 2 and k == KC - 1))
                mm.then_inc(h2_full, 1)

            def spread_logits(p, i):
                pe.wait_ge(h2b_done, 2 * i + (p + 1))
                freed(pe, row_out, 2 * i + (p - 1))
                pe.matmul(bank[4 + p][0:NP, 0:NP], as2c[p][:, 0:1].to_broadcast([NP, NP]), ident[0:NP, 0:NP],
                          start=True, stop=True).then_inc(row_full, 1)

            second_features(0, 0)
            second_features(1, 0)
            spread_logits(0, 0)

            def second_tiles(i):
                second_features(0, i)
                spread_logits(1, i - 1 if isinstance(i, int) else i + -1)
                second_features(1, i)
                spread_logits(0, i)

            second_tiles(1)
            with pe.Fori(2, NG - 1) as i:
                second_tiles(i)
            spread_logits(1, NG - 2)
            for k in range(KC):
                mm = pe.matmul(bank[6][0:NP, 0:GW], watt2[:, k, 0:1].to_broadcast([128, NP]), hT[:, k, N - GW:N],
                               start=(k == 0), stop=(k == KC - 1))
            mm.then_inc(row_full, 1)
            second_features(0, NG - 1)
            second_features(1, NG - 1)
            pe.wait_ge(row_out, NT - 1)
            pe.wait_ge(h2a_done, NT)
            pe.wait_ge(h2b_done, NT)

            def turn_5(i):
                pe.wait_ge(exp5, i + 1)
                for b in range(5):
                    if b >= 2:
                        pe.wait_ge(t5_evac, 5 * i + (b - 1))
                    elif i > 0:
                        pe.wait_ge(t5_evac, 5 * i)
                        if i > 1:
                            pe.wait_ge(y_evac, 3 * (i - 1))
                    for s in range(2):
                        for j in range(2):
                            mm = pe.transpose(bank[b % 2][0:NP, (2 * s + j) * NP:(2 * s + j + 1) * NP],
                                              L5[j][:, (2 * b + s) * NP:(2 * b + s + 1) * NP], ident[0:NP, 0:NP])
                    mm.then_inc(t5_full, 1)

            def aggregate_5(i, j):
                if j == 0:
                    pe.wait_ge(t5_evac, 5 * i + 5)
                freed(pe, x2_done[j], i)
                for b in range(2):
                    for s in range(NT):
                        mm = pe.matmul(bank[2 + 2 * j + b][0:NP, 0:HALF], PT5[:, s, j * NP:(j + 1) * NP],
                                       h2[:, s, b * HALF:(b + 1) * HALF], start=(s == 0), stop=(s == NT - 1))
                mm.then_inc(agg5, 1)

            def turn_y(i):
                pe.wait_ge(y_ready, 2 * i + 2)
                for c in range(3):
                    if c < 2:
                        if i < NG - 1:
                            pe.wait_ge(t5_evac, 5 * i + (9 + c))
                    else:
                        pe.wait_ge(y_evac, 3 * i + 1)
                    for kk in range(2):
                        for j in range(2):
                            k = 2 * c + kk
                            mm = pe.transpose(bank[(c + 1) % 2][:, (2 * kk + j) * NP:(2 * kk + j + 1) * NP],
                                              y5[j][:, k * 128:(k + 1) * 128], ident[0:NP, 0:NP])
                    mm.then_inc(y_full, 1)

            def ffn_up(i, atoms=range(0)):
                pe.wait_ge(y_evac, 3 * i + 3)
                freed(pe, out_done[1], i)
                for a in atoms:
                    pe.wait_ge(tokT_done, 1)
                    pe.wait_ge(atom_in_sem[a % 3], 16 * (a // 3 + 1))
                    w = atom_w[a % 3][:, :].rearrange("p (k n) -> p k n", k=KD)
                    for m in range(KF):
                        for k in range(KD):
                            c = HALF + (a * KF + m) * 8
                            mm = pe.matmul(bank[7][:, c:c + NCLS], w[:, k, m * 128:(m + 1) * 128],
                                           tokT[:, k, :], start=(k == 0), stop=(k == KD - 1))
                    mm.then_inc(atom_used, 1)
                for m in range(KF):
                    for k in range(KD):
                        mm = pe.matmul(bank[6 + m // 2][:, (m % 2) * GW:(m % 2 + 1) * GW],
                                       fc1_sb[:, k, m * 128:(m + 1) * 128],
                                       yT[:, k, :, :].rearrange("p j n -> p (j n)"),
                                       start=(k == 0), stop=(k == KD - 1))
                mm.then_inc(hid_full, 1)

            def ffn_down(i, j):
                if j == 0:
                    pe.wait_ge(gelu_done, i + 1)
                    if i < 2:
                        pe.wait_ge(hid_done, (3, NATOM)[i])
                elif i == NG - 1:
                    pe.wait_ge(x2_done[0], NG)
                else:
                    pe.wait_ge(out_done[0], i + 1)
                for b in range(2):
                    for m in range(KF):
                        mm = pe.matmul(bank[down_bank(i, j) + b][0:NP, 0:HALF], gT[:, m, j * NP:(j + 1) * NP],
                                       fc2_sb[:, m, b * HALF:(b + 1) * HALF], start=(m == 0), stop=(m == KF - 1))
                mm.then_inc(ffn_full, 1)

            def candidates(r, first):
                pe.wait_ge(pick_done, 12)
                pe.wait_ge(out_done[1], first)
                atoms = (range(3, 5), range(0, 3))[r]
                for a in atoms:
                    s = NATOM + a
                    pe.wait_ge(atom_in_sem[s % 3], 16 * (s // 3 + 1))
                    w = atom_w[s % 3][:, :].rearrange("p (m n) -> p m n", m=KF)
                    for b in range(2):
                        for m in range(KF):
                            mm = pe.matmul(bank[6 + b][0:NCLS, 0:HALF], pick[:, a, m, :],
                                           w[:, m, b * HALF:(b + 1) * HALF], start=(a == atoms[0] and m == 0),
                                           stop=(a == atoms[-1] and m == KF - 1))
                    mm.then_inc(atom_used, 1)

            turn_5(0)
            aggregate_5(0, 0)
            aggregate_5(0, 1)
            for i in range(1, NG):
                turn_5(i)
                turn_y(i - 1)
                if i == 1:
                    pe.wait_ge(ffn_in, 32)
                if i > 3:
                    pe.wait_ge(cand_read, i - 3)
                ffn_up(i - 1, atoms={1: range(0, 3), 2: range(3, NATOM)}.get(i, range(0)))
                aggregate_5(i, 0)
                ffn_down(i - 1, 0)
                aggregate_5(i, 1)
                ffn_down(i - 1, 1)
                if i >= 3:
                    candidates(4 - i, i)
            turn_y(NG - 1)
            pe.wait_ge(cand_read, 2)
            ffn_up(NG - 1)
            ffn_down(NG - 1, 0)
            ffn_down(NG - 1, 1)

        @block.vector
        def _(dve):
            dve.memset(attz[:, :, :], 0.0).then_inc(attz_set, 1)

            dve.wait_ge(edges_in, 48)
            dve.tensor_reduce(cmin[:, :], dsr[:, :], mybir.AxisListType.X, ALU.min).then_inc(span_step, 1)
            dve.tensor_reduce(cmax[:, :], dsr[:, :], mybir.AxisListType.X, ALU.max).then_inc(span_step, 1)
            dve.wait_ge(span_step, 2)
            dve.wait_ge(consts_made, 8)
            dve.tensor_scalar(a1[:, :], tlo[:, :], cmax[:, 0:1], None, ALU.is_le).then_inc(span_step, 1)
            dve.tensor_scalar(a2[:, :], tlo[:, :], float(NP - 1), cmin[:, 0:1], ALU.add, ALU.is_ge
                              ).then_inc(span_step, 1)
            dve.wait_ge(span_step, 4)
            dve.tensor_tensor(a3[:, :], a1[:, :], a2[:, :], ALU.mult).then_inc(span_step, 1)
            dve.wait_ge(span_step, 5)
            dve.tensor_scalar(vv[:, 0:NT], a3[:, :], cidx[:, 0:1], None, ALU.mult).then_inc(span_step, 1)
            dve.tensor_scalar(vv[:, NT:2 * NT], a3[:, :], cidx[:, 1:2], None, ALU.mult).then_inc(span_step, 1)
            dve.memset(srcf[:, NCH:NCH + 6], -1.0)
            dve.memset(dstf[:, NCH:NCH + 6], -1.0)
            dve.tensor_copy(srcf[:, 0:NCH], srci[:, :])
            dve.tensor_copy(dstf[:, 0:NCH], dsti[:, :]).then_inc(span_step, 1)
            for a in range(RING):
                dve.memset(ohd[a][:, :], 0.0).then_inc(oh_used[a], 1)
            dve.wait_ge(span_max, 1)
            dve.tensor_scalar(sp0[:, 0:NT], vr[0:1, 0:NT], -1.0, float(NS), ALU.mult, ALU.add).then_inc(span_step, 1)
            dve.wait_ge(span_step, 9)
            dve.tensor_scalar(sp0[:, 0:NT], sp0[:, 0:NT], float(NS - 1), None, ALU.min).then_inc(span_step, 1)
            dve.wait_ge(span_step, 10)
            dve.tensor_tensor(hi0[:, :], vr[0:1, NT:2 * NT], sp0[:, 0:NT], ALU.subtract).then_inc(span_step, 1)
            dve.wait_ge(span_step, 11)
            dve.tensor_scalar(hi0[:, :], hi0[:, :], 1.0, 0.5, ALU.max, ALU.mult).then_inc(span_step, 1)
            dve.wait_ge(span_step, 12)
            dve.tensor_scalar(hi0[:, :], hi0[:, :], 0.25, None, ALU.add).then_inc(span_step, 1)
            dve.wait_ge(span_step, 13)
            dve.tensor_scalar(hi0[:, :], hi0[:, :], 2.0 ** 23, None, ALU.add).then_inc(span_step, 1)
            dve.wait_ge(span_step, 14)
            dve.tensor_scalar(sp0[:, NT:2 * NT], hi0[:, :], -2.0 ** 23, 2.0, ALU.add, ALU.max).then_inc(span_step, 1)
            dve.memset(sp0[:, 2 * NT:2 * NT + 1], 0.0).then_inc(span_step, 1)
            for t in range(1, NT):
                dve.wait_ge(span_step, 15 + t)
                dve.tensor_tensor(sp0[:, 2 * NT + t:2 * NT + t + 1], sp0[:, 2 * NT + t - 1:2 * NT + t],
                                  sp0[:, NT + t - 1:NT + t], ALU.add).then_inc(span_step, 1)
            dve.wait_ge(span_step, 15 + NT)
            dve.tensor_copy(spans[:, :], sp0[:, :]).then_inc(spans_ready, 1)

            def one_hots(p, i):
                start = dve.value_load(spans[0:1, ds(2 * i + p, 1)], min_val=0, max_val=NS - 1)
                count = dve.value_load(spans[0:1, ds(2 * i + (NT + p), 1)], min_val=2, max_val=NQ)
                before = dve.value_load(spans[0:1, ds(2 * i + (2 * NT + p), 1)], min_val=0, max_val=NQ * NT)
                with dve.Fori(0, count) as c:
                    pair = (start + 2 * c).with_bounds(min_val=0, max_val=NS + 1)
                    for a in range(RING):
                        dve.wait_ge(oh_used[a], before + c + 1)
                        dve.tensor_scalar(ohs[a][:, :], iota16[:, :], srcf[:, ds(2 * pair + a, 1)], None,
                                          ALU.is_equal)
                        dve.tensor_scalar(ohd[a][:, :], iota16[:, ds((2 * i + p) * NP, NP)],
                                          dstf[:, ds(2 * pair + a, 1)], None, ALU.is_equal
                                          ).then_inc(oh_ready[a], 1)

            def mend(p, i):
                dve.wait_ge(ln_done, 2 * i + (p + 1))
                v = LC[:, ds(2 * i + p, 1), :].rearrange("p t n -> p (t n)")
                dve.scalar_tensor_tensor(v, v, 1e30, v, ALU.mult, ALU.min).then_inc(lc_done, 1)

            def statistics(p, i):
                t = 2 * i + p
                dve.wait_ge(x_in[p], 16 * (i + 1))
                for b in range(2):
                    s = dve.bn_stats(stats[p][:, b, :], xin[p][:, b * HALF:(b + 1) * HALF])
                s.then_inc(stat_step, 1)
                dve.wait_ge(stat_step, 3 * t + 1)
                alone(dve)
                dve.bn_aggr(mv[p][:, :], stats[p][:, :, :]).then_inc(stat_step, 1)
                dve.wait_ge(stat_step, 3 * t + 2)
                dve.tensor_scalar(var[p][:, :], mv[p][:, 1:2], LN_EPS, None, ALU.add).then_inc(stat_step, 1)

            def normalise(p, i):
                t = 2 * i + p
                dve.wait_ge(rstd_ready, t + 1)
                freed(dve, xt_full, t - 1)
                dve.tensor_scalar(xn[p][:, :], xin[p][:, :], mv[p][:, 0:1], rstd[p][:, 0:1],
                                  ALU.subtract, ALU.mult).then_inc(xn_ready, 1)

            def logits_out(p, i):
                t = 2 * i + p
                dve.wait_ge(logit_full, t + 1)
                dve.tensor_copy(tile_rows[p][:, :], bank[5][0:2 * H, 0:NP])
                dve.tensor_copy(rows1[:, 0, ds(t * NP, NP)], bank[5][0:H, 0:NP])
                dve.tensor_scalar(rows1[:, 1, ds(t * NP, NP)], bank[5][0:H, 0:NP], SLOPE, None, ALU.mult
                                  ).then_inc(logit_rows, 1)
                dve.tensor_tensor(xT_lo[p][:, :, :], xT[p][:, :, :], xT_hi[p][:, :, :].bitcast(F32), ALU.subtract
                                  ).then_inc(xT_lo_done, 1)

            def logit_columns_out(p, i):
                t = 2 * i + p
                dve.wait_ge(column_full, t + 1)
                dve.tensor_scalar(nad1[:, :, ds(t, 1)].rearrange("p h t -> p (h t)"),
                                  bank[5][0:NP, 128 + H:128 + 2 * H], SLOPE - 1.0, None, ALU.mult
                                  ).then_inc(logit_done, 1)

            dve.wait_ge(spans_ready, 1)
            for p in range(2):
                one_hots(p, 0)
            dve.wait_ge(attz_set, 1)
            dve.wait_ge(att_in, 16 * 4)
            flat = attz[:, :, :].rearrange("c h m -> c (h m)")
            for side in range(2):
                first = side * H
                dve.tensor_copy(flat[:, first:first + (2 * H + 1) * (H - 1) + 1:2 * H + 1], att1[:, side, :]
                                ).then_inc(attz_set, 1)
            statistics(0, 0)
            normalise(0, 0)
            for p in range(2):
                mend(p, 0)
            dve.wait_ge(wattp, 1)
            for b in range(2):
                r = dve.tensor_copy(wrow1[:, b * HALF:(b + 1) * HALF], bank[6 + b][0:2 * H, 0:HALF])
            r.then_inc(watt_done, 1)
            dve.wait_ge(wattp, 2)
            dve.tensor_copy(watt1[:, :, :], bank[5][:, 0:2 * H * KD].rearrange("p (k c) -> p k c", k=KD)
                            ).then_inc(watt_done, 1)

            def features(i):
                for p in range(2):
                    one_hots(p, i + 1)
                    statistics(1 - p, i + p)
                    normalise(1 - p, i + p)
                    mend(p, i + 1)
                    logits_out(p, i)
                    logit_columns_out(p, i)

            rounds(dve, NG - 1, features)
            statistics(1, NG - 1)
            normalise(1, NG - 1)
            dve.wait_ge(wattp, 3)
            for b in range(2):
                r = dve.tensor_copy(wrow2[:, b * 512:(b + 1) * 512], bank[b][0:2, :])
            r.then_inc(watt_done, 1)
            logits_out(0, NG - 1)
            logit_columns_out(0, NG - 1)
            dve.wait_ge(wattp, 4)
            both = bank[2][:, 0:2 * KC].rearrange("p (k c) -> p k c", k=KC)
            dve.tensor_copy(watt2[:, :, :], both).then_inc(watt_done, 1)
            dve.tensor_copy(w2_sb[:, :, D:D + 2], both).then_inc(watt_done, 1)
            logits_out(1, NG - 1)
            logit_columns_out(1, NG - 1)
            dve.wait_ge(lc_done, NT)
            dve.wait_ge(logit_done, NT)
            dve.wait_ge(rows_stored, 16)

            def logits(hh, k, first=False, last=False):
                if last:
                    return
                q, g, n, h = at(hh, k, 0)
                if g == 0:
                    dve.wait_ge(asb_in[q], 16 * (hh + 1))
                    dve.tensor_copy(nadh[q][:, :], nad1[:, ds(h, 1), :].rearrange("p h t -> p (h t)")
                                    ).then_inc(nadh_done, 1)
                    dve.wait_ge(nadh_done, h + 1)
                for j in range(2):
                    r, t = (2 * k + j) % 4, 2 * g + j
                    if not (first and k < 2):
                        dve.wait_ge(tb_full, NG * n + -NG)
                    dve.scalar_tensor_tensor(L[r][:, :], asb[q][:, 1, :], nadh[q][:, t:t + 1], asb[q][:, 0, :],
                                             ALU.add, ALU.max).then_inc(stt_done, 1)
                for j in range(2):
                    r, t = (2 * k + j) % 4, 2 * g + j
                    dve.wait_ge(stt_done, 2 * n + (j + 1))
                    alone(dve)
                    dve.tensor_tensor_reduce(out=L[r][:, :], in0=L[r][:, :], in1=LC[:, t, :], scale=1.0,
                                             scalar=-3e38, op0=ALU.add, op1=ALU.max,
                                             accum_out=mx[q][:, t:t + 1]).then_inc(max_done, 1)
                dve.wait_ge(max_done, 2 * n + 2)
                dve.tensor_scalar(nm[q][:, 2 * g:2 * g + 2], mx[q][:, 2 * g:2 * g + 2], FLOOR, -1.0,
                                  ALU.max, ALU.mult).then_inc(nm_ready, 1)

            def reciprocals(hh, k, first=False, last=False):
                lag = 1
                if (first and k < lag) or (last and k - lag >= 2 * NG):
                    return
                q, g, n, h = at(hh, k, lag)
                dve.wait_ge(exp_done, n + 1)
                dve.tensor_scalar(dn[q][:, 2 * g:2 * g + 2], den[q][:, 2 * g:2 * g + 2], EPS, None, ALU.add
                                  ).then_inc(dn_done, 1)
                dve.wait_ge(dn_done, n + 1)
                dve.reciprocal(rden[q][:, 2 * g:2 * g + 2], dn[q][:, 2 * g:2 * g + 2]).then_inc(rden_ready, 1)

            def multiply(hh, k, first=False, last=False):
                lag = 3
                if (first and k < lag) or (last and k - lag >= 2 * NG):
                    return
                q, g, n, h = at(hh, k, lag)
                dve.wait_ge(agg_done, n + 1)
                dve.wait_ge(rdb_ready, n + 1)
                if not (first and k - lag < 2):
                    dve.wait_ge(relu_done, n + -1)
                i = (k - lag) % 2
                dve.tensor_tensor(tmp[i][:, :], bank[2 + i][:, 0:GW], rdb[i][:, :], ALU.mult).then_inc(mul_done, 1)

            def step(hh, k, **at_end):
                logits(hh, k, **at_end)
                reciprocals(hh, k, **at_end)
                multiply(hh, k, **at_end)

            for k in range(2 * NG):
                step(0, k, first=True)
            with dve.Fori(1, H // 2) as hh:
                for k in range(2 * NG):
                    step(hh, k)
            def w2_lower(ks):
                for k in ks:
                    dve.wait_ge(w2_hi_done, k + 1)
                    dve.tensor_tensor(w2_lo[:, k, :], w2_sb[:, k, :], w2_hi[:, k, :].bitcast(F32), ALU.subtract
                                      ).then_inc(w2_lo_done, 1)

            for k in range(2 * NG, 2 * NG + 2):
                step(H // 2 - 1, k, last=True)
            w2_lower(range(0, KC // 2))
            step(H // 2 - 1, 2 * NG + 2, last=True)
            w2_lower(range(KC // 2, KC))

            dve.wait_ge(lc_stored, 16 * NT)

            def h2_out(p, i):
                t = 2 * i + p
                dve.wait_ge(h2_full, t + 1)
                last = bank[2 * p + 1]
                dve.tensor_copy(as2c[p][:, :], last[0:NP, HALF:HALF + 1])
                dve.tensor_scalar(nad2[:, ds(t, 1)], last[0:NP, HALF + 1:HALF + 2], SLOPE - 1.0, None, ALU.mult)
                dve.tensor_copy(h2[:, ds(t, 1), HALF:D].rearrange("p t n -> p (t n)"), last[0:NP, 0:HALF]
                                ).then_inc(h2b_done, 1)

            def row_of(source, t, start, width):
                dve.wait_ge(row_full, t + 1)
                dve.tensor_copy(asb2[:, 0, ds(start, width)], source[0:NP, 0:width])
                dve.tensor_scalar(asb2[:, 1, ds(start, width)], source[0:NP, 0:width], SLOPE, None, ALU.mult
                                  ).then_inc(row_out, 1)

            def tile_row(p, i):
                row_of(bank[4 + p], 2 * i + p, (2 * i + p) * NP, NP)

            def tile_lower(p, i):
                dve.wait_ge(tile_ready, 2 * i + (p + 1))
                dve.tensor_tensor(h1Tt_lo[p][:, :, :], hT[:, :, ds((2 * i + p) * NP, NP)],
                                  h1Tt_hi[p][:, :, :].bitcast(F32), ALU.subtract).then_inc(tile_lo_done, 1)

            tile_lower(0, 0)
            tile_lower(1, 0)
            h2_out(0, 0)
            tile_lower(0, 1)
            h2_out(1, 0)
            tile_lower(1, 1)
            tile_row(0, 0)
            with dve.Fori(1, NG - 1) as i:
                h2_out(0, i)
                tile_lower(0, i + 1)
                tile_row(1, i + -1)
                h2_out(1, i)
                tile_lower(1, i + 1)
                tile_row(0, i)
            tile_row(1, NG - 2)
            row_of(bank[6], NT - 2, N - GW, GW)

            def reciprocals_5(i):
                dve.wait_ge(exp5, i + 1)
                dve.tensor_scalar(dn5[:, :], den5[:, :], EPS, None, ALU.add).then_inc(dn5_done, 1)
                dve.wait_ge(dn5_done, i + 1)
                dve.reciprocal(rden5[:, :], dn5[:, :]).then_inc(rden5_done, 1)

            def logits_5(i, first=False):
                for j in range(2):
                    if not first:
                        dve.wait_ge(t5_full, 5 * i)
                        alone(dve)
                    dve.scalar_tensor_tensor(L5[j][:, :], asb2[:, 1, :], nad2[:, 2 * i + j:2 * i + j + 1],
                                             asb2[:, 0, :], ALU.add, ALU.max).then_inc(stt5, 1)
                for j in range(2):
                    dve.wait_ge(stt5, 2 * i + (j + 1))
                    dve.wait_ge(lct_in[j], 16 * (i + 1))
                    alone(dve)
                    dve.tensor_tensor_reduce(out=L5[j][:, :], in0=L5[j][:, :], in1=LCt[j][:, :], scale=1.0,
                                             scalar=-3e38, op0=ALU.add, op1=ALU.max,
                                             accum_out=mx5[:, j:j + 1]).then_inc(max5, 1)
                dve.wait_ge(max5, 2 * i + 2)
                dve.tensor_scalar(nm5[:, :], mx5[:, :], FLOOR, -1.0, ALU.max, ALU.mult).then_inc(nm5_ready, 1)

            def norm_5(i, j, first=False):
                n = 3 * (2 * i + j)
                dve.wait_ge(agg5, 2 * i + (j + 1))
                dve.wait_ge(xb_done[j], i + 1)
                dve.wait_ge(rden5_done, i + 1)
                if not first:
                    dve.wait_ge(x2f_done[j], i)
                for b in range(2):
                    c = slice(b * HALF, (b + 1) * HALF)
                    s = dve.scalar_tensor_tensor(x2[j][:, c], bank[2 + 2 * j + b][0:NP, 0:HALF], rden5[:, j:j + 1],
                                                 x5[j][:, c], ALU.mult, ALU.add)
                s.then_inc(x2_done[j], 1)
                dve.wait_ge(x2_done[j], i + 1)
                for b in range(2):
                    s = dve.bn_stats(stats5[j][:, b, :], x2[j][:, b * HALF:(b + 1) * HALF])
                s.then_inc(ln_step, 1)
                dve.wait_ge(ln_step, n + 1)
                alone(dve)
                dve.bn_aggr(mv5[j][:, :], stats5[j][:, :, :]).then_inc(ln_step, 1)
                dve.wait_ge(ln_step, n + 2)
                dve.tensor_scalar(var5[j][:, :], mv5[j][:, 1:2], LN_EPS, None, ALU.add).then_inc(ln_step, 1)
                dve.wait_ge(rstd5_ready, 2 * i + (j + 1))
                if not first:
                    dve.wait_ge(y_full, 3 * i)
                dve.tensor_scalar(y5[j][:, :], x2[j][:, :], mv5[j][:, 0:1], rstd5[j][:, 0:1],
                                  ALU.subtract, ALU.mult).then_inc(y_ready, 1)

            def out_5(i, j, first=False):
                dve.wait_ge(ffn_full, 2 * i + (j + 1))
                dve.wait_ge(x2f_done[j], i + 1)
                if not first:
                    dve.wait_ge(out_stored[j], 16 * i)
                for b in range(2):
                    c = slice(b * HALF, (b + 1) * HALF)
                    s = dve.tensor_tensor(ost[j][:, c], bank[down_bank(i, j) + b][0:NP, 0:HALF], x2f[j][:, c], ALU.add)
                s.then_inc(out_done[j], 1)

            steps = [0]

            def link(ins):
                steps[0] += 1
                ins.then_inc(gate_step, 1)
                dve.wait_ge(gate_step, steps[0])

            def save_tokens():
                dve.wait_ge(y_ready, 1)
                dve.tensor_copy(tok_y[:, :], y5[0][0:NCLS, :])
                dve.tensor_copy(tok_x[:, :], x2[0][0:NCLS, :]).then_inc(tok_saved, 1)

            def gate_logits():
                dve.wait_ge(cls_in, 16 * 15)
                dve.wait_ge(tok_saved, 1)
                y = tok_y[:, :]
                for in0, in1, to in ((y, y, sq[:, 0:1]), (gp[:, 0, :], gp[:, 0, :], sq[:, 1:2]),
                                     (gp[:, 1, :], gp[:, 1, :], sq[:, 2:3]),
                                     (y, gp[:, 0, :], dots[:, 0:1]), (y, gp[:, 1, :], dots[:, 1:2])):
                    link(dve.tensor_tensor_reduce(out=scr[:, :], in0=in0, in1=in1, scale=1.0, scalar=0.0,
                                                  op0=ALU.mult, op1=ALU.add, accum_out=to))
                dve.wait_ge(gate_root, 1)
                link(dve.tensor_scalar(nr[:, :], sr[:, :], NORM_EPS, None, ALU.max))
                link(dve.tensor_scalar(lg[0][:, :], nr[:, 1:3], nr[:, 0:1], None, ALU.mult))
                link(dve.reciprocal(lg[1][:, :], lg[0][:, :]))
                link(dve.tensor_tensor(lg[2][:, :], dots[:, :], lg[1][:, :], ALU.mult))
                link(dve.tensor_tensor(lg[0][:, :], lg[2][:, :], bal[:, :], ALU.add))
                link(dve.tensor_reduce(g1[0][:, :], lg[0][:, :], mybir.AxisListType.X, ALU.max))
                link(dve.tensor_scalar(lg[1][:, :], lg[0][:, :], g1[0][:, 0:1], None, ALU.subtract))

            def gate_weights():
                dve.wait_ge(gate_exp, 1)
                link(dve.tensor_reduce(g1[1][:, :], lg[2][:, :], mybir.AxisListType.X, ALU.add))
                link(dve.reciprocal(g1[2][:, :], g1[1][:, :]))
                link(dve.tensor_scalar(lg[3][:, :], lg[2][:, :], g1[2][:, 0:1], None, ALU.mult))
                link(dve.tensor_tensor(g1[3][:, :], lg[3][:, 1:2], lg[3][:, 0:1], ALU.is_gt))
                link(dve.tensor_scalar(g1[4][:, :], g1[3][:, :], -1.0, 1.0, ALU.mult, ALU.add))
                link(dve.tensor_tensor(g1[5][:, :], g1[3][:, :], lg[3][:, 1:2], ALU.mult))
                link(dve.tensor_tensor(g1[0][:, :], g1[4][:, :], lg[3][:, 0:1], ALU.mult))

            def pick_hidden():
                dve.wait_ge(pick_zero, 1)
                dve.wait_ge(hid_done, NATOM)
                for n, (l, r) in enumerate(ATOM_SRC):
                    for a_from, a_to in ((l, r), (r, l)):
                        dve.tensor_copy(pick[:, a_to, :, n], hid[:, a_from * KF:(a_from + 1) * KF, n]
                                        ).then_inc(pick_done, 1)

            def add_route(r, used, weight):
                dve.wait_ge(atom_used, used)
                for b in range(2):
                    c = slice(b * HALF, (b + 1) * HALF)
                    s = dve.tensor_tensor(cw[:, r, c], bank[6 + b][0:NCLS, 0:HALF], bo[:, r, c], ALU.add)
                s.then_inc(cand_read, 1)
                dve.wait_ge(cand_read, 2 - r)
                return dve.scalar_tensor_tensor(tok_x[:, :], cw[:, r, :], weight[:, 0:1], tok_x[:, :],
                                                ALU.mult, ALU.add)

            dve.wait_ge(row_out, NT - 1)
            logits_5(0, first=True)
            for p in range(2):
                h2_out(p, NG - 1)
            reciprocals_5(0)
            logits_5(1)
            for j in range(2):
                norm_5(0, j, first=True)
                if j == 0:
                    save_tokens()
            reciprocals_5(1)
            logits_5(2)
            gate_logits()
            for j in range(2):
                norm_5(1, j)
                out_5(0, j, first=True)
            reciprocals_5(2)
            logits_5(3)
            for j in range(2):
                norm_5(2, j)
                out_5(1, j)
            pick_hidden()
            gate_weights()
            reciprocals_5(3)
            logits_5(4)
            for j in range(2):
                norm_5(3, j)
                out_5(2, j)
            link(add_route(1, NATOM + 3, g1[5]))
            reciprocals_5(4)
            for j in range(2):
                norm_5(4, j)
                out_5(3, j)
            add_route(0, NATOM + 5, g1[0]).then_inc(cls_done, 1)
            for j in range(2):
                out_5(4, j)


def kernel(**inputs):
    import numpy as np
    import concourse.bacc as bacc
    from concourse.bass_utils import run_bass_kernel_spmd

    a = {k: np.asarray(v) for k, v in inputs.items()}
    W1, W2 = a["L0_gnn_W1"], a["L0_gnn_W2"]
    fed = {
        "x": a["x"],
        "src_cols": a["src"].reshape(NCH, CE).T,
        "dst_cols": a["dst"].reshape(NCH, CE).T,
        "dst_rows": a["dst"].reshape(NS, 2 * CE),
        "W1": W1,
        "W1T": W1.T,
        "as1T": a["L0_gnn_att_src1"].T,
        "ad1T": a["L0_gnn_att_dst1"].T,
        "b1c": a["L0_gnn_b1"].reshape(H, C).T,
        "W2": W2,
        "W2T": W2.T,
        "as2T": a["L0_gnn_att_src2"].reshape(KD, 128).T,
        "ad2T": a["L0_gnn_att_dst2"].reshape(KD, 128).T,
        "b2": a["L0_gnn_b2"].reshape(1, D),
        "fc1T": a["L0_ffn_fc1_w"].T,
        "fc1b": a["L0_ffn_fc1_b"].reshape(KF, 128).T,
        "fc2T": a["L0_ffn_fc2_w"].T,
        "fc2b": a["L0_ffn_fc2_b"].reshape(1, D),
        "gate_pair": a["L0_ffn_gate_pair"],
        "atom_inT": a["L0_ffn_atom_in_w"].transpose(0, 2, 1),
        "atom_inb": a["L0_ffn_atom_in_b"].reshape(NATOM * KF, 128).T,
        "atom_outT": a["L0_ffn_atom_out_w"].transpose(0, 2, 1),
        "atom_outb": a["L0_ffn_atom_out_b"],
        "balance": a["L0_ffn_balance_bias"],
    }
    nc = bacc.Bacc("TRN2", target_bir_lowering=False, num_devices=1)
    arrays, args = {}, []
    for name, value in fed.items():
        value = np.ascontiguousarray(value)
        arrays[f"in_{name}"] = value
        args.append(nc.dram_tensor(f"in_{name}", value.shape, mybir.dt.from_np(value.dtype), kind="ExternalInput").ap())
    out = nc.dram_tensor("out_0", (N, D), F32, kind="ExternalOutput").ap()
    gnn_ffn_kernel(nc, *args, out)
    r = run_bass_kernel_spmd(nc, [arrays], core_ids=[0])
    return r.results[0]["out_0"]
```
